# Optimizing a Trainium2 kernel written in Bass

```python
import numpy as np
import jax
import jax.numpy as jnp

def _softmax(x, axis=-1):
    return jax.nn.softmax(x, axis=axis)

def _gelu(x):
    return jax.nn.gelu(x, approximate=True)

def _silu(x):
    return jax.nn.silu(x)

def _sigmoid(x):
    return jax.nn.sigmoid(x)

def _layernorm(x, axis=-1, eps=1e-05):
    m = jnp.mean(x, axis=axis, keepdims=True)
    v = jnp.var(x, axis=axis, keepdims=True)
    return (x - m) / jnp.sqrt(v + eps)

def _scatter_add(tgt, idx, src, axis=0):
    return tgt.at[idx].add(src)

def _segment_sum(src, seg, n):
    return jax.ops.segment_sum(src, seg, n)
kernel_name = 'mk_adj_ffn_d2_adj_r2_697c00'

def setup_inputs(seed: int=0):
    np.random.seed(seed)
    _w = jnp.asarray

    def _rec_inputs():
        import jax
        import jax.numpy as jnp
        _gk = jax.random.key(seed)
        x = -0.0002928 + 1 * jax.random.normal(jax.random.fold_in(_gk, 1), (2048, 256), jnp.float32)
        _a = jax.random.bernoulli(jax.random.fold_in(_gk, 2), 0.00390625, (2048, 2048))
        _a = jnp.logical_or(_a, jnp.swapaxes(_a, -1, -2))
        _a = jnp.logical_or(_a, jnp.eye(2048, dtype=bool))
        _af = _a.astype(jnp.float32)
        _af = _af * jax.random.uniform(jax.random.fold_in(_gk, 3), (2048, 2048), jnp.float32, 0.05, 5.41998)
        adj = _af
        return (x, adj)
    x, adj = _rec_inputs()

    def _L0_gnn_setup():
        import jax, jax.numpy as jnp
        import numpy as np
        N = 4096
        D = 256
        EPS = 1e-12
        key = jax.random.key(seed)
        k1, k2 = jax.random.split(key)
        cur = jax.random.normal(k1, (N, D), dtype=jnp.float32)
        incidence_m = jax.random.normal(k2, (N, N), dtype=jnp.float32)
        return {'cur': cur, 'incidence_m': incidence_m}
    _L0_gnn_all = _L0_gnn_setup()
    _L0_gnn_in = {k: v for k, v in _L0_gnn_all.items() if k in ()}
    del _L0_gnn_all

    def _L0_ffn_setup():
        import jax, jax.numpy as jnp
        import numpy as np
        E = 64
        K = 2
        D = 256
        H = 128
        NSH = 2
        ROUTE_SCALE = 2.5
        CAP = 512
        STD = 0.02
        key = jax.random.key(seed)
        ks = jax.random.split(key, 8)
        x = jax.random.normal(ks[0], (4, 1024, D), dtype=jnp.float32)
        gate_w = jax.random.normal(ks[1], (E, D), dtype=jnp.float32) * STD
        w1 = jax.random.normal(ks[2], (E, D, H), dtype=jnp.float32) * STD
        w3 = jax.random.normal(ks[3], (E, D, H), dtype=jnp.float32) * STD
        w2 = jax.random.normal(ks[4], (E, H, D), dtype=jnp.float32) * STD
        sw1 = jax.random.normal(ks[5], (D, H * NSH), dtype=jnp.float32) * STD
        sw3 = jax.random.normal(ks[6], (D, H * NSH), dtype=jnp.float32) * STD
        sw2 = jax.random.normal(ks[7], (H * NSH, D), dtype=jnp.float32) * STD
        return {'x': x, 'gate_w': gate_w, 'w1': w1, 'w3': w3, 'w2': w2, 'sw1': sw1, 'sw3': sw3, 'sw2': sw2}
    _L0_ffn_all = _L0_ffn_setup()
    _L0_ffn_in = {k: v for k, v in _L0_ffn_all.items() if k in ('gate_w', 'w1', 'w3', 'w2', 'sw1', 'sw3', 'sw2')}
    del _L0_ffn_all

    def _L1_gnn_setup():
        import jax, jax.numpy as jnp
        import numpy as np
        N = 3072
        D_IN = 256
        D_OUT = 256
        DENSITY = 0.005
        key = jax.random.key(seed)
        ks = jax.random.split(key, 12)
        x = jax.random.normal(ks[0], (N, D_IN), dtype=jnp.float32)
        adj_a = (jax.random.uniform(ks[1], (N, N)) < DENSITY).astype(jnp.float32)
        adj_b = (jax.random.uniform(ks[2], (N, N)) < DENSITY).astype(jnp.float32)
        W_sa = jax.random.normal(ks[3], (D_IN, D_OUT), dtype=jnp.float32) * (1.414 / np.sqrt(D_IN + D_OUT))
        a_sa = jax.random.normal(ks[4], (1, 2 * D_OUT), dtype=jnp.float32) * (1.414 / np.sqrt(1 + 2 * D_OUT))
        stdv = 1.0 / np.sqrt(D_OUT)
        W_gcnb = jax.random.uniform(ks[5], (D_IN, D_OUT), minval=-stdv, maxval=stdv, dtype=jnp.float32)
        b_gcnb = jax.random.uniform(ks[6], (D_OUT,), minval=-stdv, maxval=stdv, dtype=jnp.float32)
        s = 1.0 / np.sqrt(2 * D_IN)
        Wa = jax.random.uniform(ks[7], (1, 2 * D_IN), minval=-s, maxval=s, dtype=jnp.float32)
        ba = jax.random.uniform(ks[8], (1,), minval=-s, maxval=s, dtype=jnp.float32)
        Wb = jax.random.uniform(ks[9], (1, 2 * D_IN), minval=-s, maxval=s, dtype=jnp.float32)
        bb = jax.random.uniform(ks[10], (1,), minval=-s, maxval=s, dtype=jnp.float32)
        return {'x': x, 'adj_a': adj_a, 'adj_b': adj_b, 'W_sa': W_sa, 'a_sa': a_sa, 'W_gcnb': W_gcnb, 'b_gcnb': b_gcnb, 'Wa': Wa, 'ba': ba, 'Wb': Wb, 'bb': bb}
    _L1_gnn_all = _L1_gnn_setup()
    _L1_gnn_in = {k: v for k, v in _L1_gnn_all.items() if k in ('W_sa', 'a_sa', 'W_gcnb', 'b_gcnb', 'Wa', 'ba', 'Wb', 'bb')}
    del _L1_gnn_all

    def _L1_ffn_setup():
        import jax, jax.numpy as jnp
        import numpy as np
        EPS = 1e-05
        TOP_K = 2

        def _moe_forward(x, Wg, W1, b1, W2, b2, gamma, beta):
            B, S, D = x.shape
            xf = x.reshape(-1, D)
            logits = xf @ Wg
            topv, topi = jax.lax.top_k(logits, TOP_K)
            gate_w = jax.nn.softmax(topv, axis=-1)
            h = jax.nn.relu(jnp.einsum('td,edh->teh', xf, W1) + b1[None])
            y = jnp.einsum('teh,ehd->ted', h, W2) + b2[None]
            mu = jnp.mean(y, axis=-1, keepdims=True)
            var = jnp.mean((y - mu) ** 2, axis=-1, keepdims=True)
            y = (y - mu) / jnp.sqrt(var + EPS) * gamma[None] + beta[None]
            y_sel = jnp.take_along_axis(y, topi[:, :, None], axis=1)
            out = jnp.sum(gate_w[:, :, None] * y_sel, axis=1)
            return out.reshape(B, S, D)
        key = jax.random.key(seed)
        ks = jax.random.split(key, 8)
        B, S, D, H, E = (4, 1024, 256, 256, 8)
        sd = lambda fan_in: 1.0 / np.sqrt(fan_in)
        x = jax.random.normal(ks[0], (B, S, D), dtype=jnp.float32)
        Wg = jax.random.uniform(ks[1], (D, E), jnp.float32, -sd(D), sd(D))
        W1 = jax.random.uniform(ks[2], (E, D, H), jnp.float32, -sd(D), sd(D))
        b1 = jax.random.uniform(ks[3], (E, H), jnp.float32, -sd(D), sd(D))
        W2 = jax.random.uniform(ks[4], (E, H, D), jnp.float32, -sd(H), sd(H))
        b2 = jax.random.uniform(ks[5], (E, D), jnp.float32, -sd(H), sd(H))
        gamma = jnp.ones((E, D), jnp.float32)
        beta = jnp.zeros((E, D), jnp.float32)
        return {'x': x, 'Wg': Wg, 'W1': W1, 'b1': b1, 'W2': W2, 'b2': b2, 'gamma': gamma, 'beta': beta}
    _L1_ffn_all = _L1_ffn_setup()
    _L1_ffn_in = {k: v for k, v in _L1_ffn_all.items() if k in ('Wg', 'W1', 'b1', 'W2', 'b2', 'gamma', 'beta')}
    del _L1_ffn_all
    return {'x': x, 'adj': adj, 'L0_ffn_gate_w': _L0_ffn_in['gate_w'], 'L0_ffn_w1': _L0_ffn_in['w1'], 'L0_ffn_w3': _L0_ffn_in['w3'], 'L0_ffn_w2': _L0_ffn_in['w2'], 'L0_ffn_sw1': _L0_ffn_in['sw1'], 'L0_ffn_sw3': _L0_ffn_in['sw3'], 'L0_ffn_sw2': _L0_ffn_in['sw2'], 'L1_gnn_W_sa': _L1_gnn_in['W_sa'], 'L1_gnn_a_sa': _L1_gnn_in['a_sa'], 'L1_gnn_W_gcnb': _L1_gnn_in['W_gcnb'], 'L1_gnn_b_gcnb': _L1_gnn_in['b_gcnb'], 'L1_gnn_Wa': _L1_gnn_in['Wa'], 'L1_gnn_ba': _L1_gnn_in['ba'], 'L1_gnn_Wb': _L1_gnn_in['Wb'], 'L1_gnn_bb': _L1_gnn_in['bb'], 'L1_ffn_Wg': _L1_ffn_in['Wg'], 'L1_ffn_W1': _L1_ffn_in['W1'], 'L1_ffn_b1': _L1_ffn_in['b1'], 'L1_ffn_W2': _L1_ffn_in['W2'], 'L1_ffn_b2': _L1_ffn_in['b2'], 'L1_ffn_gamma': _L1_ffn_in['gamma'], 'L1_ffn_beta': _L1_ffn_in['beta']}

def reference(x, adj, L0_ffn_gate_w, L0_ffn_w1, L0_ffn_w3, L0_ffn_w2, L0_ffn_sw1, L0_ffn_sw3, L0_ffn_sw2, L1_gnn_W_sa, L1_gnn_a_sa, L1_gnn_W_gcnb, L1_gnn_b_gcnb, L1_gnn_Wa, L1_gnn_ba, L1_gnn_Wb, L1_gnn_bb, L1_ffn_Wg, L1_ffn_W1, L1_ffn_b1, L1_ffn_W2, L1_ffn_b2, L1_ffn_gamma, L1_ffn_beta):
    import jax
    import jax.numpy as jnp

    def _L0_gnn_ref(cur, incidence_m):
        import jax, jax.numpy as jnp
        import numpy as np
        N = 4096
        D = 256
        EPS = 1e-12
        mask = incidence_m > 0
        head = jax.lax.stop_gradient(mask.astype(incidence_m.dtype))
        head = head / jnp.maximum(jnp.sqrt(jnp.sum(head * head, axis=-1, keepdims=True)), EPS)
        inc = incidence_m + head
        edge_fea = inc @ cur
        edge_degree = jnp.sum(inc, axis=-1, keepdims=True)
        return edge_fea / edge_degree

    def _L0_ffn_ref(x, gate_w, w1, w3, w2, sw1, sw3, sw2):
        import jax, jax.numpy as jnp
        import numpy as np
        E = 64
        K = 2
        D = 256
        H = 128
        NSH = 2
        ROUTE_SCALE = 2.5
        CAP = 512
        STD = 0.02
        bs, slen, d = x.shape
        xf = x.reshape(-1, d)
        logits = xf @ gate_w.T
        scores = jax.nn.sigmoid(logits.astype(jnp.float32))
        top_scores, top_idx = jax.lax.top_k(scores, K)
        top_scores = top_scores / (top_scores.sum(-1, keepdims=True) + 1e-20)
        top_scores = top_scores * ROUTE_SCALE
        flat_e = top_idx.reshape(-1)
        x_pairs = jnp.repeat(xf, K, axis=0)
        oh = jax.nn.one_hot(flat_e, E, dtype=jnp.int32)
        pos = jnp.take_along_axis(jnp.cumsum(oh, axis=0), flat_e[:, None], axis=1)[:, 0] - 1
        buf = jnp.zeros((E, CAP, d), dtype=xf.dtype).at[flat_e, pos].set(x_pairs, mode='drop')
        h = jax.nn.silu(jnp.einsum('ecd,edh->ech', buf, w1)) * jnp.einsum('ecd,edh->ech', buf, w3)
        y = jnp.einsum('ech,ehd->ecd', h, w2)
        valid = (pos < CAP)[:, None]
        y_pairs = jnp.where(valid, y[flat_e, jnp.minimum(pos, CAP - 1)], 0.0)
        routed = (y_pairs.reshape(-1, K, d) * top_scores[..., None].astype(xf.dtype)).sum(axis=1)
        shared = jax.nn.silu(xf @ sw1) * (xf @ sw3) @ sw2
        return (shared + routed).reshape(bs, slen, d)

    def _L1_gnn_ref(x, adj_a, adj_b, W_sa, a_sa, W_gcnb, b_gcnb, Wa, ba, Wb, bb):
        import jax, jax.numpy as jnp
        import numpy as np
        N = 3072
        D_IN = 256
        D_OUT = 256
        DENSITY = 0.005
        type_sum_a = adj_a @ x
        type_sum_b = adj_b @ x
        attn_a = jax.nn.sigmoid(jnp.concatenate([type_sum_a, x], axis=1) @ Wa.T + ba)
        attn_b = jax.nn.sigmoid(jnp.concatenate([type_sum_b, x], axis=1) @ Wb.T + bb)
        h = x @ W_sa
        Hd = h.shape[1]
        s_left = h @ a_sa[0, :Hd]
        s_right = h @ a_sa[0, Hd:]
        scores = s_left[:, None] + s_right[None, :]
        e = jnp.where(adj_a != 0, jnp.exp(-jax.nn.leaky_relu(scores, 0.01)), 0.0)
        attn = e / (jnp.sum(e, axis=1, keepdims=True) + 1e-05)
        x_a = attn @ h
        x_b = adj_b @ (x @ W_gcnb) + b_gcnb
        return jax.nn.sigmoid(attn_a * x_a + attn_b * x_b)

    def _L1_ffn_ref(x, Wg, W1, b1, W2, b2, gamma, beta):
        import jax, jax.numpy as jnp
        import numpy as np
        EPS = 1e-05
        TOP_K = 2

        def _moe_forward(x, Wg, W1, b1, W2, b2, gamma, beta):
            B, S, D = x.shape
            xf = x.reshape(-1, D)
            logits = xf @ Wg
            topv, topi = jax.lax.top_k(logits, TOP_K)
            gate_w = jax.nn.softmax(topv, axis=-1)
            h = jax.nn.relu(jnp.einsum('td,edh->teh', xf, W1) + b1[None])
            y = jnp.einsum('teh,ehd->ted', h, W2) + b2[None]
            mu = jnp.mean(y, axis=-1, keepdims=True)
            var = jnp.mean((y - mu) ** 2, axis=-1, keepdims=True)
            y = (y - mu) / jnp.sqrt(var + EPS) * gamma[None] + beta[None]
            y_sel = jnp.take_along_axis(y, topi[:, :, None], axis=1)
            out = jnp.sum(gate_w[:, :, None] * y_sel, axis=1)
            return out.reshape(B, S, D)
        return _moe_forward(x, Wg, W1, b1, W2, b2, gamma, beta)
    x = x + _L0_gnn_ref(_layernorm(x, axis=-1), adj)
    x = x + _L0_ffn_ref(_layernorm(x, axis=-1)[None], L0_ffn_gate_w, L0_ffn_w1, L0_ffn_w3, L0_ffn_w2, L0_ffn_sw1, L0_ffn_sw3, L0_ffn_sw2)[0]
    x = x + _L1_gnn_ref(_layernorm(x, axis=-1), adj, adj, L1_gnn_W_sa, L1_gnn_a_sa, L1_gnn_W_gcnb, L1_gnn_b_gcnb, L1_gnn_Wa, L1_gnn_ba, L1_gnn_Wb, L1_gnn_bb)
    x = x + _L1_ffn_ref(_layernorm(x, axis=-1)[None], L1_ffn_Wg, L1_ffn_W1, L1_ffn_b1, L1_ffn_W2, L1_ffn_b2, L1_ffn_gamma, L1_ffn_beta)[0]
    return x

_drawn_inputs = setup_inputs


def setup_inputs(seed=0):
    import zlib

    import numpy as np

    out = dict(_drawn_inputs(seed))
    spreads = {'L1_ffn_gamma': (1.0, 0.2), 'L1_ffn_beta': (0.0, 0.1)}
    factors = {'L1_gnn_b_gcnb': 3.68}
    for name, (base, spread) in spreads.items():
        noise = np.random.default_rng([zlib.crc32(name.encode()), seed]).standard_normal(out[name].shape)
        drawn = base * np.exp(spread * noise) if base else spread * noise
        out[name] = jnp.asarray(drawn.astype(out[name].dtype))
    for name, factor in factors.items():
        out[name] = (out[name] * factor).astype(out[name].dtype)
    return out
```

```python
from contextlib import ExitStack

import concourse.bass as bass
from concourse import mybir

P = 128
N = 2048
D = 256
NT = N // P
DC = D // P
E0, H0, CAP = 64, 128, 512
E1, H1 = 8, 256
TOPK = 2
ROUTE_SCALE = 2.5
EPS = 1e-5
PAIRS = N * TOPK
U = 4
T0 = -(-(PAIRS // P + E0 - 1) // U) * U
T1 = -(-(PAIRS // P + E1 - 1) // U) * U
DROPPED = float(2 ** 22)
DA = D + 2

F32, BF16, I32, U32 = mybir.dt.float32, mybir.dt.bfloat16, mybir.dt.int32, mybir.dt.uint32
ALU, ACT = mybir.AluOpType, mybir.ActivationFunctionType
X = mybir.AxisListType.X


class Chain:

    def __init__(self, eng, sem):
        self.eng, self.sem, self.base, self.n, self.per = eng, sem, 0, 0, None

    def link(self, ins):
        self.n += 1
        ins.then_inc(self.sem, 1)
        self.eng.wait_ge(self.sem, self.base + self.n)

    def enter(self, turn, per):
        self.start, self.per = self.base + self.n, per
        self.base, self.n = self.start + (turn - 1) * per, 0

    def leave(self, turns):
        assert self.n == self.per, (self.n, self.per)
        self.base, self.n, self.per = self.start + (turns - 1) * self.per, 0, None


def rolled(eng, turns, body, chain=None, per=0):
    body(0)
    with eng.Fori(1, turns) as i:
        if chain:
            chain.enter(i, per)
        body(i)
        if chain:
            chain.leave(turns)


def wait(eng, sem, value):
    if not isinstance(value, int) or value > 0:
        eng.wait_ge(sem, value)


def build(nc, x, adjb, gate, sw13, sw2, moe0, wgnn, wsaT, acol, wab, bab, bgcn, wg1, w1, w2, b1, b2, gamma, beta, out, stop=9):
    ctx = ExitStack()
    with ctx:
        def sb(name, shape, dt=F32):
            return ctx.enter_context(nc.sbuf_tensor(name, shape, dt))

        def sem(name):
            return ctx.enter_context(nc.semaphore(name))

        def dram(name, shape, dt=F32):
            return nc.dram_tensor(name, shape, dt, kind="Internal").ap()

        xn_dram = [dram("xn0_dram", (N, D)), dram("xn1_dram", (N, D))]
        TT = [T0, T1]
        table = [dram("table0", (P * T0, 1), I32), dram("table1", (P * T1, 1), I32)]
        y_dram = [dram("y0_dram", (T0 * P, D)), dram("y1_dram", (T1 * P, D))]

        xs = sb("xs", [P, NT, D])
        rowsP = sb("rowsP", [P, NT, DA])
        rowsQ = sb("rowsQ", [P, NT, DA])
        xT = sb("xT", [P, DC, N])
        adj_buf = sb("adj_buf", [P, 2, N])
        inc_buf = sb("inc_buf", [P, 2, N])
        mask = sb("mask", [P, 2, N], BF16)
        negs = sb("negs", [P, N])
        slbc = sb("slbc", [P, N])
        w1_sb = sb("w1_sb", [P, E1, DC * H1])
        w2_sb = sb("w2_sb", [P, E1, DC * D])
        wm = sb("wm", [P, U, 3 * D])
        xg = sb("xg", [P, U, D])
        y_sb = sb("y_sb", [P, U, D])
        xn_t = sb("xn_t", [P, 2, D])
        xT_t = sb("xT_t", [P, 2, DC, P])
        g_t = sb("g_t", [P, 2, DC, P])
        th = sb("th", [P, 2, D])
        av = sb("av", [P, 2, D])
        w1_t = wm[:, :, :].rearrange("p u n -> p (u n)")[:, 0:2 * DC * H1].rearrange("p (a n) -> p a n", a=2)
        gate_sb = sb("gate_sb", [P, DC, E0])
        sw13_sb = sb("sw13_sb", [P, DC, 2 * D])
        sw2_sb = sb("sw2_sb", [P, DC, D])
        wc_sb = sb("wc_sb", [P, DC, 2 * DA])
        wv_sb = sb("wv_sb", [P, DC, 2])
        wsaT_sb = sb("wsaT_sb", [P, DC, D])
        acol_sb = sb("acol_sb", [P, DC, 2])
        wab_sb = sb("wab_sb", [P, DC, 4])
        slw = sb("slw", [P, DC, P])
        bab_sb = sb("bab_sb", [P, 2])
        bgcn_sb = sb("bgcn_sb", [P, D])
        wg1_sb = sb("wg1_sb", [P, DC, E1])
        b1_sb = sb("b1_sb", [P, E1, DC])
        b2_sb = negs[0:1, :].rearrange("p (e d) -> p e d", e=E1)
        gam_bc = inc_buf[:, 0, :].rearrange("p (e d) -> p e d", e=E1)
        bet_bc = inc_buf[:, 1, :].rearrange("p (e d) -> p e d", e=E1)
        sg = mask[:, :, :].rearrange("p a n -> p (a n)").bitcast(F32).rearrange("p (h n) -> p h n", h=4)[:, 0:2, :]
        sth = negs[:, 0:1024].rearrange("p (h n) -> p h n", h=2)
        sav = negs[:, 1024:2048].rearrange("p (h n) -> p h n", h=2)
        ident = sb("ident", [P, P])
        ones_f = sb("ones_f", [1, P])
        ones_b = sb("ones_b", [P, P], BF16)
        tri_b = sb("tri_b", [P, P], BF16)
        iota_e = sb("iota_e", [P, E0])
        tok = sb("tok", [P, NT], I32)
        ones_e = sb("ones_e", [P, E0])
        tile_no = sb("tile_no", [P, 1])
        eps_sb = sb("eps_sb", [P, 1])
        st6 = sb("st6", [P, NT, 6])
        st6l = sb("st6l", [P, 2, 6])
        mvl = sb("mvl", [P, 2, 2])
        mv = sb("mv", [P, NT, 2])
        rstd = sb("rstd", [P, NT])
        nrm = sb("nrm", [P, 2, P])
        rden = sb("rden", [P, 2])
        srn = sb("srn", [P, NT])
        vab = sb("vab", [P, NT, 2])
        att = sb("att", [P, 2, 4])
        spare = rowsQ[:, :, :].rearrange("p t d -> p (t d)")
        lg, sel, rt1 = (spare[:, k * NT * E0:(k + 1) * NT * E0].rearrange("p (t e) -> p t e", e=E0) for k in range(3))
        mx8 = sb("mx8", [P, NT, 8])
        ix8 = sb("ix8", [P, NT, 8], U32)
        ixf = sb("ixf", [P, NT, TOPK])
        onehot = slbc[:, :].rearrange("p (k t e) -> p k t e", k=TOPK, e=E0)
        spare_b = spare[:, 3 * NT * E0:NT * DA].bitcast(BF16)
        cnt = spare_b[:, 0:NT * E0].rearrange("p (t e) -> p t e", e=E0)
        pre = spare_b[:, NT * E0:(2 * NT + 1) * E0].rearrange("p (t e) -> p t e", e=E0)
        tot = sb("tot", [P, 4, E0])
        toti = sb("toti", [P, E0], I32)
        slot = sb("slot", [P, TOPK, NT])
        slot_i = sb("slot_i", [P, TOPK, NT], I32)
        sp_i = sb("sp_i", [P, TOPK, NT], I32)
        sp_f = sb("sp_f", [P, TOPK, NT])
        sq_f = sb("sq_f", [P, TOPK, NT])
        addr = sb("addr", [P, TOPK, NT], I32)
        back = sb("back", [P, TOPK, NT], I32)
        wts = sb("wts", [P, TOPK, NT])
        ws = sb("ws", [P, 4, NT])
        et_f = sb("et_f", [P, 1])
        et_i = sb("et_i", [P, 1], I32)
        et_junk = sb("et_junk", [P, E0])
        et_row = [sb("et_row0", [1, T0], I32), sb("et_row1", [1, T1], I32)]
        tab = [sb("tab0", [P, T0], I32), sb("tab1", [P, T1], I32)]
        idx_t = sb("idx_t", [P, U, 1], I32)
        zero_i = sb("zero_i", [P, T0], I32)

        bank = [ctx.enter_context(nc.psum_tensor(f"bank{i}", [P, 512], F32)) for i in range(8)]

        names = """x_in const_in zero_in consts mask_ready count_done nrm_ready head_ready inc_ready adj_free prod_done x1_done
            dve act_ch pool_ch stats_ready rstd_ready ln_ready tr_done xts_ready xT_ready proj_done gnn_in
            lg_ready cnt_ready pos_done rt_ready addr_ready scat tabled et_in sh_h sh_t sh_g sh_y sh_x route_end
            w0_ready slw_ready slbc_done slbc_ready e_neg e_exp e_ready pa_done pe_done at_z at_t o_ready o_t x3_done
            out_done gb_in w12_in pool_passed waits_passed wcol_ready sc_ready proj_used w_in""".split()
        s = {n: sem(n) for n in names}
        adj_in = [sem(f"adj_in{i}") for i in range(2)]
        xn_out = [sem(f"xn_out{i}") for i in range(2)]
        m = [{n: sem(f"{n}_{l}") for n in "idx_ready tr_done x_ready h_done th_ready g_ready y_done y_ready wt_ready var_ready sd_ready".split()}
             for l in range(2)]
        xg_in = [sem(f"xg_in{i}") for i in range(U)]
        wm_in = [sem(f"wm_in{i}") for i in range(U)]
        y_out = [sem(f"y_out{i}") for i in range(U)]
        back_in = [sem(f"back_in{i}") for i in range(U)]
        back_used = sem("back_used")

        block = ctx.enter_context(nc.Block())
        tiled = [a.rearrange("(t p) d -> t p d", p=P) for a in xn_dram]
        y_tiled = [a.rearrange("(t p) d -> t p d", p=P) for a in y_dram]
        CONSTS = 12

        def finish_early(sp):
            sp.wait_ge(s["w12_in"], 32)
            sp.wait_ge(s["route_end"], stop)
            sp.dma_start(out.rearrange("(t p) d -> p t d", p=P), xs[:, :, :]).then_inc(s["out_done"], 16)
            sp.wait_ge(s["out_done"], 16)

        @block.sync
        def _(sp):
            sp.dma_start(xs[:, :, :], x.rearrange("(t p) d -> p t d", p=P)).then_inc(s["x_in"], 16)

            def load_adj(t, half):
                sp.dma_start(adj_buf[:, half, :], adjb[bass.ds(t, 1), :, :].rearrange("a p n -> (a p) n")).then_inc(adj_in[half], 16)

            for half in range(2):
                load_adj(half, half)
            with sp.Fori(0, NT // 2 - 1) as i:
                for half in range(2):
                    sp.wait_ge(s["inc_ready"], 2 * i + half + 1)
                    load_adj(2 * i + half + 2, half)
            sp.wait_ge(s["zero_in"], 1)
            for l in range(2):
                sp.dma_start(table[l].rearrange("(p t) a -> p (t a)", p=P), zero_i[:, 0:TT[l]]).then_inc(s["w_in"], 16)

            def store_rows(layer):
                with sp.Fori(0, NT // 2) as i:
                    for half in range(2):
                        sp.wait_ge(s["ln_ready"], 2 * NT * layer + 2 * i + half + 1)
                        sp.dma_start(tiled[layer][bass.ds(2 * i + half, 1), :, :].rearrange("a p n -> (a p) n"), xn_t[:, half, :]).then_inc(xn_out[half], 16)

            def routed(layer):
                sp.wait_ge(s["rt_ready"], layer + 1)
                sp.dma_start(et_row[layer][0:1, :], et_i[0:TT[layer], 0:1]).then_inc(s["et_in"], 16)
                sp.wait_ge(s["scat"], 16 * TOPK * NT * (layer + 1))
                sp.dma_start(tab[layer][:, :], table[layer].rearrange("(p t) a -> p (t a)", p=P)).then_inc(s["tabled"], 16)

            store_rows(0)
            if stop < 2:
                return finish_early(sp)
            routed(0)
            sp.wait_ge(s["et_in"], 16)

            def load_w(t, u):
                e = sp.value_load(et_row[0][0:1, bass.ds(t, 1)], min_val=0, max_val=E0 - 1)
                sp.dma_start(wm[:, u, :], moe0[bass.ds(e, 1), :, :].rearrange("a p n -> (a p) n")).then_inc(wm_in[u], 16)

            def store_y(layer, t, u):
                sp.wait_ge(m[layer]["y_ready"], t + 1)
                sp.dma_start(y_tiled[layer][bass.ds(t, 1), :, :].rearrange("a p n -> (a p) n"), y_sb[:, u, :]).then_inc(y_out[u], 16)

            for u in range(U):
                load_w(u, u)
            with sp.Fori(0, T0 // U - 1) as i:
                for u in range(U):
                    sp.wait_ge(m[0]["y_done"], U * i + u + 1)
                    load_w(U * i + u + U, u)
                    store_y(0, U * i + u, u)
            for u in range(U):
                store_y(0, T0 - U + u, u)
            sp.wait_ge(s["inc_ready"], NT)
            for half in range(2):
                load_adj(half, half)
            if stop < 3:
                return finish_early(sp)
            with sp.Fori(0, NT // 2 - 1) as i:
                for half in range(2):
                    sp.wait_ge(s["e_ready"], 2 * i + half + 1)
                    sp.wait_ge(s["pa_done"], 2 * i + half + 1)
                    load_adj(2 * i + half + 2, half)
            sp.wait_ge(s["pe_done"], NT)
            sp.dma_start(gam_bc, gamma.rearrange("e d -> (e d)").partition_broadcast(P).rearrange("p (e d) -> p e d", e=E1)).then_inc(s["gb_in"], 16)
            sp.dma_start(bet_bc, beta.rearrange("e d -> (e d)").partition_broadcast(P).rearrange("p (e d) -> p e d", e=E1)).then_inc(s["gb_in"], 16)
            sp.dma_start(b2_sb, b2.rearrange("(a e) d -> a e d", a=1)).then_inc(s["gb_in"], 16)
            if stop < 4:
                return finish_early(sp)
            store_rows(1)
            routed(1)
            with sp.Fori(0, T1 // U) as i:
                for u in range(U):
                    store_y(1, U * i + u, u)
            with sp.Fori(0, NT) as i:
                sp.wait_ge(s["x3_done"], NT + i + 1)
                sp.dma_start(out.rearrange("(t p) d -> t p d", p=P)[bass.ds(i, 1), :, :].rearrange("a p n -> (a p) n"),
                             xs[:, bass.ds(i, 1), :].rearrange("p a d -> p (a d)")).then_inc(s["out_done"], 16)
            sp.wait_ge(s["out_done"], 16 * NT)

        @block.gpsimd
        def _(pool):
            own = Chain(pool, s["pool_ch"])
            own.link(pool.memset(ident[:, :], 0.0))
            own.link(pool.memset(tri_b[:, :], 1.0))
            own.link(pool.affine_select(out=ident[:, :], in_=ident[:, :], compare_op=ALU.not_equal, fill=1.0, base=0,
                                        pattern=[[-1, P]], channel_multiplier=1))
            own.link(pool.affine_select(out=tri_b[:, :], in_=tri_b[:, :], compare_op=ALU.is_gt, fill=0.0, base=0,
                                        pattern=[[1, P]], channel_multiplier=-1))
            own.link(pool.memset(ones_b[:, :], 1.0))
            own.link(pool.memset(ones_e[:, :], 1.0))
            own.link(pool.memset(ones_f[:, :], 1.0))
            own.link(pool.iota(iota_e[:, :], pattern=[[1, E0]], base=0, channel_multiplier=0, allow_small_or_imprecise_dtypes=True))
            own.link(pool.iota(tile_no[:, :], pattern=[[0, 1]], base=0, channel_multiplier=1, allow_small_or_imprecise_dtypes=True))
            own.link(pool.iota(tok[:, :], pattern=[[P, NT]], base=0, channel_multiplier=1))
            own.link(pool.memset(eps_sb[:, :], EPS))
            pool.memset(zero_i[:, :], 0).then_inc(s["zero_in"], 1)
            pool.wait_ge(s["zero_in"], 1)
            pool.sem_inc(s["consts"], 1)

            def add_adj(t, half):
                pool.wait_ge(s["head_ready"], t + 1)
                pool.tensor_tensor(inc_buf[:, half, :], inc_buf[:, half, :], adj_buf[:, half, :], ALU.add).then_inc(s["inc_ready"], 1)

            with pool.Fori(0, NT // 2) as i:
                for half in range(2):
                    add_adj(2 * i + half, half)
            if stop < 2:
                return

            def scatter_tokens(layer):
                pool.wait_ge(s["w_in"], 32)
                pool.wait_ge(s["addr_ready"], layer + 1)
                for t in range(NT):
                    for k in range(TOPK):
                        pool.indirect_dma_start(out=table[layer], out_offset=bass.IndirectOffsetOnAxis(ap=addr[:, k, t:t + 1], axis=0),
                                                in_=tok[:, t:t + 1], in_offset=None,
                                                bounds_check=P * TT[layer] - 1, oob_is_err=False).then_inc(s["scat"], 16)

            def gather_rows(layer, t, u, wait):
                if wait:
                    pool.wait_ge(m[layer]["tr_done"], t - U + 1)
                pool.tensor_copy(idx_t[:, u, :], tab[layer][:, bass.ds(t, 1)]).then_inc(m[layer]["idx_ready"], 1)
                pool.wait_ge(m[layer]["idx_ready"], t + 1)
                pool.sem_inc(s["pool_passed"], 1)
                pool.indirect_dma_start(out=xg[:, u, :], out_offset=None, in_=xn_dram[layer],
                                        in_offset=bass.IndirectOffsetOnAxis(ap=idx_t[:, u, 0:1], axis=0)).then_inc(xg_in[u], 16)

            def gather_tiles(layer):
                pool.wait_ge(s["tabled"], 16 * (layer + 1))
                for half in range(2):
                    pool.wait_ge(xn_out[half], 16 * (NT // 2) * (layer + 1))
                for u in range(U):
                    gather_rows(layer, u, u, False)
                with pool.Fori(1, TT[layer] // U) as i:
                    for u in range(U):
                        gather_rows(layer, U * i + u, u, True)

            def gather_results(layer):
                for u in range(U):
                    pool.wait_ge(y_out[u], 16 * (T0 // U) + (16 * (T1 // U) if layer else 0))
                n = 0
                for t in range(NT):
                    for k in range(TOPK):
                        at = NT * TOPK * layer + n
                        if n >= U:
                            pool.wait_ge(back_used, at - U + 1)
                        pool.indirect_dma_start(out=xg[:, n % U, :], out_offset=None, in_=y_dram[layer],
                                                in_offset=bass.IndirectOffsetOnAxis(ap=back[:, k, t:t + 1], axis=0)).then_inc(back_in[n % U], 16)
                        n += 1

            scatter_tokens(0)
            gather_tiles(0)
            gather_results(0)
            if stop < 4:
                return
            scatter_tokens(1)
            gather_tiles(1)
            gather_results(1)

        @block.scalar
        def _(act):
            own = Chain(act, s["act_ch"])
            for dst, src in ((gate_sb[:, :, :], gate), (sw13_sb[:, :, :], sw13), (sw2_sb[:, :, :], sw2),
                             (wc_sb[:, :, 0:D], wgnn[:, :, 0:D]), (wc_sb[:, :, DA:DA + D], wgnn[:, :, D:2 * D]),
                             (wsaT_sb[:, :, :], wsaT), (acol_sb[:, :, :], acol), (wab_sb[:, :, :], wab),
                             (bab_sb[:, :], bab.partition_broadcast(P)), (bgcn_sb[:, :], bgcn.partition_broadcast(P)),
                             (wg1_sb[:, :, :], wg1), (b1_sb[:, :, :], b1),):
                act.dma_start(dst, src).then_inc(s["const_in"], 16)
            act.wait_ge(s["consts"], 1)

            def sqrt_var(n):
                act.wait_ge(s["stats_ready"], n)
                act.activation(rstd[:, :], mv[:, :, 1], ACT.Sqrt, bias=eps_sb[:, 0:1]).then_inc(s["rstd_ready"], 1)

            sqrt_var(1)

            def sqrt_count(t, half, reused):
                act.wait_ge(s["count_done"], t + 1)
                if reused:
                    wait(act, s["head_ready"], t - 1)
                act.activation(nrm[:, half, :], bank[half][:, 0:P], ACT.Sqrt).then_inc(s["nrm_ready"], 1)

            sqrt_count(0, 0, False)

            def sqrt_counts(i):
                sqrt_count(2 * i + 1, 1, True)
                sqrt_count(2 * i + 2, 0, True)

            rolled(act, NT // 2 - 1, sqrt_counts)
            sqrt_count(NT - 1, 1, True)

            act.dma_start(w1_sb[:, :, :], w1.rearrange("e p n -> p e n")).then_inc(s["w12_in"], 16)
            act.dma_start(w2_sb[:, :, :], w2.rearrange("e p n -> p e n")).then_inc(s["w12_in"], 16)
            sqrt_var(2)

            def copy_T(g, t, half, full):
                act.wait_ge(s["tr_done"], g + 2)
                wait(act, s["proj_done"], g)
                src = bank[4 + half][:, 0:D].rearrange("p (c n) -> p c n", c=DC)
                if full:
                    act.activation(xT[:, :, bass.ds(t * P, P)], src, ACT.Copy)
                act.activation(xT_t[:, half, :, :], src, ACT.Copy).then_inc(s["xts_ready"], 1)

            def copies_T(phase, full):
                def two(i):
                    for half in range(2):
                        copy_T(NT * phase + 2 * i + half, 2 * i + half, half, full)

                rolled(act, NT // 2, two)

            act.sem_inc(s["proj_done"], 1)
            copies_T(0, True)
            if stop < 2:
                return
            act.wait_ge(s["proj_done"], NT + 1)
            act.activation(lg[:, 0:NT // 2, :], bank[6][:, :].rearrange("p (t e) -> p t e", e=E0), ACT.Copy).then_inc(s["lg_ready"], 1)
            act.activation(lg[:, NT // 2:NT, :], bank[7][:, :].rearrange("p (t e) -> p t e", e=E0), ACT.Copy).then_inc(s["lg_ready"], 1)
            act.wait_ge(s["sc_ready"], 1)
            act.activation(ws[:, 0:2, :], mx8[:, :, 0:TOPK].rearrange("p t k -> p k t"), ACT.Exp, scale=-1.0).then_inc(s["w0_ready"], 1)
            for c in range(4):
                for h in range(2):
                    act.wait_ge(s["sh_h"], 2 * c + h + 1)
                    if c:
                        act.wait_ge(s["sh_g"], 2 * (c - 1) + h + 1)
                    act.activation(sth[:, h, :], bank[2 * h][:, :], ACT.Tanh, scale=0.5).then_inc(s["sh_t"], 1)

            def copy_x(layer, t, half, reused):
                act.wait_ge(m[layer]["tr_done"], t + 1)
                if reused:
                    act.wait_ge(m[layer]["h_done"], t - 1)
                act.activation(xT_t[:, half, :, :], bank[half][:, 0:D].rearrange("p (c n) -> p c n", c=DC), ACT.Copy).then_inc(m[layer]["x_ready"], 1)

            def tanh_z(t, half, reused):
                act.wait_ge(m[0]["h_done"], t + 1)
                if reused:
                    wait(act, m[0]["g_ready"], t - 1)
                act.activation(th[:, half, 0:P], bank[2 + half][:, 0:P], ACT.Tanh, scale=0.5).then_inc(m[0]["th_ready"], 1)

            copy_x(0, 0, 0, False)

            def act_step(t, u, nxt, reused, reused_x):
                if nxt:
                    copy_x(0, t + 1, (u + 1) % 2, reused_x)
                tanh_z(t, u % 2, reused)

            act_step(0, 0, True, False, False)
            turns = (T0 - 2) // U

            def expert_turn(i):
                for j in range(U):
                    act_step(U * i + 1 + j, (1 + j) % U, True, True, True)

            rolled(act, turns, expert_turn)
            for t in range(U * turns + 1, T0):
                act_step(t, t % U, t + 1 < T0, True, True)

            act.wait_ge(s["slw_ready"], 1)
            for c in range(DC):
                act.activation(wc_sb[:, c, D:DA], bank[6][:, 2 * c:2 * c + 2], ACT.Copy, scale=-1.0).then_inc(s["wcol_ready"], 1)
            for t in range(NT):
                act.wait_ge(s["stats_ready"], 2 + t + 1)
                act.activation(rstd[:, t:t + 1], mv[:, t, 1:2], ACT.Sqrt, bias=eps_sb[:, 0:1]).then_inc(s["rstd_ready"], 1)
                if t:
                    copy_T(NT + t - 1, t - 1, (t - 1) % 2, True)
            copy_T(2 * NT - 1, NT - 1, 1, True)
            if stop < 3:
                return
            for c in range(4):
                act.wait_ge(s["slbc_done"], c + 1)
                act.activation(slbc[:, c * 512:(c + 1) * 512], bank[6 + c % 2][:, :], ACT.Copy).then_inc(s["slbc_ready"], 1)

            def exp_e(t):
                act.wait_ge(s["e_neg"], t + 1)
                act.activation(negs[:, :], negs[:, :], ACT.Exp).then_inc(s["e_exp"], 1)

            def gates(t, half):
                act.wait_ge(s["pa_done"], t + 1)
                wait(act, s["o_ready"], t)
                for k in range(2):
                    act.activation(att[:, half, k:k + 1], bank[2 + half][:, D + k:D + k + 1], ACT.Tanh, scale=0.5,
                                   bias=vab[:, bass.ds(t, 1), k]).then_inc(s["at_t"], 1)

            def tanh_o(t, half):
                act.wait_ge(s["o_ready"], t + 1)
                wait(act, s["x3_done"], t)
                act.activation(th[:, half, :], av[:, half, :], ACT.Tanh, scale=0.5).then_inc(s["o_t"], 1)

            exp_e(0)

            def attention_turn(i):
                for half in range(2):
                    exp_e(2 * i + half + 1)
                    gates(2 * i + half, half)
                    tanh_o(2 * i + half, half)

            rolled(act, NT // 2 - 1, attention_turn)
            exp_e(NT - 1)
            gates(NT - 2, 0)
            tanh_o(NT - 2, 0)
            gates(NT - 1, 1)
            tanh_o(NT - 1, 1)
            if stop < 4:
                return
            sqrt_var(2 + NT + 1)
            copies_T(2, False)
            act.wait_ge(s["proj_done"], 3 * NT + 1)
            act.activation(lg[:, :, 0:E1], bank[6][:, 0:NT * E1].rearrange("p (t e) -> p t e", e=E1), ACT.Copy).then_inc(s["lg_ready"], 1)
            act.wait_ge(s["sc_ready"], 2)
            act.activation(ws[:, 1, :], ws[:, 0, :], ACT.Exp).then_inc(s["w0_ready"], 1)

            def copy_w1(t, half, reused):
                e = act.value_load(et_row[1][0:1, bass.ds(t, 1)], min_val=0, max_val=E1 - 1)
                if reused:
                    act.wait_ge(m[1]["h_done"], t - 1)
                act.activation(w1_t[:, half, :], w1_sb[:, bass.ds(e, 1), :].rearrange("p a n -> p (a n)"), ACT.Copy).then_inc(m[1]["wt_ready"], 1)

            def relu_h(t, half, reused):
                e = act.value_load(et_row[1][0:1, bass.ds(t, 1)], min_val=0, max_val=E1 - 1)
                act.wait_ge(m[1]["h_done"], t + 1)
                if reused:
                    wait(act, m[1]["y_done"], t - 1)
                for c in range(DC):
                    act.activation(g_t[:, half, c, :], bank[2 + half][:, c * P:(c + 1) * P], ACT.Relu,
                                   bias=b1_sb[:, bass.ds(e, 1), c]).then_inc(m[1]["g_ready"], 1)

            def sd_y(t, half):
                act.wait_ge(m[1]["var_ready"], t + 1)
                act.activation(att[:, half, 0:1], mvl[:, half, 1:2], ACT.Sqrt, bias=eps_sb[:, 0:1]).then_inc(m[1]["sd_ready"], 1)

            act.wait_ge(s["w12_in"], 32)
            act.wait_ge(s["const_in"], 16 * CONSTS)
            act.wait_ge(s["et_in"], 32)
            copy_w1(0, 0, False)
            copy_x(1, 0, 0, False)

            def act_step1(t, u, nxt, prev, reused):
                if nxt:
                    copy_w1(t + 1, (u + 1) % 2, reused)
                    copy_x(1, t + 1, (u + 1) % 2, reused)
                relu_h(t, u % 2, reused)
                if prev:
                    sd_y(t - 1, (u + 1) % 2)

            act_step1(0, 0, True, False, False)
            turns = (T1 - 2) // U

            def expert_turn1(i):
                for j in range(U):
                    act_step1(U * i + 1 + j, (1 + j) % U, True, True, True)

            rolled(act, turns, expert_turn1)
            for t in range(U * turns + 1, T1):
                act_step1(t, t % U, t + 1 < T1, True, True)
            sd_y(T1 - 1, (T1 - 1) % 2)

        @block.vector
        def _(dve):
            own = Chain(dve, s["dve"])
            link = own.link
            dve.sem_inc(s["tr_done"], 1)
            dve.wait_ge(s["consts"], 1)
            dve.wait_ge(s["x_in"], 16)

            def normalise(dst, t):
                return dve.tensor_scalar(dst, xs[:, t, :], mv[:, t, 0:1], rstd[:, t:t + 1], ALU.subtract, ALU.mult)

            link(dve.memset(rowsP[:, :, D:DA], 1.0))
            for t in range(NT):
                last = dve.bn_stats(st6[:, t, :], xs[:, t, :])
            link(last)
            for t in range(NT):
                last = dve.bn_aggr(mv[:, t, :], st6[:, t, :])
            last.then_inc(s["stats_ready"], 1)
            dve.wait_ge(s["rstd_ready"], 1)
            link(dve.reciprocal(rstd[:, :], rstd[:, :]))
            for t in range(NT):
                last = normalise(rowsP[:, t, 0:D], t)
            link(last)
            LN0 = own.n

            def mask_adj(t, turn, half):
                dve.wait_ge(adj_in[half], 16 * turn + 16)
                wait(dve, s["count_done"], t - 1)
                dve.tensor_scalar(mask[:, half, :], adj_buf[:, half, :], 0.0, None, ALU.is_gt).then_inc(s["mask_ready"], 1)

            def heads(t, half, reused):
                dve.wait_ge(s["nrm_ready"], t + 1)
                if reused:
                    wait(dve, s["prod_done"], t - 1)
                link(dve.tensor_scalar(nrm[:, half, :], nrm[:, half, :], 1e-12, None, ALU.max))
                link(dve.reciprocal(nrm[:, half, :], nrm[:, half, :]))
                dve.scalar_tensor_tensor(out=inc_buf[:, half, :].rearrange("p (t i) -> p t i", i=P),
                                         in0=adj_buf[:, half, :].rearrange("p (t i) -> p t i", i=P), scalar=0.0,
                                         in1=nrm[:, half, :].unsqueeze(1).to_broadcast([P, NT, P]),
                                         op0=ALU.is_gt, op1=ALU.mult).then_inc(s["head_ready"], 1)

            def passed():
                dve.sem_inc(s["waits_passed"], 1)

            def statistics(t, half):
                passed()
                link(dve.bn_stats(st6l[:, half, :], xs[:, bass.ds(t, 1), :].rearrange("p a d -> p (a d)")))
                passed()
                link(dve.bn_aggr(mvl[:, half, :], st6l[:, half, :]))
                link(dve.tensor_copy(mv[:, bass.ds(t, 1), :].rearrange("p a d -> p (a d)"), mvl[:, half, :]))

            def finish_rows(t, half):
                dve.wait_ge(s["prod_done"], t + 1)
                link(dve.reciprocal(rden[:, half:half + 1], bank[2 + half][:, D:D + 1]))
                row = xs[:, bass.ds(t, 1), :].rearrange("p a d -> p (a d)")
                dve.scalar_tensor_tensor(out=row, in0=bank[2 + half][:, 0:D], scalar=rden[:, half:half + 1], in1=row,
                                         op0=ALU.mult, op1=ALU.add).then_inc(s["x1_done"], 1)
                dve.wait_ge(s["x1_done"], t + 1)
                statistics(t, half)

            mask_adj(0, 0, 0)
            mask_adj(1, 0, 1)
            heads(0, 0, False)

            def aggregate_turn(i):
                for j, half in ((1, 1), (2, 0)):
                    mask_adj(2 * i + j + 1, i + 1, 1 - half)
                    heads(2 * i + j, half, True)
                    finish_rows(2 * i + j - 1, 1 - half)

            rolled(dve, NT // 2 - 1, aggregate_turn, own, 12)
            heads(NT - 1, 1, True)
            finish_rows(NT - 2, 0)
            finish_rows(NT - 1, 1)
            dve.sem_inc(s["stats_ready"], 1)

            def normalise_tiles(phase, layer):
                link(dve.reciprocal(rstd[:, :], rstd[:, :]))
                def two(i):
                    for half in range(2):
                        t = 2 * i + half
                        g = NT * phase + t
                        wait(dve, s["tr_done"], g)
                        wait(dve, xn_out[half], 16 * (NT // 2) * layer + 16 * i)
                        dve.tensor_scalar(xn_t[:, half, :], xs[:, bass.ds(t, 1), :].rearrange("p a d -> p (a d)"),
                                          mv[:, bass.ds(t, 1), 0], rstd[:, bass.ds(t, 1)], ALU.subtract, ALU.mult).then_inc(s["ln_ready"], 1)

                rolled(dve, NT // 2, two)

            dve.wait_ge(s["rstd_ready"], 2)
            normalise_tiles(0, 0)
            if stop < 2:
                dve.wait_ge(s["ln_ready"], NT)
                dve.sem_inc(s["route_end"], 1)
                return

            def route(layer):
                E, T = (E0, T0) if layer == 0 else (E1, T1)
                logit = lg[:, :, 0:E]
                oh = onehot[:, :, :, 0:E]
                dve.wait_ge(s["lg_ready"], 3 if layer else 2)
                for t in range(NT):
                    last = dve.max(mx8[:, t, :], logit[:, t, :])
                link(last)
                if layer:
                    link(dve.tensor_tensor(ws[:, 0, :], mx8[:, :, 1], mx8[:, :, 0], ALU.subtract))
                dve.sem_inc(s["sc_ready"], 1)
                for t in range(NT):
                    last = dve.max_index(ix8[:, t, :], mx8[:, t, :], logit[:, t, :])
                link(last)
                link(dve.tensor_copy(ixf[:, :, :], ix8[:, :, 0:TOPK]))
                for k in range(TOPK):
                    last = dve.tensor_tensor(oh[:, k], iota_e[:, 0:E].unsqueeze(1).to_broadcast([P, NT, E]),
                                             ixf[:, :, k:k + 1].to_broadcast([P, NT, E]), ALU.is_equal)
                link(last)
                link(dve.memset(pre[:, 0, 0:E], 0.0))
                link(dve.tensor_tensor(cnt[:, :, 0:E], oh[:, 0], oh[:, 1], ALU.add))
                for t in range(NT):
                    link(dve.tensor_tensor(pre[:, t + 1, 0:E], pre[:, t, 0:E], cnt[:, t, 0:E], ALU.add))
                dve.sem_inc(s["cnt_ready"], 1)
                dve.wait_ge(s["w0_ready"], layer + 1)
                if layer == 0:
                    link(dve.tensor_scalar(ws[:, 0:2, :], ws[:, 0:2, :], 1.0, None, ALU.add))
                    link(dve.reciprocal(ws[:, 0:2, :], ws[:, 0:2, :]))
                    link(dve.tensor_tensor(ws[:, 2, :], ws[:, 0, :], ws[:, 1, :], ALU.add))
                    link(dve.tensor_scalar(ws[:, 2, :], ws[:, 2, :], 1e-20, None, ALU.add))
                    link(dve.reciprocal(ws[:, 3, :], ws[:, 2, :]))
                    for k in range(TOPK):
                        last = dve.scalar_tensor_tensor(out=wts[:, k, :], in0=ws[:, k, :], scalar=ROUTE_SCALE, in1=ws[:, 3, :], op0=ALU.mult, op1=ALU.mult)
                    link(last)
                else:
                    link(dve.tensor_scalar(ws[:, 2, :], ws[:, 1, :], 1.0, None, ALU.add))
                    link(dve.reciprocal(wts[:, 0, :], ws[:, 2, :]))
                    link(dve.tensor_tensor(wts[:, 1, :], wts[:, 0, :], ws[:, 1, :], ALU.mult))
                dve.wait_ge(s["pos_done"], layer + 1)
                tt = bank[5][:, 256:256 + E]
                if layer == 0:
                    link(dve.tensor_scalar(tot[:, 0, 0:E], tt, float(CAP), float(P - 1), ALU.min, ALU.add))
                else:
                    link(dve.tensor_scalar(tot[:, 0, 0:E], tt, float(P - 1), None, ALU.add))
                link(dve.tensor_copy(toti[:, 0:E], tot[:, 0, 0:E]))
                link(dve.tensor_scalar(toti[:, 0:E], toti[:, 0:E], 7, None, ALU.arith_shift_right))
                link(dve.tensor_copy(tot[:, 1, 0:E], toti[:, 0:E]))
                link(dve.tensor_tensor_scan(tot[:, 2, 0:E], ones_e[:, 0:E], tot[:, 1, 0:E], 0.0, ALU.mult, ALU.add))
                link(dve.tensor_tensor(tot[:, 3, 0:E], tot[:, 2, 0:E], tot[:, 1, 0:E], ALU.subtract))
                link(dve.tensor_scalar(et_junk[:, 0:E], tot[:, 2, 0:E], tile_no[:, 0:1], None, ALU.is_le))
                link(dve.reduce_sum(et_f[:, :], et_junk[:, 0:E], X))
                link(dve.tensor_scalar(et_f[:, :], et_f[:, :], float(E - 1), None, ALU.min))
                dve.tensor_copy(et_i[:, :], et_f[:, :]).then_inc(s["rt_ready"], 1)
                if layer == 0:
                    for b in range(2):
                        pos = bank[6 + b][:, :].rearrange("p (t e) -> p t e", e=E)
                        h = slice(b * NT // 2, (b + 1) * NT // 2)
                        last = dve.tensor_scalar(rt1[:, h, :], pos, float(CAP), DROPPED, ALU.is_ge, ALU.mult)
                    link(last)
                    for b in range(2):
                        pos = bank[6 + b][:, :].rearrange("p (t e) -> p t e", e=E)
                        h = slice(b * NT // 2, (b + 1) * NT // 2)
                        last = dve.tensor_tensor(rt1[:, h, :], rt1[:, h, :], pos, ALU.add)
                    link(last)
                else:
                    link(dve.tensor_copy(rt1[:, :, 0:E], bank[7][:, 0:NT * E].rearrange("p (t e) -> p t e", e=E)))
                link(dve.scalar_tensor_tensor(out=rt1[:, :, 0:E], in0=tot[:, 3, 0:E].unsqueeze(1).to_broadcast([P, NT, E]), scalar=float(P),
                                              in1=rt1[:, :, 0:E], op0=ALU.mult, op1=ALU.add))
                for k in range(TOPK):
                    link(dve.tensor_tensor(sel[:, :, 0:E], oh[:, k], rt1[:, :, 0:E], ALU.mult))
                    link(dve.reduce_sum(slot[:, k, :], sel[:, :, 0:E], X))
                link(dve.tensor_copy(slot_i[:, :, :], slot[:, :, :]))
                link(dve.tensor_scalar(sp_i[:, :, :], slot_i[:, :, :], P - 1, None, ALU.bitwise_and))
                link(dve.tensor_copy(sp_f[:, :, :], sp_i[:, :, :]))
                link(dve.tensor_scalar(sp_i[:, :, :], slot_i[:, :, :], 7, None, ALU.arith_shift_right))
                link(dve.tensor_copy(sq_f[:, :, :], sp_i[:, :, :]))
                link(dve.scalar_tensor_tensor(out=sp_f[:, :, :], in0=sp_f[:, :, :], scalar=float(T), in1=sq_f[:, :, :], op0=ALU.mult, op1=ALU.add))
                dve.tensor_copy(addr[:, :, :], sp_f[:, :, :]).then_inc(s["addr_ready"], 1)
                if layer == 0:
                    link(dve.tensor_scalar(sq_f[:, :, :], slot[:, :, :], DROPPED, None, ALU.is_lt))
                    link(dve.tensor_tensor(slot[:, :, :], slot[:, :, :], sq_f[:, :, :], ALU.mult))
                    link(dve.tensor_tensor(wts[:, :, :], wts[:, :, :], sq_f[:, :, :], ALU.mult))
                link(dve.tensor_copy(back[:, :, :], slot[:, :, :]))

            route(0)

            for c in range(4):
                for h in range(2):
                    dve.wait_ge(s["sh_t"], 2 * c + h + 1)
                    link(dve.scalar_tensor_tensor(out=sav[:, h, :], in0=sth[:, h, :], scalar=1.0, in1=bank[2 * h][:, :], op0=ALU.add, op1=ALU.mult))
                    if c:
                        dve.wait_ge(s["sh_y"], 4 * c)
                    dve.scalar_tensor_tensor(out=sg[:, h, :], in0=bank[2 * h + 1][:, :], scalar=0.5, in1=sav[:, h, :],
                                             op0=ALU.mult, op1=ALU.mult).then_inc(s["sh_g"], 1)
                for j in range(4):
                    t = 4 * c + j
                    dve.wait_ge(s["sh_y"], t + 1)
                    dve.tensor_tensor(xs[:, t, :], bank[4 + j % 2][:, 0:D], xs[:, t, :], ALU.add).then_inc(s["sh_x"], 1)

            def gate_h(t, half, reused):
                dve.wait_ge(m[0]["th_ready"], t + 1)
                link(dve.scalar_tensor_tensor(out=av[:, half, 0:P], in0=th[:, half, 0:P], scalar=1.0, in1=bank[2 + half][:, 0:P], op0=ALU.add, op1=ALU.mult))
                if reused:
                    wait(dve, m[0]["y_done"], t - 1)
                dve.scalar_tensor_tensor(out=g_t[:, half, 0, :], in0=bank[2 + half][:, P:2 * P], scalar=0.5, in1=av[:, half, 0:P],
                                         op0=ALU.mult, op1=ALU.mult).then_inc(m[0]["g_ready"], 1)

            def copy_y(t, u, turn):
                dve.wait_ge(m[0]["y_done"], t + 1)
                wait(dve, y_out[u], 16 * turn)
                dve.tensor_copy(y_sb[:, u, :], bank[4 + u % 2][:, 0:D]).then_inc(m[0]["y_ready"], 1)

            gate_h(0, 0, False)
            turns = (T0 - 2) // U

            def expert_turn(i):
                for j in range(U):
                    gate_h(U * i + 1 + j, (1 + j) % 2, True)
                    copy_y(U * i + j, j, i)

            rolled(dve, turns, expert_turn, own, U)
            for t in range(U * turns + 1, T0):
                gate_h(t, t % 2, True)
                copy_y(t - 1, (t - 1) % U, (t - 1) // U)
            copy_y(T0 - 1, (T0 - 1) % U, (T0 - 1) // U)

            dve.wait_ge(s["const_in"], 16 * CONSTS)
            dve.wait_ge(s["wcol_ready"], DC)
            link(dve.tensor_copy(slw[:, :, :], wc_sb[:, :, D:D + 1].to_broadcast([P, DC, P])))
            link(dve.tensor_copy(wc_sb[:, :, DA + D:2 * DA], wab_sb[:, :, 0:2]))
            link(dve.tensor_copy(wv_sb[:, :, :], wab_sb[:, :, 2:4]))
            dve.sem_inc(s["gnn_in"], 1)

            def combine(layer, t):
                for k in range(TOPK):
                    n = TOPK * t + k
                    dve.wait_ge(back_in[n % U], 16 * (n // U + 1) + 16 * (TOPK * NT // U) * layer)
                    dve.scalar_tensor_tensor(out=xs[:, t, :], in0=xg[:, n % U, :], scalar=wts[:, k, t:t + 1], in1=xs[:, t, :],
                                             op0=ALU.mult, op1=ALU.add).then_inc(back_used, 1)
                    dve.wait_ge(back_used, NT * TOPK * layer + n + 1)

            def norm_t(t):
                dve.wait_ge(s["rstd_ready"], 2 + t + 1)
                link(dve.reciprocal(rstd[:, t:t + 1], rstd[:, t:t + 1]))
                dve.wait_ge(s["tr_done"], NT + t)
                dve.wait_ge(xn_out[t % 2], 16 * (NT // 2))
                normalise(xn_t[:, t % 2, :], t).then_inc(s["ln_ready"], 1)

            def keep_proj(t):
                half = t % 2
                dve.wait_ge(s["proj_done"], 1 + NT + t + 1)
                dve.tensor_copy(rowsP[:, t, 0:D], bank[half][:, 0:D])
                dve.tensor_copy(srn[:, t:t + 1], bank[half][:, D + 1:D + 2])
                dve.tensor_copy(rowsQ[:, t, :], bank[2 + half][:, 0:DA])
                link(dve.tensor_tensor(vab[:, t, :], bank[2 + half][:, DA:DA + 2], bab_sb[:, :], ALU.add))
                dve.tensor_scalar(vab[:, t, :], vab[:, t, :], 0.5, None, ALU.mult).then_inc(s["proj_used"], 1)

            for t in range(NT):
                combine(0, t)
                link(dve.bn_stats(st6[:, t, :], xs[:, t, :]))
                dve.bn_aggr(mv[:, t, :], st6[:, t, :]).then_inc(s["stats_ready"], 1)
                if t >= 1:
                    norm_t(t - 1)
                if t >= 3:
                    keep_proj(t - 3)
            norm_t(NT - 1)
            for t in range(NT - 3, NT):
                keep_proj(t)
            if stop < 3:
                dve.sem_inc(s["route_end"], 2)
                return

            def attention(t, turn, half, reused):
                v = lambda a: a.rearrange("p (t i) -> p t i", i=P)
                link(dve.tensor_tensor(v(negs[:, :]), slbc[:, bass.ds(t * P, P)].unsqueeze(1).to_broadcast([P, NT, P]),
                                       srn[:, :].unsqueeze(2).to_broadcast([P, NT, P]), ALU.add))
                dve.scalar_tensor_tensor(out=negs[:, :], in0=negs[:, :], scalar=0.01, in1=negs[:, :], op0=ALU.mult, op1=ALU.min).then_inc(s["e_neg"], 1)
                dve.wait_ge(s["e_exp"], t + 1)
                dve.wait_ge(adj_in[half], 16 * (NT // 2) + 16 * turn + 16)
                if reused:
                    dve.wait_ge(s["pe_done"], t - 1)
                dve.scalar_tensor_tensor(out=inc_buf[:, half, :], in0=adj_buf[:, half, :], scalar=0.0, in1=negs[:, :],
                                         op0=ALU.not_equal, op1=ALU.mult).then_inc(s["e_ready"], 1)
                dve.wait_ge(s["e_ready"], t + 1)

            def finish_nodes(t, half):
                dve.wait_ge(s["pe_done"], t + 1)
                dve.wait_ge(s["at_t"], 2 * t + 2)
                link(dve.tensor_scalar(att[:, half, 0:2], att[:, half, 0:2], 0.5, 0.5, ALU.mult, ALU.add))
                link(dve.tensor_scalar(att[:, half, 2:3], bank[half][:, D:D + 1], 1e-5, None, ALU.add))
                link(dve.reciprocal(att[:, half, 3:4], att[:, half, 2:3]))
                link(dve.tensor_tensor(att[:, half, 2:3], att[:, half, 3:4], att[:, half, 0:1], ALU.mult))
                link(dve.tensor_tensor(av[:, half, :], bank[2 + half][:, 0:D], bgcn_sb[:, :], ALU.add))
                link(dve.tensor_scalar(av[:, half, :], av[:, half, :], att[:, half, 1:2], None, ALU.mult))
                dve.scalar_tensor_tensor(out=av[:, half, :], in0=bank[half][:, 0:D], scalar=att[:, half, 2:3], in1=av[:, half, :],
                                         op0=ALU.mult, op1=ALU.add).then_inc(s["o_ready"], 1)

            def add_nodes(t, half):
                dve.wait_ge(s["o_t"], t + 1)
                row = xs[:, bass.ds(t, 1), :].rearrange("p a d -> p (a d)")
                link(dve.scalar_tensor_tensor(out=row, in0=th[:, half, :], scalar=0.5, in1=row, op0=ALU.mult, op1=ALU.add))
                dve.tensor_scalar(row, row, 0.5, None, ALU.add).then_inc(s["x3_done"], 1)
                dve.wait_ge(s["x3_done"], t + 1)
                statistics(t, half)

            dve.wait_ge(s["slbc_ready"], 4)
            attention(0, 0, 0, False)
            attention(1, 0, 1, False)
            finish_nodes(0, 0)

            def attention_turn(i):
                for j, half in ((1, 1), (2, 0)):
                    attention(2 * i + j + 1, i + 1, 1 - half, True)
                    add_nodes(2 * i + j - 1, 1 - half)
                    finish_nodes(2 * i + j, half)

            rolled(dve, NT // 2 - 1, attention_turn, own, 22)
            add_nodes(NT - 2, 0)
            finish_nodes(NT - 1, 1)
            add_nodes(NT - 1, 1)
            dve.sem_inc(s["stats_ready"], 1)
            if stop < 4:
                dve.sem_inc(s["route_end"], 3)
                return
            dve.wait_ge(s["rstd_ready"], 2 + NT + 1)
            normalise_tiles(2, 1)
            route(1)

            def stats_y(t, half):
                dve.wait_ge(m[1]["y_done"], t + 1)
                passed()
                link(dve.bn_stats(st6l[:, half, :], bank[4 + half][:, 0:D]))
                passed()
                dve.bn_aggr(mvl[:, half, :], st6l[:, half, :]).then_inc(m[1]["var_ready"], 1)

            def norm_y(t, u, turn):
                half = u % 2
                e = dve.value_load(et_row[1][0:1, bass.ds(t, 1)], min_val=0, max_val=E1 - 1)
                dve.wait_ge(m[1]["sd_ready"], t + 1)
                link(dve.reciprocal(att[:, half, 1:2], att[:, half, 0:1]))
                dve.wait_ge(y_out[u], 16 * (T0 // U) + 16 * turn)
                link(dve.tensor_scalar(y_sb[:, u, :], bank[4 + half][:, 0:D], mvl[:, half, 0:1], att[:, half, 1:2], ALU.subtract, ALU.mult))
                link(dve.tensor_tensor(y_sb[:, u, :], y_sb[:, u, :], gam_bc[:, bass.ds(e, 1), :].rearrange("p a d -> p (a d)"), ALU.mult))
                dve.tensor_tensor(y_sb[:, u, :], y_sb[:, u, :], bet_bc[:, bass.ds(e, 1), :].rearrange("p a d -> p (a d)"), ALU.add).then_inc(m[1]["y_ready"], 1)

            dve.wait_ge(s["et_in"], 32)
            dve.wait_ge(s["gb_in"], 48)
            stats_y(0, 0)
            turns = (T1 - 2) // U

            def expert_turn1(i):
                for j in range(U):
                    stats_y(U * i + 1 + j, (1 + j) % 2)
                    norm_y(U * i + j, j, i)

            rolled(dve, turns, expert_turn1, own, 4 * U)
            for t in range(U * turns + 1, T1):
                stats_y(t, t % 2)
                norm_y(t - 1, (t - 1) % U, (t - 1) // U)
            norm_y(T1 - 1, (T1 - 1) % U, (T1 - 1) // U)
            for t in range(NT):
                combine(1, t)
                dve.sem_inc(s["x3_done"], 1)

        @block.tensor
        def _(pe):
            pe.wait_ge(s["consts"], 1)

            def count(t, half, reused):
                pe.wait_ge(s["mask_ready"], t + 1)
                if reused:
                    pe.wait_ge(s["nrm_ready"], t - 1)
                for j in range(NT):
                    last = pe.matmul(bank[half][:, 0:P], ones_b[:, :], mask[:, half, j * P:(j + 1) * P], start=(j == 0), stop=(j == NT - 1))
                last.then_inc(s["count_done"], 1)

            def product(ready, t, half, lhs, rhs, cols, dst, done):
                pe.wait_ge(ready, t + 1)
                for j in range(NT):
                    last = pe.matmul(dst[:, 0:cols], lhs[:, half, j * P:(j + 1) * P], rhs[:, j, 0:cols], start=(j == 0), stop=(j == NT - 1))
                last.then_inc(done, 1)

            def aggregate(t, half, reused):
                if reused:
                    wait(pe, s["x1_done"], t - 1)
                product(s["inc_ready"], t, half, inc_buf, rowsP, D + 1, bank[2 + half], s["prod_done"])

            count(0, 0, False)
            count(1, 1, False)
            pe.wait_ge(s["dve"], 4)
            aggregate(0, 0, False)

            def aggregate_turn(i):
                count(2 * i + 2, 0, True)
                aggregate(2 * i + 1, 1, True)
                count(2 * i + 3, 1, True)
                aggregate(2 * i + 2, 0, True)

            rolled(pe, NT // 2 - 1, aggregate_turn)
            aggregate(NT - 1, 1, True)

            def transposes(g, half):
                pe.wait_ge(s["ln_ready"], g + 1)
                for c in range(DC):
                    last = pe.transpose(bank[4 + half][:, c * P:(c + 1) * P], xn_t[:, half, c * P:(c + 1) * P], ident[:, :])
                last.then_inc(s["tr_done"], 1)

            def logits(phase, t, half, w, dst):
                g = NT * phase + t
                pe.wait_ge(s["xts_ready"], g + 1)
                for c in range(DC):
                    last = pe.matmul(dst, xT_t[:, half, c, :], w[:, c, :], start=(c == 0), stop=(c == DC - 1))
                last.then_inc(s["proj_done"], 1)

            pe.wait_ge(s["const_in"], 16 * CONSTS)

            def route_logits(phase, w, E, banks):
                per = NT // len(banks)
                for b, bk in enumerate(banks):
                    with pe.Fori(0, per // 2) as i:
                        for half in range(2):
                            t = 2 * i + half + per * b
                            transposes(NT * phase + t, half)
                            logits(phase, t, half, w, bk[:, bass.ds((2 * i + half) * E, E)])

            def positions(layer, E, banks, total):
                pe.wait_ge(s["cnt_ready"], layer + 1)
                per = NT // len(banks)
                for b, bk in enumerate(banks):
                    for j in range(per):
                        t = b * per + j
                        pe.matmul(bk[:, j * E:(j + 1) * E], tri_b[:, :], cnt[:, t, 0:E], start=True, stop=False)
                        pe.matmul(bk[:, j * E:(j + 1) * E], ones_b[:, :], pre[:, t, 0:E], start=False, stop=True)
                pe.matmul(total[:, 256:256 + E], ones_b[:, :], pre[:, NT, 0:E], start=True, stop=True).then_inc(s["pos_done"], 1)

            route_logits(0, gate_sb, E0, [bank[6], bank[7]])
            if stop < 2:
                return
            pe.wait_ge(s["lg_ready"], 2)
            positions(0, E0, [bank[6], bank[7]], bank[5])

            for c in range(4):
                for h in range(2):
                    if c:
                        pe.wait_ge(s["sh_g"], 2 * (c - 1) + h + 1)
                    for v in range(2):
                        for k in range(DC):
                            last = pe.matmul(bank[2 * h + v][:, :], sw13_sb[:, k, v * D + h * P:v * D + (h + 1) * P], xT[:, k, c * 512:(c + 1) * 512],
                                             start=(k == 0), stop=(k == DC - 1))
                    last.then_inc(s["sh_h"], 1)
                pe.wait_ge(s["sh_g"], 2 * c + 2)
                for j in range(4):
                    t = 4 * c + j
                    if t >= 2:
                        pe.wait_ge(s["sh_x"], t - 1)
                    for k in range(DC):
                        last = pe.matmul(bank[4 + j % 2][:, 0:D], sg[:, k, j * P:(j + 1) * P], sw2_sb[:, k, :], start=(k == 0), stop=(k == DC - 1))
                    last.then_inc(s["sh_y"], 1)
            pe.wait_ge(s["sh_x"], NT)

            def tr_x(layer, t, u, turn, reused):
                base = 16 * (T0 // U) * layer
                pe.wait_ge(xg_in[u], base + 16 * turn + 16)
                if reused:
                    wait(pe, m[layer]["x_ready"], t - 1)
                for c in range(DC):
                    last = pe.transpose(bank[u % 2][:, c * P:(c + 1) * P], xg[:, u, c * P:(c + 1) * P], ident[:, :])
                last.then_inc(m[layer]["tr_done"], 1)

            def hidden0(t, u, turn, reused):
                half = u % 2
                pe.wait_ge(m[0]["x_ready"], t + 1)
                pe.wait_ge(wm_in[u], 16 * turn + 16)
                if reused:
                    wait(pe, m[0]["g_ready"], t - 1)
                for v in range(2):
                    for k in range(DC):
                        last = pe.matmul(bank[2 + half][:, v * P:(v + 1) * P], wm[:, u, v * D + k * P:v * D + (k + 1) * P], xT_t[:, half, k, :],
                                         start=(k == 0), stop=(k == DC - 1))
                last.then_inc(m[0]["h_done"], 1)

            def down0(t, u):
                half = u % 2
                pe.wait_ge(m[0]["g_ready"], t + 1)
                if not isinstance(t, int) or t >= 2:
                    pe.wait_ge(m[0]["y_ready"], t - 1)
                pe.matmul(bank[4 + half][:, 0:D], g_t[:, half, 0, :], wm[:, u, 2 * D:3 * D], start=True, stop=True).then_inc(m[0]["y_done"], 1)

            tr_x(0, 0, 0, 0, False)
            tr_x(0, 1, 1, 0, False)
            hidden0(0, 0, 0, False)
            for t in (1, 2):
                tr_x(0, t + 1, t + 1, 0, True)
                hidden0(t, t, 0, True)
                down0(t - 1, t - 1)
            turns = (T0 - 4) // U
            with pe.Fori(0, turns) as i:
                for j in range(U):
                    t, u = U * i + 3 + j, (3 + j) % U
                    tr_x(0, t + 1, (u + 1) % U, i + 1, True)
                    hidden0(t, u, i + (1 if j else 0), True)
                    down0(t - 1, (u - 1) % U)
            for t in range(U * turns + 3, T0):
                if t + 1 < T0:
                    tr_x(0, t + 1, (t + 1) % U, (t + 1) // U, True)
                hidden0(t, t % U, t // U, True)
                down0(t - 1, (t - 1) % U)
            down0(T0 - 1, (T0 - 1) % U)

            for c in range(DC):
                for k in range(DC):
                    last = pe.matmul(bank[6][:, 2 * c:2 * c + 2], wsaT_sb[:, k, c * P:(c + 1) * P], acol_sb[:, k, :], start=(k == 0), stop=(k == DC - 1))
            last.then_inc(s["slw_ready"], 1)
            pe.wait_ge(s["gnn_in"], 1)
            pe.wait_ge(m[0]["y_ready"], T0)

            def project(t):
                half = t % 2
                g = NT + t
                pe.wait_ge(s["xts_ready"], g + 1)
                if t >= 2:
                    pe.wait_ge(s["proj_used"], t - 1)
                for k in range(DC):
                    pe.matmul(bank[half][:, 0:DA], xT_t[:, half, k, :], wc_sb[:, k, 0:DA], start=(k == 0), stop=(k == DC - 1))
                for k in range(DC):
                    pe.matmul(bank[2 + half][:, 0:DA], xT_t[:, half, k, :], wc_sb[:, k, DA:2 * DA], start=(k == 0), stop=(k == DC - 1))
                for k in range(DC):
                    last = pe.matmul(bank[2 + half][:, DA:DA + 2], xT_t[:, half, k, :], wv_sb[:, k, :], start=(k == 0), stop=(k == DC - 1))
                last.then_inc(s["proj_done"], 1)

            for t in range(NT):
                transposes(NT + t, t % 2)
                if t >= 1:
                    project(t - 1)
            project(NT - 1)
            if stop < 3:
                return
            for c in range(4):
                if c >= 2:
                    pe.wait_ge(s["slbc_ready"], c - 1)
                for k in range(DC):
                    last = pe.matmul(bank[6 + c % 2][:, :], slw[:, k, :], xT[:, k, c * 512:(c + 1) * 512], start=(k == 0), stop=(k == DC - 1))
                last.then_inc(s["slbc_done"], 1)
            pe.wait_ge(s["proj_used"], NT)

            def attend(t, turn, half, reused):
                if reused:
                    pe.wait_ge(s["o_ready"], t - 1)
                pe.wait_ge(adj_in[half], 16 * (NT // 2) + 16 * turn + 16)
                for j in range(NT):
                    last = pe.matmul(bank[2 + half][:, 0:DA], adj_buf[:, half, j * P:(j + 1) * P], rowsQ[:, j, :], start=(j == 0), stop=(j == NT - 1))
                last.then_inc(s["pa_done"], 1)
                product(s["e_ready"], t, half, inc_buf, rowsP, D + 1, bank[half], s["pe_done"])

            attend(0, 0, 0, False)
            attend(1, 0, 1, False)
            with pe.Fori(1, NT // 2) as i:
                for half in range(2):
                    attend(2 * i + half, i, half, True)
            if stop < 4:
                return
            route_logits(2, wg1_sb, E1, [bank[6]])
            positions(1, E1, [bank[7]], bank[5])

            def hidden1(t, u, reused):
                half = u % 2
                pe.wait_ge(m[1]["x_ready"], t + 1)
                pe.wait_ge(m[1]["wt_ready"], t + 1)
                if reused:
                    wait(pe, m[1]["g_ready"], 2 * t - 2)
                for c in range(DC):
                    for k in range(DC):
                        last = pe.matmul(bank[2 + half][:, c * P:(c + 1) * P], w1_t[:, half, k * H1 + c * P:k * H1 + (c + 1) * P], xT_t[:, half, k, :],
                                         start=(k == 0), stop=(k == DC - 1))
                last.then_inc(m[1]["h_done"], 1)

            def down1(t, u):
                half = u % 2
                e = pe.value_load(et_row[1][0:1, bass.ds(t, 1)], min_val=0, max_val=E1 - 1)
                pe.wait_ge(m[1]["g_ready"], 2 * t + 2)
                if not isinstance(t, int) or t >= 2:
                    pe.wait_ge(m[1]["y_ready"], t - 1)
                for k in range(DC):
                    pe.matmul(bank[4 + half][:, 0:D], g_t[:, half, k, :], w2_sb[:, bass.ds(e, 1), k * D:(k + 1) * D].rearrange("p a d -> p (a d)"), start=(k == 0), stop=False)
                pe.matmul(bank[4 + half][:, 0:D], ones_f[0:1, :], b2_sb[0:1, bass.ds(e, 1), :].rearrange("p a d -> p (a d)"), start=False, stop=True).then_inc(m[1]["y_done"], 1)

            pe.wait_ge(s["w12_in"], 32)
            pe.wait_ge(s["gb_in"], 48)
            pe.wait_ge(s["et_in"], 32)
            tr_x(1, 0, 0, 0, False)
            tr_x(1, 1, 1, 0, False)
            hidden1(0, 0, False)
            for t in (1, 2):
                tr_x(1, t + 1, t + 1, 0, True)
                hidden1(t, t, True)
                down1(t - 1, t - 1)
            turns = (T1 - 4) // U
            with pe.Fori(0, turns) as i:
                for j in range(U):
                    t, u = U * i + 3 + j, (3 + j) % U
                    tr_x(1, t + 1, (u + 1) % U, i + 1, True)
                    hidden1(t, u, True)
                    down1(t - 1, (u - 1) % U)
            for t in range(U * turns + 3, T1):
                if t + 1 < T1:
                    tr_x(1, t + 1, (t + 1) % U, (t + 1) // U, True)
                hidden1(t, t % U, True)
                down1(t - 1, (t - 1) % U)
            down1(T1 - 1, (T1 - 1) % U)


def kernel(x, adj, L0_ffn_gate_w, L0_ffn_w1, L0_ffn_w3, L0_ffn_w2, L0_ffn_sw1, L0_ffn_sw3, L0_ffn_sw2, L1_gnn_W_sa, L1_gnn_a_sa,
           L1_gnn_W_gcnb, L1_gnn_b_gcnb, L1_gnn_Wa, L1_gnn_ba, L1_gnn_Wb, L1_gnn_bb, L1_ffn_Wg, L1_ffn_W1, L1_ffn_b1, L1_ffn_W2,
           L1_ffn_b2, L1_ffn_gamma, L1_ffn_beta):
    import numpy as np
    import concourse.bacc as bacc
    from concourse.bass_utils import run_bass_kernel_spmd as run

    def chunked(w):
        w = np.asarray(w)
        return w.reshape(w.shape[0] // P, P, -1).transpose(1, 0, 2)

    def per_expert(w):
        w = np.asarray(w)
        e, k, n = w.shape
        return w.reshape(e, k // P, P, n).transpose(0, 2, 1, 3).reshape(e, P, k // P * n)

    wa, wb = np.asarray(L1_gnn_Wa), np.asarray(L1_gnn_Wb)
    columns = np.concatenate([wa[:, :D], wb[:, :D], wa[:, D:], wb[:, D:]], axis=0).T
    arrays = {
        "x": x,
        "adjb": np.asarray(adj).reshape(NT, P, NT, P).transpose(0, 3, 2, 1).reshape(NT, P, N),
        "gate": chunked(np.asarray(L0_ffn_gate_w).T),
        "sw13": np.concatenate([chunked(L0_ffn_sw1), chunked(L0_ffn_sw3)], axis=2),
        "sw2": chunked(L0_ffn_sw2),
        "moe0": np.concatenate([per_expert(L0_ffn_w1), per_expert(L0_ffn_w3), per_expert(L0_ffn_w2)], axis=2),
        "wgnn": np.concatenate([chunked(L1_gnn_W_sa), chunked(L1_gnn_W_gcnb)], axis=2),
        "wsaT": chunked(np.asarray(L1_gnn_W_sa).T),
        "acol": chunked(np.asarray(L1_gnn_a_sa).reshape(2, D).T),
        "wab": chunked(columns),
        "bab": np.concatenate([np.asarray(L1_gnn_ba), np.asarray(L1_gnn_bb)]),
        "bgcn": L1_gnn_b_gcnb,
        "wg1": chunked(L1_ffn_Wg),
        "w1": per_expert(L1_ffn_W1),
        "w2": per_expert(L1_ffn_W2),
        "b1": np.asarray(L1_ffn_b1).reshape(E1, DC, P).transpose(2, 0, 1),
        "b2": L1_ffn_b2,
        "gamma": L1_ffn_gamma,
        "beta": L1_ffn_beta,
    }
    arrays = {name: np.ascontiguousarray(a) for name, a in arrays.items()}
    nc = bacc.Bacc("TRN2", target_bir_lowering=False, num_devices=1)
    args = [nc.dram_tensor("in_" + name, a.shape, mybir.dt.from_np(a.dtype), kind="ExternalInput").ap() for name, a in arrays.items()]
    out = nc.dram_tensor("out_x", (N, D), F32, kind="ExternalOutput").ap()
    build(nc, *args, out)
    result = run(nc, [{"in_" + name: a for name, a in arrays.items()}], core_ids=[0])
    return result.results[0]["out_x"]
```

```python
from contextlib import ExitStack

import concourse.bass as bass
from concourse import mybir

P = 128
N = 2048
D = 256
NT = N // P
DC = D // P
E0, H0, CAP = 64, 128, 512
E1, H1 = 8, 256
TOPK = 2
ROUTE_SCALE = 2.5
EPS = 1e-5
PAIRS = N * TOPK
U = 4
T0 = -(-(PAIRS // P + E0 - 1) // U) * U
T1 = -(-(PAIRS // P + E1 - 1) // U) * U
MAIN = E0
DROPPED = float(2 ** 22)
DA = D + 2

F32, BF16, I32, U32 = mybir.dt.float32, mybir.dt.bfloat16, mybir.dt.int32, mybir.dt.uint32
ALU, ACT = mybir.AluOpType, mybir.ActivationFunctionType
X = mybir.AxisListType.X


class Chain:

    def __init__(self, eng, sem):
        self.eng, self.sem, self.base, self.n, self.per = eng, sem, 0, 0, None

    def link(self, ins):
        self.n += 1
        ins.then_inc(self.sem, 1)
        self.eng.wait_ge(self.sem, self.base + self.n)

    def enter(self, turn, per):
        self.start, self.per = self.base + self.n, per
        self.base, self.n = self.start + (turn - 1) * per, 0

    def leave(self, turns):
        assert self.n == self.per, (self.n, self.per)
        self.base, self.n, self.per = self.start + (turns - 1) * self.per, 0, None


def rolled(eng, turns, body, chain=None, per=0):
    body(0)
    with eng.Fori(1, turns) as i:
        if chain:
            chain.enter(i, per)
        body(i)
        if chain:
            chain.leave(turns)


def wait(eng, sem, value):
    if not isinstance(value, int) or value > 0:
        eng.wait_ge(sem, value)


def if_more(eng, tiles, rest, sems):
    n = eng.value_load(tiles, min_val=0, max_val=T0)
    with eng.If(n > MAIN):
        rest()
    with eng.Else():
        for signal, value in sems:
            eng.sem_inc(signal, value)


def build(nc, x, adjb, gate, sw13, sw2, moe0, wgnn, wsaT, acol, wab, bab, bgcn, wg1, w1, w2, b1, b2, gamma, beta, out):
    ctx = ExitStack()
    with ctx:
        def sb(name, shape, dt=F32):
            return ctx.enter_context(nc.sbuf_tensor(name, shape, dt))

        def sem(name):
            return ctx.enter_context(nc.semaphore(name))

        def dram(name, shape, dt=F32):
            return nc.dram_tensor(name, shape, dt, kind="Internal").ap()

        xn_dram = [dram("xn0_dram", (N, D)), dram("xn1_dram", (N, D))]
        TT = [T0, T1]
        table = [dram("table0", (P * T0, 1), I32), dram("table1", (P * T1, 1), I32)]
        y_dram = [dram("y0_dram", (T0 * P, D)), dram("y1_dram", (T1 * P, D))]

        xs = sb("xs", [P, NT, D])
        rowsP = sb("rowsP", [P, NT, DA])
        rowsQ = sb("rowsQ", [P, NT, DA])
        xT = sb("xT", [P, DC, N])
        adj_buf = sb("adj_buf", [P, 2, N])
        inc_buf = sb("inc_buf", [P, 2, N])
        mask = sb("mask", [P, 2, N], BF16)
        negs = sb("negs", [P, N])
        slbc = sb("slbc", [P, N])
        w1_sb = sb("w1_sb", [P, E1, DC * H1])
        w2_sb = sb("w2_sb", [P, E1, DC * D])
        wm = sb("wm", [P, U, 3 * D])
        xg = sb("xg", [P, U, D])
        y_sb = sb("y_sb", [P, U, D])
        xn_t = sb("xn_t", [P, 2, D])
        xT_t = sb("xT_t", [P, 2, DC, P])
        g_t = sb("g_t", [P, 2, DC, P])
        th = sb("th", [P, 2, D])
        av = sb("av", [P, 2, D])
        w1_rows = w1_sb[:, :, :].rearrange("p e n -> p (e n)")
        adj4 = [adj_buf[:, 0, :], adj_buf[:, 1, :], w1_rows[:, 0:N], w1_rows[:, N:2 * N]]
        w1_t = wm[:, :, :].rearrange("p u n -> p (u n)")[:, 0:2 * DC * H1].rearrange("p (a n) -> p a n", a=2)
        gate_sb = sb("gate_sb", [P, DC, E0])
        sw13_sb = sb("sw13_sb", [P, DC, 2 * D])
        sw2_sb = sb("sw2_sb", [P, DC, D])
        wc_sb = sb("wc_sb", [P, DC, 2 * DA])
        wv_sb = sb("wv_sb", [P, DC, 2])
        wsaT_sb = sb("wsaT_sb", [P, DC, D])
        acol_sb = sb("acol_sb", [P, DC, 2])
        wab_sb = sb("wab_sb", [P, DC, 4])
        slw = sb("slw", [P, DC, P])
        bab_sb = sb("bab_sb", [P, 2])
        bgcn_sb = sb("bgcn_sb", [P, D])
        wg1_sb = sb("wg1_sb", [P, DC, E1])
        b1_sb = sb("b1_sb", [P, E1, DC])
        b2_sb = negs[0:1, :].rearrange("p (e d) -> p e d", e=E1)
        gam_bc = inc_buf[:, 0, :].rearrange("p (e d) -> p e d", e=E1)
        bet_bc = inc_buf[:, 1, :].rearrange("p (e d) -> p e d", e=E1)
        sg = mask[:, :, :].rearrange("p a n -> p (a n)").bitcast(F32).rearrange("p (h n) -> p h n", h=4)[:, 0:2, :]
        sth = negs[:, 0:1024].rearrange("p (h n) -> p h n", h=2)
        sav = negs[:, 1024:2048].rearrange("p (h n) -> p h n", h=2)
        ident = sb("ident", [P, P])
        ones_f = sb("ones_f", [1, P])
        ones_b = sb("ones_b", [P, P], BF16)
        tri_b = sb("tri_b", [P, P], BF16)
        iota_e = sb("iota_e", [P, E0])
        tok = sb("tok", [P, NT], I32)
        ones_e = sb("ones_e", [P, E0])
        tile_no = sb("tile_no", [P, 1])
        eps_sb = sb("eps_sb", [P, 1])
        st6 = sb("st6", [P, NT, 6])
        st6l = sb("st6l", [P, 2, 6])
        mvl = sb("mvl", [P, 2, 2])
        mv = sb("mv", [P, NT, 2])
        rstd = sb("rstd", [P, NT])
        nrm = sb("nrm", [P, 2, P])
        rden = sb("rden", [P, 2])
        srn = sb("srn", [P, NT])
        vab = sb("vab", [P, NT, 2])
        att = sb("att", [P, 2, 4])
        spare = rowsQ[:, :, :].rearrange("p t d -> p (t d)")
        lg, sel, rt1 = (spare[:, k * NT * E0:(k + 1) * NT * E0].rearrange("p (t e) -> p t e", e=E0) for k in range(3))
        mx8 = sb("mx8", [P, NT, 8])
        ix8 = sb("ix8", [P, NT, 8], U32)
        ixf = sb("ixf", [P, NT, TOPK])
        onehot = slbc[:, :].rearrange("p (k t e) -> p k t e", k=TOPK, e=E0)
        spare_b = spare[:, 3 * NT * E0:NT * DA].bitcast(BF16)
        cnt = spare_b[:, 0:NT * E0].rearrange("p (t e) -> p t e", e=E0)
        pre = spare_b[:, NT * E0:(2 * NT + 1) * E0].rearrange("p (t e) -> p t e", e=E0)
        tot = sb("tot", [P, 4, E0])
        toti = sb("toti", [P, E0], I32)
        slot = sb("slot", [P, TOPK, NT])
        slot_i = sb("slot_i", [P, TOPK, NT], I32)
        sp_i = sb("sp_i", [P, TOPK, NT], I32)
        sp_f = sb("sp_f", [P, TOPK, NT])
        sq_f = sb("sq_f", [P, TOPK, NT])
        addr = sb("addr", [P, TOPK, NT], I32)
        back = sb("back", [P, TOPK, NT], I32)
        wts = sb("wts", [P, TOPK, NT])
        ws = sb("ws", [P, 4, NT])
        et_f = sb("et_f", [P, 1])
        et_i = sb("et_i", [P, 1], I32)
        et_junk = sb("et_junk", [P, E0])
        et_row = [sb("et_row0", [1, T0], I32), sb("et_row1", [1, T1], I32)]
        tiles_i = sb("tiles_i", [1, 1], I32)
        tab = [sb("tab0", [P, T0], I32), sb("tab1", [P, T1], I32)]
        idx_t = sb("idx_t", [P, U, 1], I32)
        zero_i = sb("zero_i", [P, T0], I32)

        bank = [ctx.enter_context(nc.psum_tensor(f"bank{i}", [P, 512], F32)) for i in range(8)]

        names = """fill_ready filled const_in zero_in consts mask_ready count_done nrm_ready head_ready inc_ready adj_free prod_done x1_done
            dve pool_ch stats_ready rstd_ready ln_ready tr_done xts_ready xT_ready proj_done gnn_in
            lg_ready cnt_ready pos_done rt_ready addr_ready scat tabled et_in sh_h sh_t sh_g sh_y sh_x
            w0_ready slw_ready slbc_done slbc_ready e_neg e_exp e_ready pa_done pe_done at_z at_t o_ready o_t x3_done
            out_done gb_in w12_in pool_passed waits_passed wcol_ready sc_ready proj_used w_in""".split()
        s = {n: sem(n) for n in names}
        x_in = [sem(f"x_in{i}") for i in range(4)]
        adj4_in = [sem(f"adj4_in{i}") for i in range(4)]
        adj_in = [sem(f"adj_in{i}") for i in range(2)]
        xn_out = [sem(f"xn_out{i}") for i in range(2)]
        m = [{n: sem(f"{n}_{l}") for n in "idx_ready tr_done x_ready h_done th_ready g_ready y_done y_ready wt_ready var_ready sd_ready".split()}
             for l in range(2)]
        xg_in = [sem(f"xg_in{i}") for i in range(U)]
        xg_more = [sem(f"xg_more{i}") for i in range(U)]
        wm_in = [sem(f"wm_in{i}") for i in range(U)]
        wm_more = [sem(f"wm_more{i}") for i in range(U)]
        y_more = [sem(f"y_more{i}") for i in range(U)]
        y_out = [sem(f"y_out{i}") for i in range(U)]
        back_in = [sem(f"back_in{i}") for i in range(U)]
        back_used = sem("back_used")

        block = ctx.enter_context(nc.Block())
        tiled = [a.rearrange("(t p) d -> t p d", p=P) for a in xn_dram]
        y_tiled = [a.rearrange("(t p) d -> t p d", p=P) for a in y_dram]
        CONSTS = 12

        @block.sync
        def _(sp):
            def load_adj(t, dst, signal):
                sp.dma_start(dst, adjb[bass.ds(t, 1), :, :].rearrange("a p n -> (a p) n")).then_inc(signal, 16)

            load_adj(0, adj4[0], adj4_in[0])
            for q in range(4):
                sp.dma_start(xs[:, 4 * q:4 * q + 4, :], x[4 * q * P:(4 * q + 4) * P, :].rearrange("(t p) d -> p t d", p=P)).then_inc(x_in[q], 16)
            for u in range(1, 4):
                load_adj(u, adj4[u], adj4_in[u])
            for dst, src in ((gate_sb[:, :, :], gate), (sw13_sb[:, :, :], sw13), (sw2_sb[:, :, :], sw2),
                             (wc_sb[:, :, 0:D], wgnn[:, :, 0:D]), (wc_sb[:, :, DA:DA + D], wgnn[:, :, D:2 * D]),
                             (wsaT_sb[:, :, :], wsaT), (acol_sb[:, :, :], acol), (wab_sb[:, :, :], wab),
                             (bab_sb[:, :], bab.partition_broadcast(P)), (bgcn_sb[:, :], bgcn.partition_broadcast(P)),
                             (wg1_sb[:, :, :], wg1), (b1_sb[:, :, :], b1),):
                sp.dma_start(dst, src).then_inc(s["const_in"], 16)
            sp.wait_ge(s["fill_ready"], 1)
            with sp.Fori(MAIN // U, T0 // U) as i:
                sp.dma_start(y_dram[0].rearrange("(i u p) d -> i p u d", u=U, p=P)[bass.ds(i, 1), :, :, :].rearrange("a p u d -> (a p) u d"),
                             xg[:, :, :]).then_inc(s["filled"], 16)
            with sp.Fori(0, NT // 4 - 1) as i:
                for u in range(4):
                    sp.wait_ge(s["inc_ready"], 4 * i + u + 1)
                    load_adj(4 * i + u + 4, adj4[u], adj4_in[u])
            sp.wait_ge(s["zero_in"], 1)
            for l in range(2):
                sp.dma_start(table[l].rearrange("(p t) a -> p (t a)", p=P), zero_i[:, 0:TT[l]]).then_inc(s["w_in"], 16)

            def store_rows(layer):
                with sp.Fori(0, NT // 2) as i:
                    for half in range(2):
                        sp.wait_ge(s["ln_ready"], 2 * NT * layer + 2 * i + half + 1)
                        sp.dma_start(tiled[layer][bass.ds(2 * i + half, 1), :, :].rearrange("a p n -> (a p) n"), xn_t[:, half, :]).then_inc(xn_out[half], 16)

            def routed(layer):
                sp.wait_ge(s["rt_ready"], layer + 1)
                sp.dma_start(et_row[layer][0:1, :], et_i[0:TT[layer], 0:1]).then_inc(s["et_in"], 16)
                sp.wait_ge(s["scat"], 16 * TOPK * NT * (layer + 1))
                sp.dma_start(tab[layer][:, :], table[layer].rearrange("(p t) a -> p (t a)", p=P)).then_inc(s["tabled"], 16)

            store_rows(0)
            routed(0)
            sp.wait_ge(s["et_in"], 16)

            def load_w(t, u, loads):
                e = sp.value_load(et_row[0][0:1, bass.ds(t, 1)], min_val=0, max_val=E0 - 1)
                sp.dma_start(wm[:, u, :], moe0[bass.ds(e, 1), :, :].rearrange("a p n -> (a p) n")).then_inc(loads[u], 16)

            def store_y(layer, t, u, stores):
                sp.wait_ge(m[layer]["y_ready"], t + 1)
                sp.dma_start(y_tiled[layer][bass.ds(t, 1), :, :].rearrange("a p n -> (a p) n"), y_sb[:, u, :]).then_inc(stores[u], 16)

            def weights_and_results(first, n, loads, stores):
                for u in range(U):
                    if first:
                        sp.wait_ge(m[0]["y_done"], first - U + u + 1)
                    load_w(first + u, u, loads)
                with sp.Fori(0, n // U - 1) as i:
                    for u in range(U):
                        sp.wait_ge(m[0]["y_done"], first + U * i + u + 1)
                        load_w(first + U * i + u + U, u, loads)
                        store_y(0, first + U * i + u, u, stores)
                for u in range(U):
                    store_y(0, first + n - U + u, u, stores)

            weights_and_results(0, MAIN, wm_in, y_out)
            sp.wait_ge(s["rt_ready"], 1)
            if_more(sp, tiles_i[0:1, 0:1], lambda: weights_and_results(MAIN, T0 - MAIN, wm_more, y_more),
                    [])
            sp.wait_ge(s["inc_ready"], NT)
            for half in range(2):
                load_adj(half, adj_buf[:, half, :], adj_in[half])
            with sp.Fori(0, NT // 2 - 1) as i:
                for half in range(2):
                    sp.wait_ge(s["e_ready"], 2 * i + half + 1)
                    sp.wait_ge(s["pa_done"], 2 * i + half + 1)
                    load_adj(2 * i + half + 2, adj_buf[:, half, :], adj_in[half])
            sp.wait_ge(s["pe_done"], NT)
            sp.dma_start(gam_bc, gamma.rearrange("e d -> (e d)").partition_broadcast(P).rearrange("p (e d) -> p e d", e=E1)).then_inc(s["gb_in"], 16)
            sp.dma_start(bet_bc, beta.rearrange("e d -> (e d)").partition_broadcast(P).rearrange("p (e d) -> p e d", e=E1)).then_inc(s["gb_in"], 16)
            sp.dma_start(b2_sb, b2.rearrange("(a e) d -> a e d", a=1)).then_inc(s["gb_in"], 16)
            store_rows(1)
            routed(1)
            with sp.Fori(0, T1 // U) as i:
                for u in range(U):
                    store_y(1, U * i + u, u, y_out)
            with sp.Fori(0, NT) as i:
                sp.wait_ge(s["x3_done"], NT + i + 1)
                sp.dma_start(out.rearrange("(t p) d -> t p d", p=P)[bass.ds(i, 1), :, :].rearrange("a p n -> (a p) n"),
                             xs[:, bass.ds(i, 1), :].rearrange("p a d -> p (a d)")).then_inc(s["out_done"], 16)
            sp.wait_ge(s["out_done"], 16 * NT)

        @block.gpsimd
        def _(pool):
            own = Chain(pool, s["pool_ch"])
            own.link(pool.memset(ident[:, :], 0.0))
            own.link(pool.memset(tri_b[:, :], 1.0))
            own.link(pool.affine_select(out=ident[:, :], in_=ident[:, :], compare_op=ALU.not_equal, fill=1.0, base=0,
                                        pattern=[[-1, P]], channel_multiplier=1))
            own.link(pool.affine_select(out=tri_b[:, :], in_=tri_b[:, :], compare_op=ALU.is_gt, fill=0.0, base=0,
                                        pattern=[[1, P]], channel_multiplier=-1))
            own.link(pool.memset(ones_b[:, :], 1.0))
            own.link(pool.memset(ones_e[:, :], 1.0))
            own.link(pool.memset(ones_f[:, :], 1.0))
            own.link(pool.iota(iota_e[:, :], pattern=[[1, E0]], base=0, channel_multiplier=0, allow_small_or_imprecise_dtypes=True))
            own.link(pool.iota(tile_no[:, :], pattern=[[0, 1]], base=0, channel_multiplier=1, allow_small_or_imprecise_dtypes=True))
            own.link(pool.iota(tok[:, :], pattern=[[P, NT]], base=0, channel_multiplier=1))
            own.link(pool.memset(eps_sb[:, :], EPS))
            pool.memset(zero_i[:, :], 0).then_inc(s["zero_in"], 1)
            pool.wait_ge(s["zero_in"], 1)
            pool.sem_inc(s["consts"], 1)

            pool.memset(xg[:, :, :], 0.0).then_inc(s["fill_ready"], 1)

            def add_adj(t, u):
                half = u % 2
                pool.wait_ge(s["head_ready"], t + 1)
                pool.tensor_tensor(inc_buf[:, half, :], inc_buf[:, half, :], adj4[u], ALU.add).then_inc(s["inc_ready"], 1)

            with pool.Fori(0, NT // 4) as i:
                for u in range(4):
                    add_adj(4 * i + u, u)

            def scatter_tokens(layer):
                pool.wait_ge(s["w_in"], 32)
                pool.wait_ge(s["addr_ready"], layer + 1)
                for t in range(NT):
                    for k in range(TOPK):
                        pool.indirect_dma_start(out=table[layer], out_offset=bass.IndirectOffsetOnAxis(ap=addr[:, k, t:t + 1], axis=0),
                                                in_=tok[:, t:t + 1], in_offset=None,
                                                bounds_check=P * TT[layer] - 1, oob_is_err=False).then_inc(s["scat"], 16)

            def gather_rows(layer, t, u, wait, signals=xg_in):
                if wait:
                    pool.wait_ge(m[layer]["tr_done"], t - U + 1)
                pool.tensor_copy(idx_t[:, u, :], tab[layer][:, bass.ds(t, 1)]).then_inc(m[layer]["idx_ready"], 1)
                pool.wait_ge(m[layer]["idx_ready"], t + 1)
                pool.sem_inc(s["pool_passed"], 1)
                pool.indirect_dma_start(out=xg[:, u, :], out_offset=None, in_=xn_dram[layer],
                                        in_offset=bass.IndirectOffsetOnAxis(ap=idx_t[:, u, 0:1], axis=0)).then_inc(signals[u], 16)

            def gather_tiles(layer):
                pool.wait_ge(s["tabled"], 16 * (layer + 1))
                for half in range(2):
                    pool.wait_ge(xn_out[half], 16 * (NT // 2) * (layer + 1))
                for u in range(U):
                    gather_rows(layer, u, u, False)
                with pool.Fori(1, (T1 if layer else MAIN) // U) as i:
                    for u in range(U):
                        gather_rows(layer, U * i + u, u, True)

            def gather_results(layer):
                for u in range(U):
                    pool.wait_ge(y_out[u], 16 * (MAIN // U) + (16 * (T1 // U) if layer else 0))
                n = 0
                for t in range(NT):
                    for k in range(TOPK):
                        at = NT * TOPK * layer + n
                        if n >= U:
                            pool.wait_ge(back_used, at - U + 1)
                        pool.indirect_dma_start(out=xg[:, n % U, :], out_offset=None, in_=y_dram[layer],
                                                in_offset=bass.IndirectOffsetOnAxis(ap=back[:, k, t:t + 1], axis=0)).then_inc(back_in[n % U], 16)
                        n += 1

            pool.wait_ge(s["filled"], 16 * (T0 - MAIN) // U)
            scatter_tokens(0)
            gather_tiles(0)

            def gather_more():
                with pool.Fori(MAIN // U, T0 // U) as i:
                    for u in range(U):
                        gather_rows(0, U * i + u, u, True, xg_more)
                for q in y_more:
                    pool.wait_ge(q, 16 * (T0 - MAIN) // U)

            pool.wait_ge(s["rt_ready"], 1)
            pool.wait_ge(m[0]["tr_done"], MAIN)
            if_more(pool, tiles_i[0:1, 0:1], gather_more, [(m[0]["idx_ready"], T0 - MAIN), (s["pool_passed"], T0 - MAIN)])
            gather_results(0)
            scatter_tokens(1)
            gather_tiles(1)
            gather_results(1)

        @block.scalar
        def _(act):
            act.wait_ge(s["consts"], 1)

            def sqrt_var(n):
                act.wait_ge(s["stats_ready"], n)
                act.activation(rstd[:, :], mv[:, :, 1], ACT.Sqrt, bias=eps_sb[:, 0:1]).then_inc(s["rstd_ready"], 1)

            sqrt_var(1)

            def sqrt_count(t, half, reused):
                act.wait_ge(s["count_done"], t + 1)
                if reused:
                    wait(act, s["head_ready"], t - 1)
                act.activation(nrm[:, half, :], bank[half][:, 0:P], ACT.Sqrt).then_inc(s["nrm_ready"], 1)

            sqrt_count(0, 0, False)

            def sqrt_counts(i):
                sqrt_count(2 * i + 1, 1, True)
                sqrt_count(2 * i + 2, 0, True)

            rolled(act, NT // 2 - 1, sqrt_counts)
            sqrt_count(NT - 1, 1, True)

            act.wait_ge(s["inc_ready"], NT)
            act.dma_start(w1_sb[:, :, :], w1.rearrange("e p n -> p e n")).then_inc(s["w12_in"], 16)
            act.dma_start(w2_sb[:, :, :], w2.rearrange("e p n -> p e n")).then_inc(s["w12_in"], 16)
            sqrt_var(2)

            def copy_T(g, t, half, full):
                act.wait_ge(s["tr_done"], g + 2)
                wait(act, s["proj_done"], g)
                src = bank[4 + half][:, 0:D].rearrange("p (c n) -> p c n", c=DC)
                if full:
                    act.activation(xT[:, :, bass.ds(t * P, P)], src, ACT.Copy)
                act.activation(xT_t[:, half, :, :], src, ACT.Copy).then_inc(s["xts_ready"], 1)

            def copies_T(phase, full):
                def two(i):
                    for half in range(2):
                        copy_T(NT * phase + 2 * i + half, 2 * i + half, half, full)

                rolled(act, NT // 2, two)

            act.sem_inc(s["proj_done"], 1)
            copies_T(0, True)
            act.wait_ge(s["proj_done"], NT + 1)
            act.activation(lg[:, 0:NT // 2, :], bank[6][:, :].rearrange("p (t e) -> p t e", e=E0), ACT.Copy).then_inc(s["lg_ready"], 1)
            act.activation(lg[:, NT // 2:NT, :], bank[7][:, :].rearrange("p (t e) -> p t e", e=E0), ACT.Copy).then_inc(s["lg_ready"], 1)
            act.wait_ge(s["sc_ready"], 1)
            act.activation(ws[:, 0:2, :], mx8[:, :, 0:TOPK].rearrange("p t k -> p k t"), ACT.Exp, scale=-1.0).then_inc(s["w0_ready"], 1)
            for c in range(4):
                for h in range(2):
                    act.wait_ge(s["sh_h"], 2 * c + h + 1)
                    if c:
                        act.wait_ge(s["sh_g"], 2 * (c - 1) + h + 1)
                    act.activation(sth[:, h, :], bank[2 * h][:, :], ACT.Tanh, scale=0.5).then_inc(s["sh_t"], 1)

            def copy_x(layer, t, half, reused):
                act.wait_ge(m[layer]["tr_done"], t + 1)
                if reused:
                    act.wait_ge(m[layer]["h_done"], t - 1)
                act.activation(xT_t[:, half, :, :], bank[half][:, 0:D].rearrange("p (c n) -> p c n", c=DC), ACT.Copy).then_inc(m[layer]["x_ready"], 1)

            def tanh_z(t, half, reused):
                act.wait_ge(m[0]["h_done"], t + 1)
                if reused:
                    wait(act, m[0]["g_ready"], t - 1)
                act.activation(th[:, half, 0:P], bank[2 + half][:, 0:P], ACT.Tanh, scale=0.5).then_inc(m[0]["th_ready"], 1)

            def functions(first, n):
                later = first > 0
                copy_x(0, first, 0, later)
                copy_x(0, first + 1, 1, later)
                tanh_z(first, 0, later)
                turns = (n - 2) // U
                with act.Fori(0, turns) as i:
                    for j in range(U):
                        copy_x(0, first + U * i + 2 + j, j % 2, True)
                        tanh_z(first + U * i + 1 + j, (1 + j) % 2, True)
                for t in range(first + U * turns + 1, first + n):
                    if t + 1 < first + n:
                        copy_x(0, t + 1, (t + 1) % 2, True)
                    tanh_z(t, t % 2, True)

            functions(0, MAIN)
            act.wait_ge(s["rt_ready"], 1)
            act.wait_ge(m[0]["g_ready"], MAIN)
            if_more(act, tiles_i[0:1, 0:1], lambda: functions(MAIN, T0 - MAIN),
                    [(m[0]["x_ready"], T0 - MAIN), (m[0]["th_ready"], T0 - MAIN)])

            act.wait_ge(s["slw_ready"], 1)
            for c in range(DC):
                act.activation(wc_sb[:, c, D:DA], bank[6][:, 2 * c:2 * c + 2], ACT.Copy, scale=-1.0).then_inc(s["wcol_ready"], 1)
            for t in range(NT):
                act.wait_ge(s["stats_ready"], 2 + t + 1)
                act.activation(rstd[:, t:t + 1], mv[:, t, 1:2], ACT.Sqrt, bias=eps_sb[:, 0:1]).then_inc(s["rstd_ready"], 1)
                if t:
                    copy_T(NT + t - 1, t - 1, (t - 1) % 2, True)
            copy_T(2 * NT - 1, NT - 1, 1, True)
            for c in range(4):
                act.wait_ge(s["slbc_done"], c + 1)
                act.activation(slbc[:, c * 512:(c + 1) * 512], bank[6 + c % 2][:, :], ACT.Copy).then_inc(s["slbc_ready"], 1)

            def exp_e(t):
                act.wait_ge(s["e_neg"], t + 1)
                act.activation(negs[:, :], negs[:, :], ACT.Exp).then_inc(s["e_exp"], 1)

            def gates(t, half):
                act.wait_ge(s["pa_done"], t + 1)
                wait(act, s["o_ready"], t)
                for k in range(2):
                    act.activation(att[:, half, k:k + 1], bank[2 + half][:, D + k:D + k + 1], ACT.Tanh, scale=0.5,
                                   bias=vab[:, bass.ds(t, 1), k]).then_inc(s["at_t"], 1)

            def tanh_o(t, half):
                act.wait_ge(s["o_ready"], t + 1)
                wait(act, s["x3_done"], t)
                act.activation(th[:, half, :], av[:, half, :], ACT.Tanh, scale=0.5).then_inc(s["o_t"], 1)

            exp_e(0)
            exp_e(1)

            def attention_turn(i):
                for half in range(2):
                    exp_e(2 * i + half + 2)
                    gates(2 * i + half, half)
                    tanh_o(2 * i + half, half)

            rolled(act, NT // 2 - 1, attention_turn)
            for half in range(2):
                gates(NT - 2 + half, half)
                tanh_o(NT - 2 + half, half)
            sqrt_var(2 + NT + 1)
            copies_T(2, False)
            act.wait_ge(s["proj_done"], 3 * NT + 1)
            act.activation(lg[:, :, 0:E1], bank[6][:, 0:NT * E1].rearrange("p (t e) -> p t e", e=E1), ACT.Copy).then_inc(s["lg_ready"], 1)
            act.wait_ge(s["sc_ready"], 2)
            act.activation(ws[:, 1, :], ws[:, 0, :], ACT.Exp).then_inc(s["w0_ready"], 1)

            def copy_w1(t, half, reused):
                e = act.value_load(et_row[1][0:1, bass.ds(t, 1)], min_val=0, max_val=E1 - 1)
                if reused:
                    act.wait_ge(m[1]["h_done"], t - 1)
                act.activation(w1_t[:, half, :], w1_sb[:, bass.ds(e, 1), :].rearrange("p a n -> p (a n)"), ACT.Copy).then_inc(m[1]["wt_ready"], 1)

            def relu_h(t, half, reused):
                e = act.value_load(et_row[1][0:1, bass.ds(t, 1)], min_val=0, max_val=E1 - 1)
                act.wait_ge(m[1]["h_done"], t + 1)
                if reused:
                    wait(act, m[1]["y_done"], t - 1)
                for c in range(DC):
                    act.activation(g_t[:, half, c, :], bank[2 + half][:, c * P:(c + 1) * P], ACT.Relu,
                                   bias=b1_sb[:, bass.ds(e, 1), c]).then_inc(m[1]["g_ready"], 1)

            def sd_y(t, half):
                act.wait_ge(m[1]["var_ready"], t + 1)
                act.activation(att[:, half, 0:1], mvl[:, half, 1:2], ACT.Sqrt, bias=eps_sb[:, 0:1]).then_inc(m[1]["sd_ready"], 1)

            act.wait_ge(s["w12_in"], 32)
            act.wait_ge(s["const_in"], 16 * CONSTS)
            act.wait_ge(s["et_in"], 32)
            copy_w1(0, 0, False)
            copy_x(1, 0, 0, False)

            def act_step1(t, u, nxt, prev, reused):
                if nxt:
                    copy_w1(t + 1, (u + 1) % 2, reused)
                    copy_x(1, t + 1, (u + 1) % 2, reused)
                relu_h(t, u % 2, reused)
                if prev:
                    sd_y(t - 1, (u + 1) % 2)

            act_step1(0, 0, True, False, False)
            turns = (T1 - 2) // U

            def expert_turn1(i):
                for j in range(U):
                    act_step1(U * i + 1 + j, (1 + j) % U, True, True, True)

            rolled(act, turns, expert_turn1)
            for t in range(U * turns + 1, T1):
                act_step1(t, t % U, t + 1 < T1, True, True)
            sd_y(T1 - 1, (T1 - 1) % 2)

        @block.vector
        def _(dve):
            own = Chain(dve, s["dve"])
            link = own.link
            dve.sem_inc(s["tr_done"], 1)
            dve.wait_ge(s["consts"], 1)

            def normalise(dst, t):
                return dve.tensor_scalar(dst, xs[:, t, :], mv[:, t, 0:1], rstd[:, t:t + 1], ALU.subtract, ALU.mult)

            def mask_adj(t, turn, u):
                dve.wait_ge(adj4_in[u], 16 * turn + 16)
                wait(dve, s["count_done"], t - 1)
                dve.tensor_scalar(mask[:, u % 2, :], adj4[u], 0.0, None, ALU.is_gt).then_inc(s["mask_ready"], 1)

            link(dve.memset(rowsP[:, :, D:DA], 1.0))
            mask_adj(0, 0, 0)
            for t in range(NT):
                if t % 4 == 0:
                    dve.wait_ge(x_in[t // 4], 16)
                last = dve.bn_stats(st6[:, t, :], xs[:, t, :])
            link(last)
            for t in range(NT):
                last = dve.bn_aggr(mv[:, t, :], st6[:, t, :])
            last.then_inc(s["stats_ready"], 1)
            dve.wait_ge(s["rstd_ready"], 1)
            link(dve.reciprocal(rstd[:, :], rstd[:, :]))
            for t in range(NT):
                last = normalise(rowsP[:, t, 0:D], t)
            link(last)

            def heads(t, u, reused):
                half = u % 2
                dve.wait_ge(s["nrm_ready"], t + 1)
                if reused:
                    wait(dve, s["prod_done"], t - 1)
                link(dve.tensor_scalar(nrm[:, half, :], nrm[:, half, :], 1e-12, None, ALU.max))
                link(dve.reciprocal(nrm[:, half, :], nrm[:, half, :]))
                dve.scalar_tensor_tensor(out=inc_buf[:, half, :].rearrange("p (t i) -> p t i", i=P),
                                         in0=adj4[u].rearrange("p (t i) -> p t i", i=P), scalar=0.0,
                                         in1=nrm[:, half, :].unsqueeze(1).to_broadcast([P, NT, P]),
                                         op0=ALU.is_gt, op1=ALU.mult).then_inc(s["head_ready"], 1)

            def passed():
                dve.sem_inc(s["waits_passed"], 1)

            def statistics(t, half):
                passed()
                link(dve.bn_stats(st6l[:, half, :], xs[:, bass.ds(t, 1), :].rearrange("p a d -> p (a d)")))
                passed()
                link(dve.bn_aggr(mvl[:, half, :], st6l[:, half, :]))
                link(dve.tensor_copy(mv[:, bass.ds(t, 1), :].rearrange("p a d -> p (a d)"), mvl[:, half, :]))

            def finish_rows(t, half):
                dve.wait_ge(s["prod_done"], t + 1)
                link(dve.reciprocal(rden[:, half:half + 1], bank[2 + half][:, D:D + 1]))
                row = xs[:, bass.ds(t, 1), :].rearrange("p a d -> p (a d)")
                dve.scalar_tensor_tensor(out=row, in0=bank[2 + half][:, 0:D], scalar=rden[:, half:half + 1], in1=row,
                                         op0=ALU.mult, op1=ALU.add).then_inc(s["x1_done"], 1)
                dve.wait_ge(s["x1_done"], t + 1)
                statistics(t, half)

            heads(0, 0, False)
            mask_adj(1, 0, 1)
            heads(1, 1, False)
            mask_adj(2, 0, 2)

            def aggregate_turn(i):
                for j in range(4):
                    heads(4 * i + 2 + j, (2 + j) % 4, True)
                    mask_adj(4 * i + 3 + j, i + (j > 0), (3 + j) % 4)
                    finish_rows(4 * i + j, j % 2)

            rolled(dve, NT // 4 - 1, aggregate_turn, own, 24)
            for t in range(NT - 2, NT + 2):
                if t < NT:
                    heads(t, t % 4, True)
                if t + 1 < NT:
                    mask_adj(t + 1, (t + 1) // 4, (t + 1) % 4)
                finish_rows(t - 2, t % 2)
            dve.sem_inc(s["stats_ready"], 1)

            def normalise_tiles(phase, layer):
                link(dve.reciprocal(rstd[:, :], rstd[:, :]))
                def two(i):
                    for half in range(2):
                        t = 2 * i + half
                        g = NT * phase + t
                        wait(dve, s["tr_done"], g)
                        wait(dve, xn_out[half], 16 * (NT // 2) * layer + 16 * i)
                        dve.tensor_scalar(xn_t[:, half, :], xs[:, bass.ds(t, 1), :].rearrange("p a d -> p (a d)"),
                                          mv[:, bass.ds(t, 1), 0], rstd[:, bass.ds(t, 1)], ALU.subtract, ALU.mult).then_inc(s["ln_ready"], 1)

                rolled(dve, NT // 2, two)

            dve.wait_ge(s["rstd_ready"], 2)
            normalise_tiles(0, 0)

            def route(layer):
                E, T = (E0, T0) if layer == 0 else (E1, T1)
                logit = lg[:, :, 0:E]
                oh = onehot[:, :, :, 0:E]
                dve.wait_ge(s["lg_ready"], 3 if layer else 2)
                for t in range(NT):
                    last = dve.max(mx8[:, t, :], logit[:, t, :])
                link(last)
                if layer:
                    link(dve.tensor_tensor(ws[:, 0, :], mx8[:, :, 1], mx8[:, :, 0], ALU.subtract))
                dve.sem_inc(s["sc_ready"], 1)
                for t in range(NT):
                    last = dve.max_index(ix8[:, t, :], mx8[:, t, :], logit[:, t, :])
                link(last)
                link(dve.tensor_copy(ixf[:, :, :], ix8[:, :, 0:TOPK]))
                for k in range(TOPK):
                    last = dve.tensor_tensor(oh[:, k], iota_e[:, 0:E].unsqueeze(1).to_broadcast([P, NT, E]),
                                             ixf[:, :, k:k + 1].to_broadcast([P, NT, E]), ALU.is_equal)
                link(last)
                link(dve.memset(pre[:, 0, 0:E], 0.0))
                link(dve.tensor_tensor(cnt[:, :, 0:E], oh[:, 0], oh[:, 1], ALU.add))
                for t in range(NT):
                    link(dve.tensor_tensor(pre[:, t + 1, 0:E], pre[:, t, 0:E], cnt[:, t, 0:E], ALU.add))
                dve.sem_inc(s["cnt_ready"], 1)
                dve.wait_ge(s["w0_ready"], layer + 1)
                if layer == 0:
                    link(dve.tensor_scalar(ws[:, 0:2, :], ws[:, 0:2, :], 1.0, None, ALU.add))
                    link(dve.reciprocal(ws[:, 0:2, :], ws[:, 0:2, :]))
                    link(dve.tensor_tensor(ws[:, 2, :], ws[:, 0, :], ws[:, 1, :], ALU.add))
                    link(dve.tensor_scalar(ws[:, 2, :], ws[:, 2, :], 1e-20, None, ALU.add))
                    link(dve.reciprocal(ws[:, 3, :], ws[:, 2, :]))
                    for k in range(TOPK):
                        last = dve.scalar_tensor_tensor(out=wts[:, k, :], in0=ws[:, k, :], scalar=ROUTE_SCALE, in1=ws[:, 3, :], op0=ALU.mult, op1=ALU.mult)
                    link(last)
                else:
                    link(dve.tensor_scalar(ws[:, 2, :], ws[:, 1, :], 1.0, None, ALU.add))
                    link(dve.reciprocal(wts[:, 0, :], ws[:, 2, :]))
                    link(dve.tensor_tensor(wts[:, 1, :], wts[:, 0, :], ws[:, 1, :], ALU.mult))
                dve.wait_ge(s["pos_done"], layer + 1)
                tt = bank[5][:, 256:256 + E]
                if layer == 0:
                    link(dve.tensor_scalar(tot[:, 0, 0:E], tt, float(CAP), float(P - 1), ALU.min, ALU.add))
                else:
                    link(dve.tensor_scalar(tot[:, 0, 0:E], tt, float(P - 1), None, ALU.add))
                link(dve.tensor_copy(toti[:, 0:E], tot[:, 0, 0:E]))
                link(dve.tensor_scalar(toti[:, 0:E], toti[:, 0:E], 7, None, ALU.arith_shift_right))
                link(dve.tensor_copy(tot[:, 1, 0:E], toti[:, 0:E]))
                link(dve.tensor_tensor_scan(tot[:, 2, 0:E], ones_e[:, 0:E], tot[:, 1, 0:E], 0.0, ALU.mult, ALU.add))
                link(dve.tensor_tensor(tot[:, 3, 0:E], tot[:, 2, 0:E], tot[:, 1, 0:E], ALU.subtract))
                link(dve.tensor_scalar(et_junk[:, 0:E], tot[:, 2, 0:E], tile_no[:, 0:1], None, ALU.is_le))
                link(dve.reduce_sum(et_f[:, :], et_junk[:, 0:E], X))
                link(dve.tensor_scalar(et_f[:, :], et_f[:, :], float(E - 1), None, ALU.min))
                if layer == 0:
                    link(dve.tensor_copy(tiles_i[0:1, :], tot[0:1, 2, E - 1:E]))
                dve.tensor_copy(et_i[:, :], et_f[:, :]).then_inc(s["rt_ready"], 1)
                if layer == 0:
                    for b in range(2):
                        pos = bank[6 + b][:, :].rearrange("p (t e) -> p t e", e=E)
                        h = slice(b * NT // 2, (b + 1) * NT // 2)
                        last = dve.tensor_scalar(rt1[:, h, :], pos, float(CAP), DROPPED, ALU.is_ge, ALU.mult)
                    link(last)
                    for b in range(2):
                        pos = bank[6 + b][:, :].rearrange("p (t e) -> p t e", e=E)
                        h = slice(b * NT // 2, (b + 1) * NT // 2)
                        last = dve.tensor_tensor(rt1[:, h, :], rt1[:, h, :], pos, ALU.add)
                    link(last)
                else:
                    link(dve.tensor_copy(rt1[:, :, 0:E], bank[7][:, 0:NT * E].rearrange("p (t e) -> p t e", e=E)))
                link(dve.scalar_tensor_tensor(out=rt1[:, :, 0:E], in0=tot[:, 3, 0:E].unsqueeze(1).to_broadcast([P, NT, E]), scalar=float(P),
                                              in1=rt1[:, :, 0:E], op0=ALU.mult, op1=ALU.add))
                for k in range(TOPK):
                    link(dve.tensor_tensor(sel[:, :, 0:E], oh[:, k], rt1[:, :, 0:E], ALU.mult))
                    link(dve.reduce_sum(slot[:, k, :], sel[:, :, 0:E], X))
                link(dve.tensor_copy(slot_i[:, :, :], slot[:, :, :]))
                link(dve.tensor_scalar(sp_i[:, :, :], slot_i[:, :, :], P - 1, None, ALU.bitwise_and))
                link(dve.tensor_copy(sp_f[:, :, :], sp_i[:, :, :]))
                link(dve.tensor_scalar(sp_i[:, :, :], slot_i[:, :, :], 7, None, ALU.arith_shift_right))
                link(dve.tensor_copy(sq_f[:, :, :], sp_i[:, :, :]))
                link(dve.scalar_tensor_tensor(out=sp_f[:, :, :], in0=sp_f[:, :, :], scalar=float(T), in1=sq_f[:, :, :], op0=ALU.mult, op1=ALU.add))
                dve.tensor_copy(addr[:, :, :], sp_f[:, :, :]).then_inc(s["addr_ready"], 1)
                if layer == 0:
                    link(dve.tensor_scalar(sq_f[:, :, :], slot[:, :, :], DROPPED, None, ALU.is_lt))
                    link(dve.tensor_tensor(slot[:, :, :], slot[:, :, :], sq_f[:, :, :], ALU.mult))
                    link(dve.tensor_tensor(wts[:, :, :], wts[:, :, :], sq_f[:, :, :], ALU.mult))
                link(dve.tensor_copy(back[:, :, :], slot[:, :, :]))

            route(0)

            for c in range(4):
                for h in range(2):
                    dve.wait_ge(s["sh_t"], 2 * c + h + 1)
                    link(dve.scalar_tensor_tensor(out=sav[:, h, :], in0=sth[:, h, :], scalar=1.0, in1=bank[2 * h][:, :], op0=ALU.add, op1=ALU.mult))
                    if c:
                        dve.wait_ge(s["sh_y"], 4 * c)
                    dve.scalar_tensor_tensor(out=sg[:, h, :], in0=bank[2 * h + 1][:, :], scalar=0.5, in1=sav[:, h, :],
                                             op0=ALU.mult, op1=ALU.mult).then_inc(s["sh_g"], 1)
                for j in range(4):
                    t = 4 * c + j
                    dve.wait_ge(s["sh_y"], t + 1)
                    dve.tensor_tensor(xs[:, t, :], bank[4 + j % 2][:, 0:D], xs[:, t, :], ALU.add).then_inc(s["sh_x"], 1)

            def gate_h(t, half, reused):
                dve.wait_ge(m[0]["th_ready"], t + 1)
                link(dve.scalar_tensor_tensor(out=av[:, half, 0:P], in0=th[:, half, 0:P], scalar=1.0, in1=bank[2 + half][:, 0:P], op0=ALU.add, op1=ALU.mult))
                if reused:
                    wait(dve, m[0]["y_done"], t - 1)
                dve.scalar_tensor_tensor(out=g_t[:, half, 0, :], in0=bank[2 + half][:, P:2 * P], scalar=0.5, in1=av[:, half, 0:P],
                                         op0=ALU.mult, op1=ALU.mult).then_inc(m[0]["g_ready"], 1)

            def copy_y(stores, t, u, turn):
                dve.wait_ge(m[0]["y_done"], t + 1)
                wait(dve, stores[u], 16 * turn)
                dve.tensor_copy(y_sb[:, u, :], bank[4 + u % 2][:, 0:D]).then_inc(m[0]["y_ready"], 1)

            def gated(first, n):
                stores = y_more if first else y_out
                gate_h(first, 0, first > 0)
                gate_h(first + 1, 1, first > 0)
                copy_y(stores, first, 0, 0)
                gate_h(first + 2, 0, True)
                copy_y(stores, first + 1, 1, 0)
                turns = (n - 4) // U
                def step(t, u, turn):
                    gate_h(t, u % 2, True)
                    copy_y(stores, t - 1, (u - 1) % U, turn)

                def some(i):
                    for j in range(U):
                        step(first + U * i + 3 + j, (3 + j) % U, i + (j >= 2))

                rolled(dve, turns, some, own, U)
                for t in range(first + U * turns + 3, first + n):
                    gate_h(t, t % 2, True)
                    copy_y(stores, t - 1, (t - 1) % U, (t - 1 - first) // U)
                copy_y(stores, first + n - 1, (n - 1) % U, (n - 1) // U)

            gated(0, MAIN)
            dve.wait_ge(s["rt_ready"], 1)
            for q in y_out:
                dve.wait_ge(q, 16 * MAIN // U)
            if_more(dve, tiles_i[0:1, 0:1], lambda: gated(MAIN, T0 - MAIN),
                    [(m[0]["g_ready"], T0 - MAIN), (m[0]["y_ready"], T0 - MAIN), (s["dve"], T0 - MAIN)])

            dve.wait_ge(s["const_in"], 16 * CONSTS)
            dve.wait_ge(s["wcol_ready"], DC)
            link(dve.tensor_copy(slw[:, :, :], wc_sb[:, :, D:D + 1].to_broadcast([P, DC, P])))
            link(dve.tensor_copy(wc_sb[:, :, DA + D:2 * DA], wab_sb[:, :, 0:2]))
            link(dve.tensor_copy(wv_sb[:, :, :], wab_sb[:, :, 2:4]))
            dve.sem_inc(s["gnn_in"], 1)

            def combine(layer, t):
                for k in range(TOPK):
                    n = TOPK * t + k
                    dve.wait_ge(back_in[n % U], 16 * (n // U + 1) + 16 * (TOPK * NT // U) * layer)
                    dve.scalar_tensor_tensor(out=xs[:, t, :], in0=xg[:, n % U, :], scalar=wts[:, k, t:t + 1], in1=xs[:, t, :],
                                             op0=ALU.mult, op1=ALU.add).then_inc(back_used, 1)
                    dve.wait_ge(back_used, NT * TOPK * layer + n + 1)

            def norm_t(t):
                dve.wait_ge(s["rstd_ready"], 2 + t + 1)
                link(dve.reciprocal(rstd[:, t:t + 1], rstd[:, t:t + 1]))
                dve.wait_ge(s["tr_done"], NT + t)
                dve.wait_ge(xn_out[t % 2], 16 * (NT // 2))
                normalise(xn_t[:, t % 2, :], t).then_inc(s["ln_ready"], 1)

            def keep_proj(t):
                half = t % 2
                dve.wait_ge(s["proj_done"], 1 + NT + t + 1)
                dve.tensor_copy(rowsP[:, t, 0:D], bank[half][:, 0:D])
                dve.tensor_copy(srn[:, t:t + 1], bank[half][:, D + 1:D + 2])
                dve.tensor_copy(rowsQ[:, t, :], bank[2 + half][:, 0:DA])
                link(dve.tensor_tensor(vab[:, t, :], bank[2 + half][:, DA:DA + 2], bab_sb[:, :], ALU.add))
                dve.tensor_scalar(vab[:, t, :], vab[:, t, :], 0.5, None, ALU.mult).then_inc(s["proj_used"], 1)

            for t in range(NT):
                combine(0, t)
                link(dve.bn_stats(st6[:, t, :], xs[:, t, :]))
                dve.bn_aggr(mv[:, t, :], st6[:, t, :]).then_inc(s["stats_ready"], 1)
                if t >= 1:
                    norm_t(t - 1)
                if t >= 3:
                    keep_proj(t - 3)
            norm_t(NT - 1)
            for t in range(NT - 3, NT):
                keep_proj(t)

            def exponents(t):
                v = lambda a: a.rearrange("p (t i) -> p t i", i=P)
                link(dve.tensor_tensor(v(negs[:, :]), slbc[:, bass.ds(t * P, P)].unsqueeze(1).to_broadcast([P, NT, P]),
                                       srn[:, :].unsqueeze(2).to_broadcast([P, NT, P]), ALU.add))
                dve.scalar_tensor_tensor(out=negs[:, :], in0=negs[:, :], scalar=0.01, in1=negs[:, :], op0=ALU.mult, op1=ALU.min).then_inc(s["e_neg"], 1)

            def attention(t, turn, half, reused):
                dve.wait_ge(s["e_exp"], t + 1)
                dve.wait_ge(adj_in[half], 16 * turn + 16)
                if reused:
                    dve.wait_ge(s["pe_done"], t - 1)
                dve.scalar_tensor_tensor(out=inc_buf[:, half, :], in0=adj_buf[:, half, :], scalar=0.0, in1=negs[:, :],
                                         op0=ALU.not_equal, op1=ALU.mult).then_inc(s["e_ready"], 1)
                dve.wait_ge(s["e_ready"], t + 1)

            def finish_nodes(t, half):
                dve.wait_ge(s["pe_done"], t + 1)
                dve.wait_ge(s["at_t"], 2 * t + 2)
                link(dve.tensor_scalar(att[:, half, 0:2], att[:, half, 0:2], 0.5, 0.5, ALU.mult, ALU.add))
                link(dve.tensor_scalar(att[:, half, 2:3], bank[half][:, D:D + 1], 1e-5, None, ALU.add))
                link(dve.reciprocal(att[:, half, 3:4], att[:, half, 2:3]))
                link(dve.tensor_tensor(att[:, half, 2:3], att[:, half, 3:4], att[:, half, 0:1], ALU.mult))
                link(dve.tensor_tensor(av[:, half, :], bank[2 + half][:, 0:D], bgcn_sb[:, :], ALU.add))
                link(dve.tensor_scalar(av[:, half, :], av[:, half, :], att[:, half, 1:2], None, ALU.mult))
                dve.scalar_tensor_tensor(out=av[:, half, :], in0=bank[half][:, 0:D], scalar=att[:, half, 2:3], in1=av[:, half, :],
                                         op0=ALU.mult, op1=ALU.add).then_inc(s["o_ready"], 1)

            def add_nodes(t, half):
                dve.wait_ge(s["o_t"], t + 1)
                row = xs[:, bass.ds(t, 1), :].rearrange("p a d -> p (a d)")
                link(dve.scalar_tensor_tensor(out=row, in0=th[:, half, :], scalar=0.5, in1=row, op0=ALU.mult, op1=ALU.add))
                dve.tensor_scalar(row, row, 0.5, None, ALU.add).then_inc(s["x3_done"], 1)
                dve.wait_ge(s["x3_done"], t + 1)
                statistics(t, half)

            dve.wait_ge(s["slbc_ready"], 4)
            exponents(0)
            attention(0, 0, 0, False)
            exponents(1)
            attention(1, 0, 1, False)
            exponents(2)
            finish_nodes(0, 0)

            def attention_turn(i, last=False):
                for j, half in ((1, 1), (2, 0)):
                    attention(2 * i + j + 1, i + 1, 1 - half, True)
                    if not last or j == 1:
                        exponents(2 * i + j + 2)
                    add_nodes(2 * i + j - 1, 1 - half)
                    finish_nodes(2 * i + j, half)

            rolled(dve, NT // 2 - 2, attention_turn, own, 22)
            attention_turn(NT // 2 - 2, last=True)
            add_nodes(NT - 2, 0)
            finish_nodes(NT - 1, 1)
            add_nodes(NT - 1, 1)
            dve.sem_inc(s["stats_ready"], 1)
            dve.wait_ge(s["rstd_ready"], 2 + NT + 1)
            normalise_tiles(2, 1)
            route(1)

            def stats_y(t, u):
                half = u % 2
                dve.wait_ge(m[1]["y_done"], t + 1)
                passed()
                link(dve.bn_stats(st6l[:, half, :], bank[4 + u][:, 0:D]))
                passed()
                dve.bn_aggr(mvl[:, half, :], st6l[:, half, :]).then_inc(m[1]["var_ready"], 1)

            def norm_y(t, u, turn):
                half = u % 2
                e = dve.value_load(et_row[1][0:1, bass.ds(t, 1)], min_val=0, max_val=E1 - 1)
                dve.wait_ge(m[1]["sd_ready"], t + 1)
                link(dve.reciprocal(att[:, half, 1:2], att[:, half, 0:1]))
                dve.wait_ge(y_out[u], 16 * (MAIN // U) + 16 * turn)
                link(dve.tensor_scalar(y_sb[:, u, :], bank[4 + u][:, 0:D], mvl[:, half, 0:1], att[:, half, 1:2], ALU.subtract, ALU.mult))
                link(dve.tensor_tensor(y_sb[:, u, :], y_sb[:, u, :], gam_bc[:, bass.ds(e, 1), :].rearrange("p a d -> p (a d)"), ALU.mult))
                dve.tensor_tensor(y_sb[:, u, :], y_sb[:, u, :], bet_bc[:, bass.ds(e, 1), :].rearrange("p a d -> p (a d)"), ALU.add).then_inc(m[1]["y_ready"], 1)

            dve.wait_ge(s["et_in"], 32)
            dve.wait_ge(s["gb_in"], 48)
            stats_y(0, 0)
            turns = (T1 - 2) // U

            def expert_turn1(i):
                for j in range(U):
                    stats_y(U * i + 1 + j, (1 + j) % U)
                    norm_y(U * i + j, j, i)

            rolled(dve, turns, expert_turn1, own, 4 * U)
            for t in range(U * turns + 1, T1):
                stats_y(t, t % U)
                norm_y(t - 1, (t - 1) % U, (t - 1) // U)
            norm_y(T1 - 1, (T1 - 1) % U, (T1 - 1) // U)
            for t in range(NT):
                combine(1, t)
                dve.sem_inc(s["x3_done"], 1)

        @block.tensor
        def _(pe):
            pe.wait_ge(s["consts"], 1)

            def count(t, half, reused):
                pe.wait_ge(s["mask_ready"], t + 1)
                if reused:
                    pe.wait_ge(s["nrm_ready"], t - 1)
                for j in range(NT):
                    last = pe.matmul(bank[half][:, 0:P], ones_b[:, :], mask[:, half, j * P:(j + 1) * P], start=(j == 0), stop=(j == NT - 1))
                last.then_inc(s["count_done"], 1)

            def product(ready, t, half, lhs, rhs, cols, dst, done):
                pe.wait_ge(ready, t + 1)
                for j in range(NT):
                    last = pe.matmul(dst[:, 0:cols], lhs[:, half, j * P:(j + 1) * P], rhs[:, j, 0:cols], start=(j == 0), stop=(j == NT - 1))
                last.then_inc(done, 1)

            def aggregate(t, half, reused):
                if reused:
                    wait(pe, s["x1_done"], t - 1)
                product(s["inc_ready"], t, half, inc_buf, rowsP, D + 1, bank[2 + half], s["prod_done"])

            count(0, 0, False)
            pe.wait_ge(s["dve"], 4)
            count(1, 1, False)
            aggregate(0, 0, False)

            def aggregate_turn(i):
                count(2 * i + 2, 0, True)
                aggregate(2 * i + 1, 1, True)
                count(2 * i + 3, 1, True)
                aggregate(2 * i + 2, 0, True)

            rolled(pe, NT // 2 - 1, aggregate_turn)
            aggregate(NT - 1, 1, True)

            def transposes(g, half):
                pe.wait_ge(s["ln_ready"], g + 1)
                for c in range(DC):
                    last = pe.transpose(bank[4 + half][:, c * P:(c + 1) * P], xn_t[:, half, c * P:(c + 1) * P], ident[:, :])
                last.then_inc(s["tr_done"], 1)

            def logits(phase, t, half, w, dst):
                g = NT * phase + t
                pe.wait_ge(s["xts_ready"], g + 1)
                for c in range(DC):
                    last = pe.matmul(dst, xT_t[:, half, c, :], w[:, c, :], start=(c == 0), stop=(c == DC - 1))
                last.then_inc(s["proj_done"], 1)

            pe.wait_ge(s["const_in"], 16 * CONSTS)

            def route_logits(phase, w, E, banks):
                per = NT // len(banks)
                for b, bk in enumerate(banks):
                    with pe.Fori(0, per // 2) as i:
                        for half in range(2):
                            t = 2 * i + half + per * b
                            transposes(NT * phase + t, half)
                            logits(phase, t, half, w, bk[:, bass.ds((2 * i + half) * E, E)])

            def positions(layer, E, banks, total):
                pe.wait_ge(s["cnt_ready"], layer + 1)
                per = NT // len(banks)
                for b, bk in enumerate(banks):
                    for j in range(per):
                        t = b * per + j
                        pe.matmul(bk[:, j * E:(j + 1) * E], tri_b[:, :], cnt[:, t, 0:E], start=True, stop=False)
                        pe.matmul(bk[:, j * E:(j + 1) * E], ones_b[:, :], pre[:, t, 0:E], start=False, stop=True)
                pe.matmul(total[:, 256:256 + E], ones_b[:, :], pre[:, NT, 0:E], start=True, stop=True).then_inc(s["pos_done"], 1)

            route_logits(0, gate_sb, E0, [bank[6], bank[7]])
            pe.wait_ge(s["lg_ready"], 2)
            def shared_hidden(c, h):
                if c:
                    pe.wait_ge(s["sh_g"], 2 * (c - 1) + h + 1)
                for v in range(2):
                    for k in range(DC):
                        last = pe.matmul(bank[2 * h + v][:, :], sw13_sb[:, k, v * D + h * P:v * D + (h + 1) * P], xT[:, k, c * 512:(c + 1) * 512],
                                         start=(k == 0), stop=(k == DC - 1))
                last.then_inc(s["sh_h"], 1)

            for h in range(2):
                shared_hidden(0, h)
            positions(0, E0, [bank[6], bank[7]], bank[5])
            for c in range(4):
                for h in range(2):
                    if c:
                        shared_hidden(c, h)
                pe.wait_ge(s["sh_g"], 2 * c + 2)
                for j in range(4):
                    t = 4 * c + j
                    if t >= 2:
                        pe.wait_ge(s["sh_x"], t - 1)
                    for k in range(DC):
                        last = pe.matmul(bank[4 + j % 2][:, 0:D], sg[:, k, j * P:(j + 1) * P], sw2_sb[:, k, :], start=(k == 0), stop=(k == DC - 1))
                    last.then_inc(s["sh_y"], 1)
            pe.wait_ge(s["sh_x"], NT)

            def tr_x(layer, loads, t, u, turn, reused):
                pe.wait_ge(loads[u], 16 * turn + 16)
                if reused:
                    wait(pe, m[layer]["x_ready"], t - 1)
                for c in range(DC):
                    last = pe.transpose(bank[u % 2][:, c * P:(c + 1) * P], xg[:, u, c * P:(c + 1) * P], ident[:, :])
                last.then_inc(m[layer]["tr_done"], 1)

            def hidden0(loads, t, u, turn, reused):
                half = u % 2
                pe.wait_ge(m[0]["x_ready"], t + 1)
                pe.wait_ge(loads[u], 16 * turn + 16)
                if reused:
                    wait(pe, m[0]["g_ready"], t - 1)
                for v in range(2):
                    for k in range(DC):
                        last = pe.matmul(bank[2 + half][:, v * P:(v + 1) * P], wm[:, u, v * D + k * P:v * D + (k + 1) * P], xT_t[:, half, k, :],
                                         start=(k == 0), stop=(k == DC - 1))
                last.then_inc(m[0]["h_done"], 1)

            def down0(t, u):
                half = u % 2
                pe.wait_ge(m[0]["g_ready"], t + 1)
                if not isinstance(t, int) or t >= 2:
                    pe.wait_ge(m[0]["y_ready"], t - 1)
                pe.matmul(bank[4 + half][:, 0:D], g_t[:, half, 0, :], wm[:, u, 2 * D:3 * D], start=True, stop=True).then_inc(m[0]["y_done"], 1)

            def experts0(first, n):
                later, b = first > 0, first // U
                loads, weights = (xg_more, wm_more) if later else (xg_in, wm_in)
                tr_x(0, loads, first, 0, 0, later)
                tr_x(0, loads, first + 1, 1, 0, later)
                hidden0(weights, first, 0, 0, later)
                for j in (1, 2):
                    tr_x(0, loads, first + j + 1, j + 1, 0, True)
                    hidden0(weights, first + j, j, 0, True)
                    down0(first + j - 1, j - 1)
                turns = (n - 4) // U
                with pe.Fori(0, turns) as i:
                    for j in range(U):
                        t, u = first + U * i + 3 + j, (3 + j) % U
                        tr_x(0, loads, t + 1, (u + 1) % U, i + 1, True)
                        hidden0(weights, t, u, i + (j > 0), True)
                        down0(t - 1, (u - 1) % U)
                for t in range(first + U * turns + 3, first + n):
                    if t + 1 < first + n:
                        tr_x(0, loads, t + 1, (t + 1) % U, (t + 1) // U - b, True)
                    hidden0(weights, t, t % U, t // U - b, True)
                    down0(t - 1, (t - 1) % U)
                down0(first + n - 1, (first + n - 1) % U)

            experts0(0, MAIN)
            pe.wait_ge(s["rt_ready"], 1)
            pe.wait_ge(m[0]["y_ready"], MAIN)
            if_more(pe, tiles_i[0:1, 0:1], lambda: experts0(MAIN, T0 - MAIN),
                    [(m[0][q], T0 - MAIN) for q in ("tr_done", "h_done", "y_done")])

            for c in range(DC):
                for k in range(DC):
                    last = pe.matmul(bank[6][:, 2 * c:2 * c + 2], wsaT_sb[:, k, c * P:(c + 1) * P], acol_sb[:, k, :], start=(k == 0), stop=(k == DC - 1))
            last.then_inc(s["slw_ready"], 1)
            pe.wait_ge(s["gnn_in"], 1)
            pe.wait_ge(m[0]["y_ready"], T0)

            def project(t):
                half = t % 2
                g = NT + t
                pe.wait_ge(s["xts_ready"], g + 1)
                if t >= 2:
                    pe.wait_ge(s["proj_used"], t - 1)
                for k in range(DC):
                    pe.matmul(bank[half][:, 0:DA], xT_t[:, half, k, :], wc_sb[:, k, 0:DA], start=(k == 0), stop=(k == DC - 1))
                for k in range(DC):
                    pe.matmul(bank[2 + half][:, 0:DA], xT_t[:, half, k, :], wc_sb[:, k, DA:2 * DA], start=(k == 0), stop=(k == DC - 1))
                for k in range(DC):
                    last = pe.matmul(bank[2 + half][:, DA:DA + 2], xT_t[:, half, k, :], wv_sb[:, k, :], start=(k == 0), stop=(k == DC - 1))
                last.then_inc(s["proj_done"], 1)

            for t in range(NT):
                transposes(NT + t, t % 2)
                if t >= 1:
                    project(t - 1)
            project(NT - 1)
            for c in range(4):
                if c >= 2:
                    pe.wait_ge(s["slbc_ready"], c - 1)
                for k in range(DC):
                    last = pe.matmul(bank[6 + c % 2][:, :], slw[:, k, :], xT[:, k, c * 512:(c + 1) * 512], start=(k == 0), stop=(k == DC - 1))
                last.then_inc(s["slbc_done"], 1)
            pe.wait_ge(s["proj_used"], NT)

            def attend(t, turn, half, reused):
                if reused:
                    pe.wait_ge(s["o_ready"], t - 1)
                pe.wait_ge(adj_in[half], 16 * turn + 16)
                for j in range(NT):
                    last = pe.matmul(bank[2 + half][:, 0:DA], adj_buf[:, half, j * P:(j + 1) * P], rowsQ[:, j, :], start=(j == 0), stop=(j == NT - 1))
                last.then_inc(s["pa_done"], 1)
                product(s["e_ready"], t, half, inc_buf, rowsP, D + 1, bank[half], s["pe_done"])

            attend(0, 0, 0, False)
            attend(1, 0, 1, False)
            with pe.Fori(1, NT // 2) as i:
                for half in range(2):
                    attend(2 * i + half, i, half, True)
            route_logits(2, wg1_sb, E1, [bank[6]])
            positions(1, E1, [bank[7]], bank[5])

            def hidden1(t, u, reused):
                half = u % 2
                pe.wait_ge(m[1]["x_ready"], t + 1)
                pe.wait_ge(m[1]["wt_ready"], t + 1)
                if reused:
                    wait(pe, m[1]["g_ready"], 2 * t - 2)
                for c in range(DC):
                    for k in range(DC):
                        last = pe.matmul(bank[2 + half][:, c * P:(c + 1) * P], w1_t[:, half, k * H1 + c * P:k * H1 + (c + 1) * P], xT_t[:, half, k, :],
                                         start=(k == 0), stop=(k == DC - 1))
                last.then_inc(m[1]["h_done"], 1)

            def down1(t, u):
                half = u % 2
                e = pe.value_load(et_row[1][0:1, bass.ds(t, 1)], min_val=0, max_val=E1 - 1)
                pe.wait_ge(m[1]["g_ready"], 2 * t + 2)
                if not isinstance(t, int) or t >= U:
                    wait(pe, m[1]["y_ready"], t - U + 1)
                for k in range(DC):
                    pe.matmul(bank[4 + u][:, 0:D], g_t[:, half, k, :], w2_sb[:, bass.ds(e, 1), k * D:(k + 1) * D].rearrange("p a d -> p (a d)"), start=(k == 0), stop=False)
                pe.matmul(bank[4 + u][:, 0:D], ones_f[0:1, :], b2_sb[0:1, bass.ds(e, 1), :].rearrange("p a d -> p (a d)"), start=False, stop=True).then_inc(m[1]["y_done"], 1)

            pe.wait_ge(s["w12_in"], 32)
            pe.wait_ge(s["gb_in"], 48)
            pe.wait_ge(s["et_in"], 32)
            tr_x(1, xg_in, 0, 0, MAIN // U, False)
            tr_x(1, xg_in, 1, 1, MAIN // U, False)
            hidden1(0, 0, False)
            for t in range(1, U + 3):
                tr_x(1, xg_in, t + 1, (t + 1) % U, (MAIN + t + 1) // U, True)
                hidden1(t, t % U, True)
                down1(t - 1, (t - 1) % U)
            turns = (T1 - 4) // U - 1
            with pe.Fori(0, turns) as i:
                for j in range(U):
                    t, u = U * i + U + 3 + j, (3 + j) % U
                    tr_x(1, xg_in, t + 1, (u + 1) % U, MAIN // U + i + 2, True)
                    hidden1(t, u, True)
                    down1(t - 1, (u - 1) % U)
            for t in range(U * turns + U + 3, T1):
                if t + 1 < T1:
                    tr_x(1, xg_in, t + 1, (t + 1) % U, (MAIN + t + 1) // U, True)
                hidden1(t, t % U, True)
                down1(t - 1, (t - 1) % U)
            down1(T1 - 1, (T1 - 1) % U)


def kernel(x, adj, L0_ffn_gate_w, L0_ffn_w1, L0_ffn_w3, L0_ffn_w2, L0_ffn_sw1, L0_ffn_sw3, L0_ffn_sw2, L1_gnn_W_sa, L1_gnn_a_sa,
           L1_gnn_W_gcnb, L1_gnn_b_gcnb, L1_gnn_Wa, L1_gnn_ba, L1_gnn_Wb, L1_gnn_bb, L1_ffn_Wg, L1_ffn_W1, L1_ffn_b1, L1_ffn_W2,
           L1_ffn_b2, L1_ffn_gamma, L1_ffn_beta):
    import numpy as np
    import concourse.bacc as bacc
    from concourse.bass_utils import run_bass_kernel_spmd as run

    def chunked(w):
        w = np.asarray(w)
        return w.reshape(w.shape[0] // P, P, -1).transpose(1, 0, 2)

    def per_expert(w):
        w = np.asarray(w)
        e, k, n = w.shape
        return w.reshape(e, k // P, P, n).transpose(0, 2, 1, 3).reshape(e, P, k // P * n)

    wa, wb = np.asarray(L1_gnn_Wa), np.asarray(L1_gnn_Wb)
    columns = np.concatenate([wa[:, :D], wb[:, :D], wa[:, D:], wb[:, D:]], axis=0).T
    arrays = {
        "x": x,
        "adjb": np.asarray(adj).reshape(NT, P, NT, P).transpose(0, 3, 2, 1).reshape(NT, P, N),
        "gate": chunked(np.asarray(L0_ffn_gate_w).T),
        "sw13": np.concatenate([chunked(L0_ffn_sw1), chunked(L0_ffn_sw3)], axis=2),
        "sw2": chunked(L0_ffn_sw2),
        "moe0": np.concatenate([per_expert(L0_ffn_w1), per_expert(L0_ffn_w3), per_expert(L0_ffn_w2)], axis=2),
        "wgnn": np.concatenate([chunked(L1_gnn_W_sa), chunked(L1_gnn_W_gcnb)], axis=2),
        "wsaT": chunked(np.asarray(L1_gnn_W_sa).T),
        "acol": chunked(np.asarray(L1_gnn_a_sa).reshape(2, D).T),
        "wab": chunked(columns),
        "bab": np.concatenate([np.asarray(L1_gnn_ba), np.asarray(L1_gnn_bb)]),
        "bgcn": L1_gnn_b_gcnb,
        "wg1": chunked(L1_ffn_Wg),
        "w1": per_expert(L1_ffn_W1),
        "w2": per_expert(L1_ffn_W2),
        "b1": np.asarray(L1_ffn_b1).reshape(E1, DC, P).transpose(2, 0, 1),
        "b2": L1_ffn_b2,
        "gamma": L1_ffn_gamma,
        "beta": L1_ffn_beta,
    }
    arrays = {name: np.ascontiguousarray(a) for name, a in arrays.items()}
    nc = bacc.Bacc("TRN2", target_bir_lowering=False, num_devices=1)
    args = [nc.dram_tensor("in_" + name, a.shape, mybir.dt.from_np(a.dtype), kind="ExternalInput").ap() for name, a in arrays.items()]
    out = nc.dram_tensor("out_x", (N, D), F32, kind="ExternalOutput").ap()
    build(nc, *args, out)
    result = run(nc, [{"in_" + name: a for name, a in arrays.items()}], core_ids=[0])
    return result.results[0]["out_x"]
```

```python
from contextlib import ExitStack

import concourse.bass as bass
from concourse import mybir

P = 128
N = 2048
D = 256
NT = N // P
DC = D // P
E0, H0, CAP = 64, 128, 512
E1, H1 = 8, 256
TOPK = 2
ROUTE_SCALE = 2.5
EPS = 1e-5
PAIRS = N * TOPK
U = 4
V = 8
T0 = -(-(PAIRS // P + E0 - 1) // U) * U
T1 = PAIRS // P + E1 - 1
NOWHERE = 2.0 ** 20
MAIN = E0
DROPPED = float(2 ** 22)
DA = D + 2

F32, F16, BF16, I32, U32 = mybir.dt.float32, mybir.dt.float16, mybir.dt.bfloat16, mybir.dt.int32, mybir.dt.uint32
ALU, ACT = mybir.AluOpType, mybir.ActivationFunctionType
X = mybir.AxisListType.X


class Chain:

    def __init__(self, eng, sem):
        self.eng, self.sem, self.base, self.n, self.per = eng, sem, 0, 0, None

    def link(self, ins):
        self.n += 1
        ins.then_inc(self.sem, 1)
        self.eng.wait_ge(self.sem, self.base + self.n)

    def enter(self, turn, per):
        self.start, self.per = self.base + self.n, per
        self.base, self.n = self.start + (turn - 1) * per, 0

    def leave(self, turns):
        assert self.n == self.per, (self.n, self.per)
        self.base, self.n, self.per = self.start + (turns - 1) * self.per, 0, None


def rolled(eng, turns, body, chain=None, per=0):
    body(0)
    with eng.Fori(1, turns) as i:
        if chain:
            chain.enter(i, per)
        body(i)
        if chain:
            chain.leave(turns)


def sweep(eng, step, first, lo, hi, last, per, chain=None, links=0):
    for t in range(first, lo):
        step(t, t, 0)
    turns = (hi - lo) // per
    with eng.Fori(0, turns) as i:
        if chain:
            chain.enter(i + 1, links)
        for c in range(lo, lo + per):
            step(per * i + c, c, i)
        if chain:
            chain.leave(turns + 1)
    for t in range(hi, last):
        step(t, t, 0)


def within(t, n):
    return not isinstance(t, int) or 0 <= t < n


def wait(eng, sem, value):
    if not isinstance(value, int) or value > 0:
        eng.wait_ge(sem, value)


def if_more(eng, tiles, rest, sems):
    n = eng.value_load(tiles, min_val=0, max_val=T0)
    with eng.If(n > MAIN):
        rest()
    with eng.Else():
        for signal, value in sems:
            eng.sem_inc(signal, value)


def build(nc, x, adjb, gate, sw13, sw2, moe0, wgnn, wsaT, acol, wab, bab, bgcn, wg1, w1, w2, b1, b2, gamma, beta, out):
    ctx = ExitStack()
    with ctx:
        def sb(name, shape, dt=F32):
            return ctx.enter_context(nc.sbuf_tensor(name, shape, dt))

        def sem(name):
            return ctx.enter_context(nc.semaphore(name))

        def dram(name, shape, dt=F32):
            return nc.dram_tensor(name, shape, dt, kind="Internal").ap()

        xn_dram = [dram("xn0_dram", (N, D)), dram("xn1_dram", (N, D))]
        TT = [T0, T1]
        y_dram = [dram("y0_dram", (T0 * P, D)), dram("y1_dram", (PAIRS, D))]

        xs = sb("xs", [P, NT, D])
        rowsP = sb("rowsP", [P, NT, DA])
        rowsQ = sb("rowsQ", [P, NT, DA])
        xT = sb("xT", [P, DC, N])
        adj_buf = sb("adj_buf", [P, 2, N])
        inc_buf = sb("inc_buf", [P, 2, N])
        mask = sb("mask", [P, 2, N], BF16)
        negs = sb("negs", [P, N])
        slbc = sb("slbc", [P, N])
        w1_sb = sb("w1_sb", [P, E1, DC * H1])
        w2_sb = sb("w2_sb", [P, E1, DC * D])
        wm = sb("wm", [P, U, 3 * D])
        xg = sb("xg", [P, U, D])
        y_sb = sb("y_sb", [P, U, D])
        xn_t = sb("xn_t", [P, 2, D])
        xT_t = sb("xT_t", [P, 2, DC, P])
        g_t = sb("g_t", [P, 2, DC, P])
        th = sb("th", [P, 2, D])
        av = sb("av", [P, 2, D])
        w1_rows = w1_sb[:, :, :].rearrange("p e n -> p (e n)")
        adj4 = [adj_buf[:, 0, :], adj_buf[:, 1, :], w1_rows[:, 0:N], w1_rows[:, N:2 * N]]
        w1_t = wm[:, :, :].rearrange("p u n -> p (u n)")[:, 0:2 * DC * H1].rearrange("p (a n) -> p a n", a=2)
        gate_sb = sb("gate_sb", [P, DC, E0])
        sw13_sb = sb("sw13_sb", [P, DC, 2 * D])
        sw2_sb = sb("sw2_sb", [P, DC, D])
        wc_sb = sb("wc_sb", [P, DC, 2 * DA])
        wv_sb = sb("wv_sb", [P, DC, 2])
        wsaT_sb = sb("wsaT_sb", [P, DC, D])
        acol_sb = sb("acol_sb", [P, DC, 2])
        wab_sb = sb("wab_sb", [P, DC, 4])
        slw = sb("slw", [P, DC, P])
        bab_sb = sb("bab_sb", [P, 2])
        half_bab = sb("half_bab", [P, 2])
        bgcn_sb = sb("bgcn_sb", [P, D])
        wg1_sb = sb("wg1_sb", [P, DC, E1])
        b1_sb = sb("b1_sb", [P, E1, DC])
        b2_sb = negs[0:1, :].rearrange("p (e d) -> p e d", e=E1)
        gam_bc = inc_buf[:, 0, :].rearrange("p (e d) -> p e d", e=E1)
        bet_bc = inc_buf[:, 1, :].rearrange("p (e d) -> p e d", e=E1)
        sg = mask[:, :, :].rearrange("p a n -> p (a n)").bitcast(F32).rearrange("p (h n) -> p h n", h=4)[:, 0:2, :]
        sth = negs[:, 0:1024].rearrange("p (h n) -> p h n", h=2)
        sav = negs[:, 1024:2048].rearrange("p (h n) -> p h n", h=2)
        ident = sb("ident", [P, P])
        ones_f = sb("ones_f", [1, P])
        ones_b = sb("ones_b", [P, P], BF16)
        tri_b = sb("tri_b", [P, P], BF16)
        iota_e = sb("iota_e", [P, P])
        iota_h = sb("iota_h", [P, P], F16)
        token_h = sb("token_h", [P, NT], F16)
        sp_h = sb("sp_h", [P, TOPK, NT], F16)
        sq_h = sb("sq_h", [P, TOPK, NT], F16)
        token_no = sb("token_no", [P, NT])
        ones_e = sb("ones_e", [P, E0])
        tile_no = sb("tile_no", [P, 1])
        eps_sb = sb("eps_sb", [P, 1])
        st6 = sb("st6", [P, NT, 6])
        st6l = sb("st6l", [P, 2, 6])
        mvl = sb("mvl", [P, U, 2])
        rsl = sb("rsl", [P, 2])
        mv = sb("mv", [P, NT, 2])
        rstd = sb("rstd", [P, NT])
        nrm = sb("nrm", [P, 2, P])
        rden = sb("rden", [P, 2])
        srn = sb("srn", [P, NT])
        vab = sb("vab", [P, NT, 2])
        att = sb("att", [P, U, 4])
        spare = rowsQ[:, :, :].rearrange("p t d -> p (t d)")
        lg, sel, rt1 = (spare[:, k * NT * E0:(k + 1) * NT * E0].rearrange("p (t e) -> p t e", e=E0) for k in range(3))
        mx8 = sb("mx8", [P, NT, 8])
        ix8 = sb("ix8", [P, NT, 8], U32)
        ixf = sb("ixf", [P, NT, TOPK])
        onehot = slbc[:, :].rearrange("p (k t e) -> p k t e", k=TOPK, e=E0)
        spare_b = spare[:, 3 * NT * E0:NT * DA].bitcast(BF16)
        cnt = spare_b[:, 0:NT * E0].rearrange("p (t e) -> p t e", e=E0)
        pre = spare_b[:, NT * E0:(2 * NT + 1) * E0].rearrange("p (t e) -> p t e", e=E0)
        tot = sb("tot", [P, 4, E0])
        tot_n = sb("tot_n", [P, E0])
        toti = sb("toti", [P, E0], I32)
        slot = sb("slot", [P, TOPK, NT])
        slot_i = sb("slot_i", [P, TOPK, NT], I32)
        sp_i = sb("sp_i", [P, TOPK, NT], I32)
        sq_f = sb("sq_f", [P, TOPK, NT])
        back = sb("back", [P, TOPK, NT], I32)
        wts = sb("wts", [P, TOPK, NT])
        ws = sb("ws", [P, 4, NT])
        et_f = sb("et_f", [P, 1])
        et_i = sb("et_i", [P, 1], I32)
        et_junk = sb("et_junk", [P, E0])
        et_row = [sb("et_row0", [1, T0], I32), sb("et_row1", [1, T1], I32)]
        tiles_i = sb("tiles_i", [1, 1], I32)
        tab = [sb("tab0", [P, T0], I32), sb("tab1", [P, T1], I32)]
        idx_t = sb("idx_t", [P, V, 1], I32)
        tab_f = sb("tab_f", [P, T0])
        tab_n = sb("tab_n", [P, T1])
        pair_tab = sb("pair_tab", [P, T1], I32)
        pair_t = sb("pair_t", [P, V, 1], I32)
        onehot_p = [b[:, :, :].rearrange("p a n -> p (a n)").bitcast(F16)[:, 0:TOPK * N].rearrange("p (k t q) -> p k t q", k=TOPK, q=P)
                    for b in (inc_buf, adj_buf)]
        rows_flat = rowsP[:, :, :].rearrange("p t d -> p (t d)")
        onehot_q = [rows_flat.bitcast(F16)[:, 0:TOPK * NT * T].rearrange("p (k t q) -> p k t q", k=TOPK, q=T) for T in TT]
        backs = [b[:, u, :] for b in (xg, y_sb) for u in range(U)]
        xg1, y1_sb = (adj_buf[:, h, :].rearrange("p (v d) -> p v d", v=V) for h in range(2))
        back4 = [adj_buf[:, 0, :], adj_buf[:, 1, :], w1_rows[:, 0:N], w1_rows[:, N:2 * N]]

        bank = [ctx.enter_context(nc.psum_tensor(f"bank{i}", [P, 512], F32)) for i in range(6)]
        banks67 = ctx.enter_context(nc.psum_tensor("banks67", [P, 1024], F32))
        bank += [banks67[:, 0:512], banks67[:, 512:1024]]

        names = """idx1_ready totals_read fp16_ready ln0_done y_scaled y_stats_done zeros_ready zeros_stored const_in consts
            mask_ready count_done nrm_ready head_ready inc_ready prod_done x1_done vector_link pool_link stats_ready
            rstd_ready ln_ready tr_done xts_ready proj_done gnn_in lg_ready cnt_ready pos_done tiles_ready onehots_ready
            table_done tab_ready et_in shared_hidden_done shared_tanh_done shared_gated shared_down_done shared_added
            scores_exp_ready slw_ready slbc_done slbc_ready exponents_ready exp_ready e_ready pa_done pe_done
            gates_tanh_done sums_ready out_tanh_done x3_done out_done gamma_beta_b2_in w1_w2_in pool_passed waits_passed
            wcol_ready scores_ready proj_used""".split()
        s = {n: sem(n) for n in names}
        x_in = [sem(f"x_in{i}") for i in range(4)]
        adj4_in = [sem(f"adj4_in{i}") for i in range(4)]
        adj_in = [sem(f"adj_in{i}") for i in range(2)]
        xn_out = [sem(f"xn_out{i}") for i in range(2)]
        m = [{n: sem(f"{n}_{l}") for n in "idx_ready tr_done x_ready h_done th_ready g_ready y_done y_ready wt_ready var_ready sd_ready pair_ready".split()}
             for l in range(2)]
        xg_in = [sem(f"xg_in{i}") for i in range(U)]
        xg_more = [sem(f"xg_more{i}") for i in range(U)]
        wm_in = [sem(f"wm_in{i}") for i in range(U)]
        wm_more = [sem(f"wm_more{i}") for i in range(U)]
        y_more = [sem(f"y_more{i}") for i in range(U)]
        y_out = [sem(f"y_out{i}") for i in range(U)]
        back_in = [sem(f"back_in{i}") for i in range(2 * U)]
        back_used = sem("back_used")
        y1_out = [sem(f"y1_out{i}") for i in range(V)]
        xg1_in = [sem(f"xg1_in{i}") for i in range(V)]
        back4_in = [sem(f"back4_in{i}") for i in range(4)]

        block = ctx.enter_context(nc.Block())
        tiled = [a.rearrange("(t p) d -> t p d", p=P) for a in xn_dram]
        y_tiled = [a.rearrange("(t p) d -> t p d", p=P) for a in y_dram]
        CONSTS = 12

        @block.sync
        def _(sp):
            def load_adj(t, dst, signal):
                sp.dma_start(dst, adjb[bass.ds(t, 1), :, :].rearrange("a p n -> (a p) n")).then_inc(signal, 16)

            load_adj(0, adj4[0], adj4_in[0])
            for q in range(4):
                sp.dma_start(xs[:, 4 * q:4 * q + 4, :], x[4 * q * P:(4 * q + 4) * P, :].rearrange("(t p) d -> p t d", p=P)).then_inc(x_in[q], 16)
            for u in range(1, 4):
                load_adj(u, adj4[u], adj4_in[u])
            for dst, src in ((gate_sb[:, :, :], gate), (sw13_sb[:, :, :], sw13), (sw2_sb[:, :, :], sw2),
                             (wc_sb[:, :, 0:D], wgnn[:, :, 0:D]), (wc_sb[:, :, DA:DA + D], wgnn[:, :, D:2 * D]),
                             (wsaT_sb[:, :, :], wsaT), (acol_sb[:, :, :], acol), (wab_sb[:, :, :], wab),
                             (bab_sb[:, :], bab.partition_broadcast(P)), (bgcn_sb[:, :], bgcn.partition_broadcast(P)),
                             (wg1_sb[:, :, :], wg1), (b1_sb[:, :, :], b1),):
                sp.dma_start(dst, src).then_inc(s["const_in"], 16)
            sp.wait_ge(s["zeros_ready"], 1)
            with sp.Fori(MAIN // U, T0 // U) as i:
                sp.dma_start(y_dram[0].rearrange("(i u p) d -> i p u d", u=U, p=P)[bass.ds(i, 1), :, :, :].rearrange("a p u d -> (a p) u d"),
                             xg[:, :, :]).then_inc(s["zeros_stored"], 16)
            def store_row(layer, t, c):
                half = c % 2
                sp.wait_ge(s["ln_ready"], 2 * NT * layer + t + 1)
                sp.dma_start(tiled[layer][bass.ds(t, 1), :, :].rearrange("a p n -> (a p) n"), xn_t[:, half, :]).then_inc(xn_out[half], 16)

            def loads_and_rows(t, c, i):
                if within(t + 4, NT):
                    sp.wait_ge(s["inc_ready"], t + 1)
                    load_adj(t + 4, adj4[c % 4], adj4_in[c % 4])
                if within(t - 3, NT):
                    store_row(0, t - 3, c - 3)

            sweep(sp, loads_and_rows, 0, 4, NT - 4, NT + 3, 4)

            def routed(layer):
                sp.wait_ge(s["tiles_ready"], layer + 1)
                sp.dma_start(et_row[layer][0:1, :], et_i[0:TT[layer], 0:1]).then_inc(s["et_in"], 16)

            routed(0)
            sp.wait_ge(s["et_in"], 16)

            def load_w(t, u, loads):
                e = sp.value_load(et_row[0][0:1, bass.ds(t, 1)], min_val=0, max_val=E0 - 1)
                sp.dma_start(wm[:, u, :], moe0[bass.ds(e, 1), :, :].rearrange("a p n -> (a p) n")).then_inc(loads[u], 16)

            def store_y(layer, t, u, stores):
                sp.wait_ge(m[layer]["y_ready"], t + 1)
                sp.dma_start(y_tiled[layer][bass.ds(t, 1), :, :].rearrange("a p n -> (a p) n"), y_sb[:, u, :]).then_inc(stores[u], 16)

            def weights_and_results(first, n, loads, stores):
                for u in range(U):
                    if first:
                        sp.wait_ge(m[0]["y_done"], first - U + u + 1)
                    load_w(first + u, u, loads)
                with sp.Fori(0, n // U - 1) as i:
                    for u in range(U):
                        sp.wait_ge(m[0]["y_done"], first + U * i + u + 1)
                        load_w(first + U * i + u + U, u, loads)
                        store_y(0, first + U * i + u, u, stores)
                for u in range(U):
                    store_y(0, first + n - U + u, u, stores)

            weights_and_results(0, MAIN, wm_in, y_out)
            sp.wait_ge(s["tiles_ready"], 1)
            if_more(sp, tiles_i[0:1, 0:1], lambda: weights_and_results(MAIN, T0 - MAIN, wm_more, y_more),
                    [])
            sp.wait_ge(s["inc_ready"], NT)
            for half in range(2):
                load_adj(half, adj_buf[:, half, :], adj_in[half])
            def loads_and_rows1(t, c, i):
                if within(t + 2, NT):
                    sp.wait_ge(s["e_ready"], t + 1)
                    sp.wait_ge(s["pa_done"], t + 1)
                    load_adj(t + 2, adj_buf[:, c % 2, :], adj_in[c % 2])
                if within(t - 2, NT):
                    store_row(1, t - 2, c - 2)

            sweep(sp, loads_and_rows1, 0, 2, NT - 2, NT, 2)
            sp.wait_ge(s["pe_done"], NT)
            sp.dma_start(gam_bc, gamma.rearrange("e d -> (e d)").partition_broadcast(P).rearrange("p (e d) -> p e d", e=E1)).then_inc(s["gamma_beta_b2_in"], 16)
            sp.dma_start(bet_bc, beta.rearrange("e d -> (e d)").partition_broadcast(P).rearrange("p (e d) -> p e d", e=E1)).then_inc(s["gamma_beta_b2_in"], 16)
            sp.dma_start(b2_sb, b2.rearrange("(a e) d -> a e d", a=1)).then_inc(s["gamma_beta_b2_in"], 16)
            for t in range(NT - 2, NT):
                store_row(1, t, t)
            routed(1)
            for v in range(V):
                sp.wait_ge(y1_out[v], 16 * len(range(v, T1, V)))
            for q in range(4):
                for k in range(TOPK):
                    sp.dma_start(back4[q].rearrange("p (k t d) -> p k t d", k=TOPK, d=D)[:, k],
                                 y_dram[1].rearrange("(k q t p) d -> k q p t d", k=TOPK, q=4, p=P)[k, q]).then_inc(back4_in[q], 16)
            for q in range(4):
                sp.wait_ge(s["x3_done"], NT + 4 * q + 4)
                sp.dma_start(out.rearrange("(q t p) d -> q p t d", q=4, p=P)[q], xs[:, 4 * q:4 * q + 4, :]).then_inc(s["out_done"], 16)
            sp.wait_ge(s["out_done"], 16 * 4)

        @block.gpsimd
        def _(pool):
            own = Chain(pool, s["pool_link"])
            own.link(pool.memset(ident[:, :], 0.0))
            own.link(pool.memset(tri_b[:, :], 1.0))
            own.link(pool.affine_select(out=ident[:, :], in_=ident[:, :], compare_op=ALU.not_equal, fill=1.0, base=0,
                                        pattern=[[-1, P]], channel_multiplier=1))
            own.link(pool.affine_select(out=tri_b[:, :], in_=tri_b[:, :], compare_op=ALU.is_gt, fill=0.0, base=0,
                                        pattern=[[1, P]], channel_multiplier=-1))
            own.link(pool.memset(ones_b[:, :], 1.0))
            own.link(pool.memset(ones_e[:, :], 1.0))
            own.link(pool.memset(ones_f[:, :], 1.0))
            own.link(pool.iota(iota_e[:, :], pattern=[[1, P]], base=0, channel_multiplier=0, allow_small_or_imprecise_dtypes=True))
            own.link(pool.iota(tile_no[:, :], pattern=[[0, 1]], base=0, channel_multiplier=1, allow_small_or_imprecise_dtypes=True))
            own.link(pool.iota(token_no[:, :], pattern=[[P, NT]], base=1, channel_multiplier=1, allow_small_or_imprecise_dtypes=True))
            own.link(pool.memset(eps_sb[:, :], EPS))
            pool.sem_inc(s["consts"], 1)

            own.link(pool.tensor_copy(iota_h[:, :], iota_e[:, :]))
            pool.tensor_copy(token_h[:, :], token_no[:, :]).then_inc(s["fp16_ready"], 1)
            pool.memset(xg[:, :, :], 0.0).then_inc(s["zeros_ready"], 1)

            def add_adj(t, u):
                half = u % 2
                pool.wait_ge(s["head_ready"], t + 1)
                pool.tensor_tensor(inc_buf[:, half, :], inc_buf[:, half, :], adj4[u], ALU.add).then_inc(s["inc_ready"], 1)

            with pool.Fori(0, NT // 4) as i:
                for u in range(4):
                    add_adj(4 * i + u, u)

            def gather(layer, u, signals):
                pool.indirect_dma_start(out=(xg1 if layer else xg)[:, u, :], out_offset=None, in_=xn_dram[layer],
                                        in_offset=bass.IndirectOffsetOnAxis(ap=idx_t[:, u, 0:1], axis=0)).then_inc(signals[u], 16)

            def gather_rows(layer, t, u, reused, signals=xg_in):
                if reused:
                    pool.wait_ge(m[layer]["tr_done"], t - U + 1)
                pool.tensor_copy(idx_t[:, u, :], tab[layer][:, bass.ds(t, 1)]).then_inc(m[layer]["idx_ready"], 1)
                pool.wait_ge(m[layer]["idx_ready"], t + 1)
                pool.sem_inc(s["pool_passed"], 1)
                gather(layer, u, signals)

            def gather_tiles(layer):
                pool.wait_ge(s["tab_ready"], layer + 1)
                for half in range(2):
                    pool.wait_ge(xn_out[half], 16 * (NT // 2) * (layer + 1))
                for u in range(V if layer else U):
                    gather_rows(layer, u, u, False, xg1_in if layer else xg_in)
                if layer == 0:
                    with pool.Fori(1, MAIN // U) as i:
                        for u in range(U):
                            gather_rows(layer, U * i + u, u, True)

            def scatter_results(t, u):
                pool.wait_ge(m[1]["y_ready"], t + 1)
                pool.wait_ge(m[1]["pair_ready"], t + 1)
                pool.sem_inc(s["pool_passed"], 1)
                pool.indirect_dma_start(out=y_dram[1], out_offset=bass.IndirectOffsetOnAxis(ap=pair_t[:, u, 0:1], axis=0),
                                        in_=y1_sb[:, u, :], in_offset=None,
                                        bounds_check=PAIRS - 1, oob_is_err=False).then_inc(y1_out[u], 16)

            def gather_results():
                for u in range(U):
                    pool.wait_ge(y_out[u], 16 * (MAIN // U))
                n = 0
                for t in range(NT):
                    for k in range(TOPK):
                        if n >= 2 * U:
                            pool.wait_ge(back_used, n - 2 * U + 1)
                        pool.indirect_dma_start(out=backs[n % (2 * U)], out_offset=None, in_=y_dram[0],
                                                in_offset=bass.IndirectOffsetOnAxis(ap=back[:, k, t:t + 1], axis=0)).then_inc(back_in[n % (2 * U)], 16)
                        n += 1

            pool.wait_ge(s["zeros_stored"], 16 * (T0 - MAIN) // U)
            gather_tiles(0)

            def gather_more():
                with pool.Fori(MAIN // U, T0 // U) as i:
                    for u in range(U):
                        gather_rows(0, U * i + u, u, True, xg_more)
                for q in y_more:
                    pool.wait_ge(q, 16 * (T0 - MAIN) // U)

            pool.wait_ge(s["tiles_ready"], 1)
            pool.wait_ge(m[0]["tr_done"], MAIN)
            if_more(pool, tiles_i[0:1, 0:1], gather_more, [(m[0]["idx_ready"], T0 - MAIN), (s["pool_passed"], T0 - MAIN)])
            gather_results()
            gather_tiles(1)
            LAG = 8

            def expert_step1(t, c, i):
                if within(t, T1):
                    pool.wait_ge(s["idx1_ready"], t - V + 1)
                    pool.sem_inc(s["pool_passed"], 1)
                    gather(1, c % V, xg1_in)
                if within(t - LAG, T1):
                    scatter_results(t - LAG, (c - LAG) % V)

            sweep(pool, expert_step1, V, V, T1 // V * V, T1 + LAG, V)

        @block.scalar
        def _(act):
            act.wait_ge(s["consts"], 1)

            def sqrt_var(n):
                act.wait_ge(s["stats_ready"], n)
                act.activation(rstd[:, :], mv[:, :, 1], ACT.Sqrt, bias=eps_sb[:, 0:1]).then_inc(s["rstd_ready"], 1)

            def sqrt_count(t, half, reused):
                act.wait_ge(s["count_done"], t + 1)
                if reused:
                    wait(act, s["head_ready"], t - 1)
                act.activation(nrm[:, half, :], bank[half][:, 0:P], ACT.Sqrt).then_inc(s["nrm_ready"], 1)

            def sqrt_row(g, c):
                act.wait_ge(s["stats_ready"], g + 2)
                act.activation(rsl[:, c % 2:c % 2 + 1], mvl[:, c % 2, 1:2], ACT.Sqrt, bias=eps_sb[:, 0:1]).then_inc(s["rstd_ready"], 1)

            def copy_T(g, t, half, full):
                act.wait_ge(s["tr_done"], g + 2)
                wait(act, s["proj_done"], g)
                src = bank[4 + half][:, 0:D].rearrange("p (c n) -> p c n", c=DC)
                if full:
                    act.activation(xT[:, :, bass.ds(t * P, P)], src, ACT.Copy)
                act.activation(xT_t[:, half, :, :], src, ACT.Copy).then_inc(s["xts_ready"], 1)

            act.sem_inc(s["proj_done"], 1)

            def aggregation_step(t, c, i):
                if within(t + 1, NT):
                    sqrt_count(t + 1, (c + 1) % 2, c >= 1)
                if within(t - 2, NT):
                    sqrt_row(t - 2, c)
                if within(t - 4, NT):
                    copy_T(t - 4, t - 4, c % 2, True)

            sqrt_count(0, 0, False)
            sqrt_var(1)
            sweep(act, aggregation_step, 0, 6, NT - 2, NT + 4, 2)
            act.dma_start(w1_sb[:, :, :], w1.rearrange("e p n -> p e n")).then_inc(s["w1_w2_in"], 16)
            act.dma_start(w2_sb[:, :, :], w2.rearrange("e p n -> p e n")).then_inc(s["w1_w2_in"], 16)
            act.wait_ge(s["proj_done"], NT + 1)
            act.activation(lg[:, 0:NT // 2, :], bank[6][:, :].rearrange("p (t e) -> p t e", e=E0), ACT.Copy).then_inc(s["lg_ready"], 1)
            act.activation(lg[:, NT // 2:NT, :], bank[7][:, :].rearrange("p (t e) -> p t e", e=E0), ACT.Copy).then_inc(s["lg_ready"], 1)
            act.wait_ge(s["scores_ready"], 1)
            act.activation(ws[:, 0:2, :], mx8[:, :, 0:TOPK].rearrange("p t k -> p k t"), ACT.Exp, scale=-1.0).then_inc(s["scores_exp_ready"], 1)

            def shared_tanh(c):
                for h in range(2):
                    act.wait_ge(s["shared_hidden_done"], 2 * c + h + 1)
                    if c:
                        act.wait_ge(s["shared_gated"], 2 * (c - 1) + h + 1)
                    act.activation(sth[:, h, :], bank[2 * h][:, :], ACT.Tanh, scale=0.5).then_inc(s["shared_tanh_done"], 1)

            for c in range(3):
                shared_tanh(c)

            def copy_x(layer, t, half, reused):
                act.wait_ge(m[layer]["tr_done"], t + 1)
                if reused:
                    act.wait_ge(m[layer]["h_done"], t - 1)
                act.activation(xT_t[:, half, :, :], bank[half][:, 0:D].rearrange("p (c n) -> p c n", c=DC), ACT.Copy).then_inc(m[layer]["x_ready"], 1)

            def tanh_z(t, half, reused):
                act.wait_ge(m[0]["h_done"], t + 1)
                if reused:
                    wait(act, m[0]["g_ready"], t - 1)
                act.activation(th[:, half, 0:P], bank[2 + half][:, 0:P], ACT.Tanh, scale=0.5).then_inc(m[0]["th_ready"], 1)

            def functions(first, n):
                later = first > 0
                copy_x(0, first, 0, later)
                copy_x(0, first + 1, 1, later)
                tanh_z(first, 0, later)
                turns = (n - 2) // U
                with act.Fori(0, turns) as i:
                    for j in range(U):
                        copy_x(0, first + U * i + 2 + j, j % 2, True)
                        tanh_z(first + U * i + 1 + j, (1 + j) % 2, True)
                for t in range(first + U * turns + 1, first + n):
                    if t + 1 < first + n:
                        copy_x(0, t + 1, (t + 1) % 2, True)
                    tanh_z(t, t % 2, True)

            functions(0, MAIN)
            act.wait_ge(s["tiles_ready"], 1)
            act.wait_ge(m[0]["g_ready"], MAIN)
            if_more(act, tiles_i[0:1, 0:1], lambda: functions(MAIN, T0 - MAIN),
                    [(m[0]["x_ready"], T0 - MAIN), (m[0]["th_ready"], T0 - MAIN)])

            act.wait_ge(s["slw_ready"], 1)
            for c in range(DC):
                act.activation(wc_sb[:, c, D:DA], bank[6][:, 2 * c:2 * c + 2], ACT.Copy, scale=-1.0).then_inc(s["wcol_ready"], 1)
            shared_tanh(3)
            act.wait_ge(s["gnn_in"], 1)

            def keep_proj(t):
                half = t % 2
                act.wait_ge(s["proj_done"], 1 + NT + t + 1)
                act.activation(rowsP[:, t, 0:D], bank[half][:, 0:D], ACT.Copy)
                act.activation(srn[:, t:t + 1], bank[half][:, D + 1:D + 2], ACT.Copy)
                act.activation(rowsQ[:, t, :], bank[2 + half][:, 0:DA], ACT.Copy)
                for k in range(2):
                    last = act.activation(vab[:, t, k:k + 1], bank[2 + half][:, DA + k:DA + k + 1], ACT.Identity, scale=0.5, bias=half_bab[:, k:k + 1])
                last.then_inc(s["proj_used"], 1)

            for t in range(NT):
                act.wait_ge(s["stats_ready"], 1 + NT + t + 1)
                act.activation(rstd[:, t:t + 1], mv[:, t, 1:2], ACT.Sqrt, bias=eps_sb[:, 0:1]).then_inc(s["rstd_ready"], 1)
                if t:
                    copy_T(NT + t - 1, t - 1, (t - 1) % 2, True)
                if t >= 3:
                    keep_proj(t - 3)
            copy_T(2 * NT - 1, NT - 1, 1, True)
            for t in range(NT - 3, NT):
                keep_proj(t)
            for c in range(4):
                act.wait_ge(s["slbc_done"], c + 1)
                act.activation(slbc[:, c * 512:(c + 1) * 512], bank[6 + c % 2][:, :], ACT.Copy).then_inc(s["slbc_ready"], 1)

            def exp_e(t):
                act.wait_ge(s["exponents_ready"], t + 1)
                act.activation(negs[:, :], negs[:, :], ACT.Exp).then_inc(s["exp_ready"], 1)

            def gates(t, half):
                act.wait_ge(s["pa_done"], t + 1)
                wait(act, s["sums_ready"], t)
                for k in range(2):
                    act.activation(att[:, half, k:k + 1], bank[2 + half][:, D + k:D + k + 1], ACT.Tanh, scale=0.5,
                                   bias=vab[:, bass.ds(t, 1), k]).then_inc(s["gates_tanh_done"], 1)

            def tanh_o(t, half):
                act.wait_ge(s["sums_ready"], t + 1)
                wait(act, s["x3_done"], t)
                act.activation(th[:, half, :], av[:, half, :], ACT.Tanh, scale=0.5).then_inc(s["out_tanh_done"], 1)

            exp_e(0)
            exp_e(1)

            def attention_step(t, c, i):
                if within(t + 2, NT):
                    exp_e(t + 2)
                if within(t - 3, NT):
                    copy_T(2 * NT + t - 3, t - 3, (c + 1) % 2, False)
                if within(t, NT):
                    gates(t, c % 2)
                    tanh_o(t, c % 2)
                if within(t - 1, NT):
                    sqrt_row(2 * NT + t - 1, c - 1)

            sweep(act, attention_step, 0, 4, NT - 2, NT + 3, 2)
            act.wait_ge(s["proj_done"], 3 * NT + 1)
            act.activation(lg[:, :, 0:E1], bank[6][:, 0:NT * E1].rearrange("p (t e) -> p t e", e=E1), ACT.Copy).then_inc(s["lg_ready"], 1)
            act.wait_ge(s["scores_ready"], 2)
            act.activation(ws[:, 1, :], ws[:, 0, :], ACT.Exp).then_inc(s["scores_exp_ready"], 1)

            def copy_w1(t, half, reused):
                e = act.value_load(et_row[1][0:1, bass.ds(t, 1)], min_val=0, max_val=E1 - 1)
                if reused:
                    act.wait_ge(m[1]["h_done"], t - 1)
                act.activation(w1_t[:, half, :], w1_sb[:, bass.ds(e, 1), :].rearrange("p a n -> p (a n)"), ACT.Copy).then_inc(m[1]["wt_ready"], 1)

            def relu_h(t, half, reused):
                e = act.value_load(et_row[1][0:1, bass.ds(t, 1)], min_val=0, max_val=E1 - 1)
                act.wait_ge(m[1]["h_done"], t + 1)
                if reused:
                    wait(act, m[1]["y_done"], t - 1)
                for c in range(DC):
                    act.activation(g_t[:, half, c, :], bank[2 + half][:, c * P:(c + 1) * P], ACT.Relu,
                                   bias=b1_sb[:, bass.ds(e, 1), c]).then_inc(m[1]["g_ready"], 1)

            def sd_y(t, u):
                act.wait_ge(m[1]["var_ready"], t + 1)
                act.activation(att[:, u, 0:1], mvl[:, u, 1:2], ACT.Sqrt, bias=eps_sb[:, 0:1]).then_inc(m[1]["sd_ready"], 1)

            act.wait_ge(s["w1_w2_in"], 32)
            act.wait_ge(s["const_in"], 16 * CONSTS)
            act.wait_ge(s["et_in"], 32)
            copy_w1(0, 0, False)
            copy_x(1, 0, 0, False)

            def expert_step1(t, c, i):
                if within(t + 1, T1):
                    copy_w1(t + 1, (c + 1) % 2, c >= 1)
                    copy_x(1, t + 1, (c + 1) % 2, c >= 1)
                if within(t, T1):
                    relu_h(t, c % 2, True)
                if within(t - 3, T1):
                    sd_y(t - 3, (c - 3) % U)

            sweep(act, expert_step1, 0, 4, T1 // V * V - 4, T1 + 3, V)

        @block.vector
        def _(dve):
            own = Chain(dve, s["vector_link"])
            link = own.link
            dve.sem_inc(s["tr_done"], 1)
            dve.wait_ge(s["consts"], 1)

            def normalise(dst, t):
                return dve.tensor_scalar(dst, xs[:, t, :], mv[:, t, 0:1], rstd[:, t:t + 1], ALU.subtract, ALU.mult)

            def mask_adj(t, turn, u):
                dve.wait_ge(adj4_in[u], 16 * turn + 16)
                wait(dve, s["count_done"], t - 1)
                dve.tensor_scalar(mask[:, u % 2, :], adj4[u], 0.0, None, ALU.is_gt).then_inc(s["mask_ready"], 1)

            link(dve.memset(rowsP[:, :, D:DA], 1.0))
            mask_adj(0, 0, 0)
            for t in range(NT):
                if t % 4 == 0:
                    dve.wait_ge(x_in[t // 4], 16)
                last = dve.bn_stats(st6[:, t, :], xs[:, t, :])
            link(last)
            for t in range(NT):
                last = dve.bn_aggr(mv[:, t, :], st6[:, t, :])
            last.then_inc(s["stats_ready"], 1)

            def heads(t, u, reused):
                half = u % 2
                dve.wait_ge(s["nrm_ready"], t + 1)
                if reused:
                    wait(dve, s["prod_done"], t - 1)
                link(dve.tensor_scalar(nrm[:, half, :], nrm[:, half, :], 1e-12, None, ALU.max))
                link(dve.reciprocal(nrm[:, half, :], nrm[:, half, :]))
                dve.scalar_tensor_tensor(out=inc_buf[:, half, :].rearrange("p (t i) -> p t i", i=P),
                                         in0=adj4[u].rearrange("p (t i) -> p t i", i=P), scalar=0.0,
                                         in1=nrm[:, half, :].unsqueeze(1).to_broadcast([P, NT, P]),
                                         op0=ALU.is_gt, op1=ALU.mult).then_inc(s["head_ready"], 1)

            def passed():
                dve.sem_inc(s["waits_passed"], 1)

            def statistics(t, half):
                passed()
                link(dve.bn_stats(st6l[:, half, :], xs[:, bass.ds(t, 1), :].rearrange("p a d -> p (a d)")))
                passed()
                dve.bn_aggr(mvl[:, half, :], st6l[:, half, :]).then_inc(s["stats_ready"], 1)

            def normalise_row(g, layer, t, c):
                half = c % 2
                dve.wait_ge(s["rstd_ready"], g + 2)
                link(dve.reciprocal(rsl[:, half:half + 1], rsl[:, half:half + 1]))
                wait(dve, s["tr_done"], g)
                wait(dve, xn_out[half], 16 * (NT // 2) * layer + 8 * (t - half))
                dve.tensor_scalar(xn_t[:, half, :], xs[:, bass.ds(t, 1), :].rearrange("p a d -> p (a d)"), mvl[:, half, 0:1], rsl[:, half:half + 1],
                                  ALU.subtract, ALU.mult).then_inc(s["ln_ready"], 1)

            def finish_rows(t, half):
                dve.wait_ge(s["prod_done"], t + 1)
                link(dve.reciprocal(rden[:, half:half + 1], bank[2 + half][:, D:D + 1]))
                row = xs[:, bass.ds(t, 1), :].rearrange("p a d -> p (a d)")
                dve.scalar_tensor_tensor(out=row, in0=bank[2 + half][:, 0:D], scalar=rden[:, half:half + 1], in1=row,
                                         op0=ALU.mult, op1=ALU.add).then_inc(s["x1_done"], 1)
                dve.wait_ge(s["x1_done"], t + 1)
                statistics(t, half)

            heads(0, 0, False)
            mask_adj(1, 0, 1)
            dve.wait_ge(s["rstd_ready"], 1)
            link(dve.reciprocal(rstd[:, :], rstd[:, :]))
            for t in range(NT):
                last = normalise(rowsP[:, t, 0:D], t)
            last.then_inc(s["ln0_done"], 1)
            heads(1, 1, False)
            mask_adj(2, 0, 2)

            def aggregation_step(t, c, i):
                if within(t, NT):
                    heads(t, c % 4, True)
                if within(t + 1, NT):
                    mask_adj(t + 1, i + (c + 1) // 4, (c + 1) % 4)
                if within(t - 2, NT):
                    finish_rows(t - 2, c % 2)
                if within(t - 3, NT):
                    normalise_row(t - 3, 0, t - 3, c - 3)

            sweep(dve, aggregation_step, 2, 6, NT - 2, NT + 3, 4, own, 20)

            def choose(layer):
                E, T = (E0, T0) if layer == 0 else (E1, T1)
                logit = lg[:, :, 0:E]
                oh = onehot[:, :, :, 0:E]
                dve.wait_ge(s["lg_ready"], 3 if layer else 2)
                for t in range(NT):
                    last = dve.max(mx8[:, t, :], logit[:, t, :])
                link(last)
                if layer:
                    link(dve.tensor_tensor(ws[:, 0, :], mx8[:, :, 1], mx8[:, :, 0], ALU.subtract))
                dve.sem_inc(s["scores_ready"], 1)
                for t in range(NT):
                    last = dve.max_index(ix8[:, t, :], mx8[:, t, :], logit[:, t, :])
                link(last)
                link(dve.tensor_copy(ixf[:, :, :], ix8[:, :, 0:TOPK]))
                for k in range(TOPK):
                    last = dve.tensor_tensor(oh[:, k], iota_e[:, 0:E].unsqueeze(1).to_broadcast([P, NT, E]),
                                             ixf[:, :, k:k + 1].to_broadcast([P, NT, E]), ALU.is_equal)
                link(last)
                link(dve.memset(pre[:, 0, 0:E], 0.0))
                link(dve.tensor_tensor(cnt[:, :, 0:E], oh[:, 0], oh[:, 1], ALU.add))
                for t in range(NT):
                    link(dve.tensor_tensor(pre[:, t + 1, 0:E], pre[:, t, 0:E], cnt[:, t, 0:E], ALU.add))
                dve.sem_inc(s["cnt_ready"], 1)

            def weigh(layer):
                E = E1 if layer else E0
                dve.wait_ge(s["pos_done"], layer + 1)
                dve.tensor_copy(tot_n[:, 0:E], bank[5][:, 256:256 + E]).then_inc(s["totals_read"], 1)
                dve.wait_ge(s["scores_exp_ready"], layer + 1)
                if layer == 0:
                    link(dve.tensor_scalar(ws[:, 0:2, :], ws[:, 0:2, :], 1.0, None, ALU.add))
                    link(dve.reciprocal(ws[:, 0:2, :], ws[:, 0:2, :]))
                    link(dve.tensor_tensor(ws[:, 2, :], ws[:, 0, :], ws[:, 1, :], ALU.add))
                    link(dve.tensor_scalar(ws[:, 2, :], ws[:, 2, :], 1e-20, None, ALU.add))
                    link(dve.reciprocal(ws[:, 3, :], ws[:, 2, :]))
                    for k in range(TOPK):
                        last = dve.scalar_tensor_tensor(out=wts[:, k, :], in0=ws[:, k, :], scalar=ROUTE_SCALE, in1=ws[:, 3, :], op0=ALU.mult, op1=ALU.mult)
                    link(last)
                else:
                    link(dve.tensor_scalar(ws[:, 2, :], ws[:, 1, :], 1.0, None, ALU.add))
                    link(dve.reciprocal(wts[:, 0, :], ws[:, 2, :]))
                    link(dve.tensor_tensor(wts[:, 1, :], wts[:, 0, :], ws[:, 1, :], ALU.mult))

            def count_tiles(layer):
                E = E1 if layer else E0
                dve.wait_ge(s["totals_read"], layer + 1)
                tt = tot_n[:, 0:E]
                if layer == 0:
                    link(dve.tensor_scalar(tot[:, 0, 0:E], tt, float(CAP), float(P - 1), ALU.min, ALU.add))
                else:
                    link(dve.tensor_scalar(tot[:, 0, 0:E], tt, float(P - 1), None, ALU.add))
                link(dve.tensor_copy(toti[:, 0:E], tot[:, 0, 0:E]))
                link(dve.tensor_scalar(toti[:, 0:E], toti[:, 0:E], 7, None, ALU.arith_shift_right))
                link(dve.tensor_copy(tot[:, 1, 0:E], toti[:, 0:E]))
                link(dve.tensor_tensor_scan(tot[:, 2, 0:E], ones_e[:, 0:E], tot[:, 1, 0:E], 0.0, ALU.mult, ALU.add))
                link(dve.tensor_tensor(tot[:, 3, 0:E], tot[:, 2, 0:E], tot[:, 1, 0:E], ALU.subtract))
                link(dve.tensor_scalar(et_junk[:, 0:E], tot[:, 2, 0:E], tile_no[:, 0:1], None, ALU.is_le))
                link(dve.reduce_sum(et_f[:, :], et_junk[:, 0:E], X))
                link(dve.tensor_scalar(et_f[:, :], et_f[:, :], float(E - 1), None, ALU.min))
                if layer == 0:
                    link(dve.tensor_copy(tiles_i[0:1, :], tot[0:1, 2, E - 1:E]))
                dve.tensor_copy(et_i[:, :], et_f[:, :]).then_inc(s["tiles_ready"], 1)

            def place(layer):
                E = E1 if layer else E0
                oh = onehot[:, :, :, 0:E]
                if layer == 0:
                    for b in range(2):
                        pos = bank[6 + b][:, :].rearrange("p (t e) -> p t e", e=E)
                        h = slice(b * NT // 2, (b + 1) * NT // 2)
                        last = dve.tensor_scalar(rt1[:, h, :], pos, float(CAP), DROPPED, ALU.is_ge, ALU.mult)
                    link(last)
                    for b in range(2):
                        pos = bank[6 + b][:, :].rearrange("p (t e) -> p t e", e=E)
                        h = slice(b * NT // 2, (b + 1) * NT // 2)
                        last = dve.tensor_tensor(rt1[:, h, :], rt1[:, h, :], pos, ALU.add)
                    link(last)
                else:
                    link(dve.tensor_copy(rt1[:, :, 0:E], bank[7][:, 0:NT * E].rearrange("p (t e) -> p t e", e=E)))
                link(dve.scalar_tensor_tensor(out=rt1[:, :, 0:E], in0=tot[:, 3, 0:E].unsqueeze(1).to_broadcast([P, NT, E]), scalar=float(P),
                                              in1=rt1[:, :, 0:E], op0=ALU.mult, op1=ALU.add))
                for k in range(TOPK):
                    link(dve.tensor_tensor(sel[:, :, 0:E], oh[:, k], rt1[:, :, 0:E], ALU.mult))
                    link(dve.reduce_sum(slot[:, k, :], sel[:, :, 0:E], X))
                link(dve.tensor_copy(slot_i[:, :, :], slot[:, :, :]))
                link(dve.tensor_scalar(sp_i[:, :, :], slot_i[:, :, :], P - 1, None, ALU.bitwise_and))
                link(dve.tensor_copy(sp_h[:, :, :], sp_i[:, :, :]))
                link(dve.tensor_scalar(sp_i[:, :, :], slot_i[:, :, :], 7, None, ALU.arith_shift_right))
                link(dve.tensor_scalar(sp_i[:, :, :], sp_i[:, :, :], 2047, None, ALU.min))
                link(dve.tensor_copy(sq_h[:, :, :], sp_i[:, :, :]))

            def onehots(layer):
                T = TT[layer]
                dve.wait_ge(s["fp16_ready"], 1)
                for k in range(TOPK):
                    last = dve.tensor_tensor(onehot_q[layer][:, k], iota_h[:, 0:T].unsqueeze(1).to_broadcast([P, NT, T]),
                                             sq_h[:, k, :].unsqueeze(2).to_broadcast([P, NT, T]), ALU.is_equal)
                link(last)
                for k in range(TOPK):
                    dve.tensor_tensor(onehot_q[layer][:, k], onehot_q[layer][:, k], token_h[:, :].unsqueeze(2).to_broadcast([P, NT, T]), ALU.mult)
                    dve.tensor_tensor(onehot_p[layer][:, k], iota_h[:, :].unsqueeze(1).to_broadcast([P, NT, P]),
                                      sp_h[:, k, :].unsqueeze(2).to_broadcast([P, NT, P]), ALU.is_equal).then_inc(s["onehots_ready"], 1)
                if layer == 0:
                    link(dve.tensor_scalar(sq_f[:, :, :], slot[:, :, :], DROPPED, None, ALU.is_lt))
                    link(dve.tensor_tensor(slot[:, :, :], slot[:, :, :], sq_f[:, :, :], ALU.mult))
                    link(dve.tensor_tensor(wts[:, :, :], wts[:, :, :], sq_f[:, :, :], ALU.mult))
                    link(dve.tensor_copy(back[:, :, :], slot[:, :, :]))

            def keep_table(layer):
                dve.wait_ge(s["table_done"], layer + 1)
                T = TT[layer]
                link(dve.tensor_copy(tab_f[:, 0:T], bank[6][:, 0:T]))
                link(dve.scalar_tensor_tensor(out=tab_f[:, 0:T], in0=tab_f[:, 0:T], scalar=-1.0, in1=bank[6][:, T0:T0 + T], op0=ALU.add, op1=ALU.add))
                link(dve.tensor_copy(tab[layer][:, :], tab_f[:, 0:T]))
                link(dve.tensor_scalar(tab[layer][:, :], tab[layer][:, :], N - 1, None, ALU.bitwise_and))
                if layer:
                    link(dve.tensor_scalar(tab_n[:, :], tab_f[:, 0:T], 0.0, NOWHERE, ALU.is_lt, ALU.mult))
                    link(dve.tensor_tensor(tab_n[:, :], tab_n[:, :], tab_f[:, 0:T], ALU.add))
                    link(dve.tensor_scalar(tab_f[:, 0:T], bank[6][:, T0:T0 + T], 0.0, float(N), ALU.is_gt, ALU.mult))
                    link(dve.tensor_tensor(tab_n[:, :], tab_n[:, :], tab_f[:, 0:T], ALU.add))
                    link(dve.tensor_copy(pair_tab[:, :], tab_n[:, :]))
                else:
                    link(dve.memset(rowsP[:, :, D:DA], 1.0))
                dve.sem_inc(s["tab_ready"], 1)

            choose(0)

            def shared_gates(c):
                for h in range(2):
                    dve.wait_ge(s["shared_tanh_done"], 2 * c + h + 1)
                    link(dve.scalar_tensor_tensor(out=sav[:, h, :], in0=sth[:, h, :], scalar=1.0, in1=bank[2 * h][:, :], op0=ALU.add, op1=ALU.mult))
                    if c:
                        dve.wait_ge(s["shared_down_done"], 4 * c)
                    dve.scalar_tensor_tensor(out=sg[:, h, :], in0=bank[2 * h + 1][:, :], scalar=0.5, in1=sav[:, h, :],
                                             op0=ALU.mult, op1=ALU.mult).then_inc(s["shared_gated"], 1)

            def shared_add(t):
                dve.wait_ge(s["shared_down_done"], t + 1)
                dve.tensor_tensor(xs[:, t, :], bank[4 + t % 2][:, 0:D], xs[:, t, :], ALU.add).then_inc(s["shared_added"], 1)

            shared_gates(0)
            weigh(0)
            shared_add(0)
            shared_add(1)
            count_tiles(0)
            shared_add(2)
            shared_add(3)
            place(0)
            shared_gates(1)
            for t in range(4, 8):
                shared_add(t)
            onehots(0)
            keep_table(0)
            shared_gates(2)
            for t in range(8, 12):
                shared_add(t)

            def gate_h(t, half, reused):
                dve.wait_ge(m[0]["th_ready"], t + 1)
                link(dve.scalar_tensor_tensor(out=av[:, half, 0:P], in0=th[:, half, 0:P], scalar=1.0, in1=bank[2 + half][:, 0:P], op0=ALU.add, op1=ALU.mult))
                if reused:
                    wait(dve, m[0]["y_done"], t - 1)
                dve.scalar_tensor_tensor(out=g_t[:, half, 0, :], in0=bank[2 + half][:, P:2 * P], scalar=0.5, in1=av[:, half, 0:P],
                                         op0=ALU.mult, op1=ALU.mult).then_inc(m[0]["g_ready"], 1)

            def copy_y(stores, t, u, turn):
                dve.wait_ge(m[0]["y_done"], t + 1)
                wait(dve, stores[u], 16 * turn)
                dve.tensor_copy(y_sb[:, u, :], bank[4 + u % 2][:, 0:D]).then_inc(m[0]["y_ready"], 1)

            def gated(first, n):
                stores = y_more if first else y_out
                gate_h(first, 0, first > 0)
                gate_h(first + 1, 1, first > 0)
                copy_y(stores, first, 0, 0)
                gate_h(first + 2, 0, True)
                copy_y(stores, first + 1, 1, 0)
                turns = (n - 4) // U

                def four_tiles(i):
                    for j in range(U):
                        gate_h(first + U * i + 3 + j, (3 + j) % 2, True)
                        copy_y(stores, first + U * i + 2 + j, (2 + j) % U, i + (j >= 2))

                rolled(dve, turns, four_tiles, own, U)
                for t in range(first + U * turns + 3, first + n):
                    gate_h(t, t % 2, True)
                    copy_y(stores, t - 1, (t - 1) % U, (t - 1 - first) // U)
                copy_y(stores, first + n - 1, (n - 1) % U, (n - 1) // U)

            gated(0, MAIN)
            dve.wait_ge(s["tiles_ready"], 1)
            for q in y_out:
                dve.wait_ge(q, 16 * MAIN // U)
            if_more(dve, tiles_i[0:1, 0:1], lambda: gated(MAIN, T0 - MAIN),
                    [(m[0]["g_ready"], T0 - MAIN), (m[0]["y_ready"], T0 - MAIN), (s["vector_link"], T0 - MAIN)])

            shared_gates(3)
            dve.wait_ge(s["const_in"], 16 * CONSTS)
            dve.wait_ge(s["wcol_ready"], DC)
            link(dve.tensor_copy(slw[:, :, :], wc_sb[:, :, D:D + 1].to_broadcast([P, DC, P])))
            link(dve.tensor_copy(wc_sb[:, :, DA + D:2 * DA], wab_sb[:, :, 0:2]))
            link(dve.tensor_copy(wv_sb[:, :, :], wab_sb[:, :, 2:4]))
            link(dve.tensor_scalar(half_bab[:, :], bab_sb[:, :], 0.5, None, ALU.mult))
            dve.sem_inc(s["gnn_in"], 1)

            def combine(t):
                for k in range(TOPK):
                    n = TOPK * t + k
                    dve.wait_ge(back_in[n % (2 * U)], 16 * (n // (2 * U) + 1))
                    dve.scalar_tensor_tensor(out=xs[:, t, :], in0=backs[n % (2 * U)], scalar=wts[:, k, t:t + 1], in1=xs[:, t, :],
                                             op0=ALU.mult, op1=ALU.add).then_inc(back_used, 1)
                    dve.wait_ge(back_used, n + 1)

            def norm_t(t):
                dve.wait_ge(s["rstd_ready"], 1 + NT + t + 1)
                link(dve.reciprocal(rstd[:, t:t + 1], rstd[:, t:t + 1]))
                dve.wait_ge(s["tr_done"], NT + t)
                dve.wait_ge(xn_out[t % 2], 16 * (NT // 2))
                normalise(xn_t[:, t % 2, :], t).then_inc(s["ln_ready"], 1)

            for t in range(NT):
                if t == 2:
                    dve.wait_ge(s["shared_down_done"], NT)
                    for q in range(4):
                        row = xs[:, NT - 4 + q, :]
                        dve.tensor_tensor(row, bank[6 + q % 2][:, q // 2 * D:(q // 2 + 1) * D], row, ALU.add).then_inc(s["shared_added"], 1)
                    dve.wait_ge(s["shared_added"], NT)
                combine(t)
                link(dve.bn_stats(st6[:, t, :], xs[:, t, :]))
                dve.bn_aggr(mv[:, t, :], st6[:, t, :]).then_inc(s["stats_ready"], 1)
                if t >= 1:
                    norm_t(t - 1)
            norm_t(NT - 1)
            dve.wait_ge(s["proj_used"], NT)

            def exponents(t):
                v = lambda a: a.rearrange("p (t i) -> p t i", i=P)
                link(dve.tensor_tensor(v(negs[:, :]), slbc[:, bass.ds(t * P, P)].unsqueeze(1).to_broadcast([P, NT, P]),
                                       srn[:, :].unsqueeze(2).to_broadcast([P, NT, P]), ALU.add))
                dve.scalar_tensor_tensor(out=negs[:, :], in0=negs[:, :], scalar=0.01, in1=negs[:, :], op0=ALU.mult, op1=ALU.min).then_inc(s["exponents_ready"], 1)

            def attention(t, turn, half, reused):
                dve.wait_ge(s["exp_ready"], t + 1)
                dve.wait_ge(adj_in[half], 16 * turn + 16)
                if reused:
                    dve.wait_ge(s["pe_done"], t - 1)
                dve.scalar_tensor_tensor(out=inc_buf[:, half, :], in0=adj_buf[:, half, :], scalar=0.0, in1=negs[:, :],
                                         op0=ALU.not_equal, op1=ALU.mult).then_inc(s["e_ready"], 1)
                dve.wait_ge(s["e_ready"], t + 1)

            def finish_nodes(t, half):
                dve.wait_ge(s["pe_done"], t + 1)
                dve.wait_ge(s["gates_tanh_done"], 2 * t + 2)
                link(dve.tensor_scalar(att[:, half, 0:2], att[:, half, 0:2], 0.5, 0.5, ALU.mult, ALU.add))
                link(dve.tensor_scalar(att[:, half, 2:3], bank[half][:, D:D + 1], 1e-5, None, ALU.add))
                link(dve.reciprocal(att[:, half, 3:4], att[:, half, 2:3]))
                link(dve.tensor_tensor(att[:, half, 2:3], att[:, half, 3:4], att[:, half, 0:1], ALU.mult))
                link(dve.tensor_tensor(av[:, half, :], bank[2 + half][:, 0:D], bgcn_sb[:, :], ALU.add))
                link(dve.tensor_scalar(av[:, half, :], av[:, half, :], att[:, half, 1:2], None, ALU.mult))
                dve.scalar_tensor_tensor(out=av[:, half, :], in0=bank[half][:, 0:D], scalar=att[:, half, 2:3], in1=av[:, half, :],
                                         op0=ALU.mult, op1=ALU.add).then_inc(s["sums_ready"], 1)

            def add_nodes(t, half):
                dve.wait_ge(s["out_tanh_done"], t + 1)
                row = xs[:, bass.ds(t, 1), :].rearrange("p a d -> p (a d)")
                link(dve.scalar_tensor_tensor(out=row, in0=th[:, half, :], scalar=0.5, in1=row, op0=ALU.mult, op1=ALU.add))
                dve.tensor_scalar(row, row, 0.5, None, ALU.add).then_inc(s["x3_done"], 1)
                dve.wait_ge(s["x3_done"], t + 1)
                statistics(t, half)

            dve.wait_ge(s["slbc_ready"], 1)
            exponents(0)
            attention(0, 0, 0, False)
            exponents(1)
            attention(1, 0, 1, False)
            exponents(2)
            dve.wait_ge(s["slbc_ready"], 4)
            finish_nodes(0, 0)

            def attention_step(t, c, i):
                if within(t + 1, NT):
                    attention(t + 1, i + (c + 1) // 2, (c + 1) % 2, True)
                if within(t + 2, NT):
                    exponents(t + 2)
                if within(t - 1, NT):
                    add_nodes(t - 1, (c - 1) % 2)
                if within(t - 2, NT):
                    normalise_row(2 * NT + t - 2, 1, t - 2, c)
                if within(t, NT):
                    finish_nodes(t, c % 2)

            sweep(dve, attention_step, 1, 3, NT - 3, NT + 2, 2, own, 20)
            choose(1)
            weigh(1)
            count_tiles(1)
            place(1)
            onehots(1)
            keep_table(1)

            dve.wait_ge(s["et_in"], 32)
            dve.wait_ge(s["gamma_beta_b2_in"], 48)

            def expert_step1(t, c, i):
                u, w, v = c % U, (c - 2) % U, (c - 2) % V
                if within(t - 2, T1):
                    e = dve.value_load(et_row[1][0:1, bass.ds(t - 2, 1)], min_val=0, max_val=E1 - 1)
                    dve.wait_ge(m[1]["sd_ready"], t - 1)
                    dve.reciprocal(att[:, w, 1:2], att[:, w, 0:1]).then_inc(s["y_scaled"], 1)
                    wait(dve, y1_out[v], 16 * (i + (c - 2) // V))
                    dve.scalar_tensor_tensor(out=y1_sb[:, v, :], in0=bank[4 + w][:, 0:D], scalar=mvl[:, w, 0:1], op0=ALU.subtract, op1=ALU.mult,
                                             in1=gam_bc[:, bass.ds(e, 1), :].rearrange("p a d -> p (a d)")).then_inc(s["y_scaled"], 1)
                    dve.tensor_copy(pair_t[:, v, :], pair_tab[:, bass.ds(t - 2, 1)]).then_inc(m[1]["pair_ready"], 1)
                if within(t, T1):
                    dve.wait_ge(m[1]["y_done"], t + 1)
                    passed()
                    dve.bn_stats(st6l[:, c % 2, :], bank[4 + u][:, 0:D]).then_inc(s["y_stats_done"], 1)
                if within(t - 2, T1):
                    dve.wait_ge(s["y_scaled"], 2 * t - 2)
                    dve.scalar_tensor_tensor(out=y1_sb[:, v, :], in0=y1_sb[:, v, :], scalar=att[:, w, 1:2], op0=ALU.mult, op1=ALU.add,
                                             in1=bet_bc[:, bass.ds(e, 1), :].rearrange("p a d -> p (a d)")).then_inc(m[1]["y_ready"], 1)
                if within(t, T1):
                    dve.wait_ge(s["y_stats_done"], t + 1)
                    passed()
                    dve.bn_aggr(mvl[:, u, :], st6l[:, c % 2, :]).then_inc(m[1]["var_ready"], 1)
                if within(t + V, T1) and within(t, T1):
                    dve.tensor_copy(idx_t[:, c % V, :], tab[1][:, bass.ds(t + V, 1)]).then_inc(s["idx1_ready"], 1)

            sweep(dve, expert_step1, 0, V + 2, V + 2 + (T1 - 2 * V - 2) // V * V, T1 + 2, V)
            for q in range(4):
                dve.wait_ge(back4_in[q], 16 * TOPK)
                rows = back4[q].rearrange("p (k t d) -> p k t d", k=TOPK, d=D)
                for k in range(TOPK):
                    for j in range(4):
                        t = 4 * q + j
                        last = dve.scalar_tensor_tensor(out=xs[:, t, :], in0=rows[:, k, j, :], scalar=wts[:, k, t:t + 1], in1=xs[:, t, :],
                                                        op0=ALU.mult, op1=ALU.add)
                        if k:
                            last.then_inc(s["x3_done"], 1)
                    if k == 0:
                        link(last)

        @block.tensor
        def _(pe):
            pe.wait_ge(s["consts"], 1)

            def count(t, half, reused):
                pe.wait_ge(s["mask_ready"], t + 1)
                if reused:
                    pe.wait_ge(s["nrm_ready"], t - 1)
                for j in range(NT):
                    last = pe.matmul(bank[half][:, 0:P], ones_b[:, :], mask[:, half, j * P:(j + 1) * P], start=(j == 0), stop=(j == NT - 1))
                last.then_inc(s["count_done"], 1)

            def product(ready, t, half, lhs, rhs, cols, dst, done):
                pe.wait_ge(ready, t + 1)
                for j in range(NT):
                    last = pe.matmul(dst[:, 0:cols], lhs[:, half, j * P:(j + 1) * P], rhs[:, j, 0:cols], start=(j == 0), stop=(j == NT - 1))
                last.then_inc(done, 1)

            def aggregate(t, half, reused):
                if reused:
                    wait(pe, s["x1_done"], t - 1)
                product(s["inc_ready"], t, half, inc_buf, rowsP, D + 1, bank[2 + half], s["prod_done"])

            count(0, 0, False)
            count(1, 1, False)
            pe.wait_ge(s["const_in"], 16 * CONSTS)
            pe.wait_ge(s["ln0_done"], 1)
            aggregate(0, 0, False)

            def transposes(g, half):
                pe.wait_ge(s["ln_ready"], g + 1)
                for c in range(DC):
                    last = pe.transpose(bank[4 + half][:, c * P:(c + 1) * P], xn_t[:, half, c * P:(c + 1) * P], ident[:, :])
                last.then_inc(s["tr_done"], 1)

            def logits(phase, t, half, w, dst):
                g = NT * phase + t
                pe.wait_ge(s["xts_ready"], g + 1)
                for c in range(DC):
                    last = pe.matmul(dst, xT_t[:, half, c, :], w[:, c, :], start=(c == 0), stop=(c == DC - 1))
                last.then_inc(s["proj_done"], 1)

            def aggregation_step(t, c, i):
                if within(t + 1, NT):
                    count(t + 1, (c + 1) % 2, c >= 1)
                if within(t, NT):
                    aggregate(t, c % 2, True)
                if within(t - 3, NT):
                    transposes(t - 3, (c - 3) % 2)
                if within(t - 4, NT):
                    logits(0, t - 4, c % 2, gate_sb, banks67[:, bass.ds((t - 4) * E0, E0)])

            sweep(pe, aggregation_step, 1, 5, NT - 1, NT + 4, 2)

            def positions(layer, E, banks, total):
                pe.wait_ge(s["cnt_ready"], layer + 1)
                per = NT // len(banks)
                for b, bk in enumerate(banks):
                    for j in range(per):
                        t = b * per + j
                        pe.matmul(bk[:, j * E:(j + 1) * E], tri_b[:, :], cnt[:, t, 0:E], start=True, stop=False)
                        pe.matmul(bk[:, j * E:(j + 1) * E], ones_b[:, :], pre[:, t, 0:E], start=False, stop=True)
                pe.matmul(total[:, 256:256 + E], ones_b[:, :], pre[:, NT, 0:E], start=True, stop=True).then_inc(s["pos_done"], 1)

            pe.wait_ge(s["lg_ready"], 2)
            def fill_table(layer):
                for n in range(TOPK * NT):
                    k, t = divmod(n, NT)
                    if t == 0:
                        pe.wait_ge(s["onehots_ready"], TOPK * layer + k + 1)
                    last = pe.matmul(bank[6][:, k * T0:k * T0 + TT[layer]], onehot_p[layer][:, k, t, :], onehot_q[layer][:, k, t, :],
                                     start=(t == 0), stop=(t == NT - 1))
                last.then_inc(s["table_done"], 1)

            def shared_hidden(c, h):
                if c:
                    pe.wait_ge(s["shared_gated"], 2 * (c - 1) + h + 1)
                for v in range(2):
                    for k in range(DC):
                        last = pe.matmul(bank[2 * h + v][:, :], sw13_sb[:, k, v * D + h * P:v * D + (h + 1) * P], xT[:, k, c * 512:(c + 1) * 512],
                                         start=(k == 0), stop=(k == DC - 1))
                last.then_inc(s["shared_hidden_done"], 1)

            def shared_down(j, dst):
                for k in range(DC):
                    last = pe.matmul(dst, sg[:, k, j * P:(j + 1) * P], sw2_sb[:, k, :], start=(k == 0), stop=(k == DC - 1))
                last.then_inc(s["shared_down_done"], 1)

            for h in range(2):
                shared_hidden(0, h)
            positions(0, E0, [bank[6], bank[7]], bank[5])
            for c in range(3):
                for h in range(2):
                    if c:
                        shared_hidden(c, h)
                if c == 2:
                    fill_table(0)
                pe.wait_ge(s["shared_gated"], 2 * c + 2)
                if c == 0:
                    pe.wait_ge(s["totals_read"], 1)
                for j in range(4):
                    t = 4 * c + j
                    if t >= 2:
                        pe.wait_ge(s["shared_added"], t - 1)
                    shared_down(j, bank[4 + j % 2][:, 0:D])
            pe.wait_ge(s["shared_added"], 12)

            def tr_x(layer, loads, rows, t, half, turn, reused):
                pe.wait_ge(loads, 16 * turn + 16)
                if reused:
                    wait(pe, m[layer]["x_ready"], t - 1)
                for c in range(DC):
                    last = pe.transpose(bank[half][:, c * P:(c + 1) * P], rows[:, c * P:(c + 1) * P], ident[:, :])
                last.then_inc(m[layer]["tr_done"], 1)

            def hidden0(loads, t, u, turn, reused):
                half = u % 2
                pe.wait_ge(m[0]["x_ready"], t + 1)
                pe.wait_ge(loads[u], 16 * turn + 16)
                if reused:
                    wait(pe, m[0]["g_ready"], t - 1)
                for v in range(2):
                    for k in range(DC):
                        last = pe.matmul(bank[2 + half][:, v * P:(v + 1) * P], wm[:, u, v * D + k * P:v * D + (k + 1) * P], xT_t[:, half, k, :],
                                         start=(k == 0), stop=(k == DC - 1))
                last.then_inc(m[0]["h_done"], 1)

            def down0(t, u):
                half = u % 2
                pe.wait_ge(m[0]["g_ready"], t + 1)
                if not isinstance(t, int) or t >= 2:
                    pe.wait_ge(m[0]["y_ready"], t - 1)
                pe.matmul(bank[4 + half][:, 0:D], g_t[:, half, 0, :], wm[:, u, 2 * D:3 * D], start=True, stop=True).then_inc(m[0]["y_done"], 1)

            def tr_x0(loads, t, u, turn, reused):
                tr_x(0, loads[u], xg[:, u, :], t, u % 2, turn, reused)

            def experts0(first, n):
                later, b = first > 0, first // U
                loads, weights = (xg_more, wm_more) if later else (xg_in, wm_in)
                tr_x0(loads, first, 0, 0, later)
                tr_x0(loads, first + 1, 1, 0, later)
                hidden0(weights, first, 0, 0, later)
                for j in (1, 2):
                    tr_x0(loads, first + j + 1, j + 1, 0, True)
                    hidden0(weights, first + j, j, 0, True)
                    down0(first + j - 1, j - 1)
                turns = (n - 4) // U
                with pe.Fori(0, turns) as i:
                    for j in range(U):
                        t, u = first + U * i + 3 + j, (3 + j) % U
                        tr_x0(loads, t + 1, (u + 1) % U, i + 1, True)
                        hidden0(weights, t, u, i + (j > 0), True)
                        down0(t - 1, (u - 1) % U)
                for t in range(first + U * turns + 3, first + n):
                    if t + 1 < first + n:
                        tr_x0(loads, t + 1, (t + 1) % U, (t + 1) // U - b, True)
                    hidden0(weights, t, t % U, t // U - b, True)
                    down0(t - 1, (t - 1) % U)
                down0(first + n - 1, (first + n - 1) % U)

            experts0(0, MAIN)
            pe.wait_ge(s["tiles_ready"], 1)
            pe.wait_ge(m[0]["y_ready"], MAIN)
            if_more(pe, tiles_i[0:1, 0:1], lambda: experts0(MAIN, T0 - MAIN),
                    [(m[0][q], T0 - MAIN) for q in ("tr_done", "h_done", "y_done")])

            for c in range(DC):
                for k in range(DC):
                    last = pe.matmul(bank[6][:, 2 * c:2 * c + 2], wsaT_sb[:, k, c * P:(c + 1) * P], acol_sb[:, k, :], start=(k == 0), stop=(k == DC - 1))
            last.then_inc(s["slw_ready"], 1)
            pe.wait_ge(m[0]["y_ready"], T0)
            for h in range(2):
                shared_hidden(3, h)
            pe.wait_ge(s["wcol_ready"], DC)
            pe.wait_ge(s["shared_gated"], 8)
            for j in range(4):
                shared_down(j, bank[6 + j % 2][:, j // 2 * D:(j // 2 + 1) * D])
            pe.wait_ge(s["gnn_in"], 1)

            def project(t):
                half = t % 2
                g = NT + t
                pe.wait_ge(s["xts_ready"], g + 1)
                if t >= 2:
                    pe.wait_ge(s["proj_used"], t - 1)
                for k in range(DC):
                    pe.matmul(bank[half][:, 0:DA], xT_t[:, half, k, :], wc_sb[:, k, 0:DA], start=(k == 0), stop=(k == DC - 1))
                for k in range(DC):
                    pe.matmul(bank[2 + half][:, 0:DA], xT_t[:, half, k, :], wc_sb[:, k, DA:2 * DA], start=(k == 0), stop=(k == DC - 1))
                for k in range(DC):
                    last = pe.matmul(bank[2 + half][:, DA:DA + 2], xT_t[:, half, k, :], wv_sb[:, k, :], start=(k == 0), stop=(k == DC - 1))
                last.then_inc(s["proj_done"], 1)

            for t in range(NT):
                transposes(NT + t, t % 2)
                if t >= 1:
                    project(t - 1)
            project(NT - 1)
            pe.wait_ge(s["shared_added"], NT)
            for c in range(4):
                if c >= 2:
                    pe.wait_ge(s["slbc_ready"], c - 1)
                for k in range(DC):
                    last = pe.matmul(bank[6 + c % 2][:, :], slw[:, k, :], xT[:, k, c * 512:(c + 1) * 512], start=(k == 0), stop=(k == DC - 1))
                last.then_inc(s["slbc_done"], 1)
            pe.wait_ge(s["proj_used"], NT)

            def attend(t, turn, half, reused):
                if reused:
                    pe.wait_ge(s["sums_ready"], t - 1)
                pe.wait_ge(adj_in[half], 16 * turn + 16)
                for j in range(NT):
                    last = pe.matmul(bank[2 + half][:, 0:DA], adj_buf[:, half, j * P:(j + 1) * P], rowsQ[:, j, :], start=(j == 0), stop=(j == NT - 1))
                last.then_inc(s["pa_done"], 1)
                product(s["e_ready"], t, half, inc_buf, rowsP, D + 1, bank[half], s["pe_done"])

            def attention_step(t, c, i):
                if within(t, NT):
                    attend(t, i + c // 2, c % 2, c >= 2)
                if within(t - 2, NT):
                    transposes(2 * NT + t - 2, c % 2)
                if within(t - 3, NT):
                    logits(2, t - 3, (c - 3) % 2, wg1_sb, bank[6][:, bass.ds((t - 3) * E1, E1)])

            sweep(pe, attention_step, 0, 4, NT, NT + 3, 2)
            positions(1, E1, [bank[7]], bank[5])
            fill_table(1)

            def hidden1(t, u, reused):
                half = u % 2
                pe.wait_ge(m[1]["x_ready"], t + 1)
                pe.wait_ge(m[1]["wt_ready"], t + 1)
                if reused:
                    wait(pe, m[1]["g_ready"], 2 * t - 2)
                for c in range(DC):
                    for k in range(DC):
                        last = pe.matmul(bank[2 + half][:, c * P:(c + 1) * P], w1_t[:, half, k * H1 + c * P:k * H1 + (c + 1) * P], xT_t[:, half, k, :],
                                         start=(k == 0), stop=(k == DC - 1))
                last.then_inc(m[1]["h_done"], 1)

            def down1(t, u):
                half = u % 2
                e = pe.value_load(et_row[1][0:1, bass.ds(t, 1)], min_val=0, max_val=E1 - 1)
                pe.wait_ge(m[1]["g_ready"], 2 * t + 2)
                if not isinstance(t, int) or t >= U:
                    wait(pe, m[1]["y_ready"], t - U + 1)
                for k in range(DC):
                    pe.matmul(bank[4 + u][:, 0:D], g_t[:, half, k, :], w2_sb[:, bass.ds(e, 1), k * D:(k + 1) * D].rearrange("p a d -> p (a d)"), start=(k == 0), stop=False)
                pe.matmul(bank[4 + u][:, 0:D], ones_f[0:1, :], b2_sb[0:1, bass.ds(e, 1), :].rearrange("p a d -> p (a d)"), start=False, stop=True).then_inc(m[1]["y_done"], 1)

            pe.wait_ge(s["w1_w2_in"], 32)
            pe.wait_ge(s["gamma_beta_b2_in"], 48)
            pe.wait_ge(s["et_in"], 32)
            def expert_step1(t, c, i):
                if within(t + 1, T1):
                    tr_x(1, xg1_in[(c + 1) % V], xg1[:, (c + 1) % V, :], t + 1, (c + 1) % 2, i + (c + 1) // V, c >= 1)
                if within(t, T1):
                    hidden1(t, c % U, c >= 2)
                if within(t - 1, T1):
                    down1(t - 1, (c - 1) % U)

            sweep(pe, expert_step1, -1, V - 1, T1 // V * V - 1, T1 + 1, V)


def kernel(x, adj, L0_ffn_gate_w, L0_ffn_w1, L0_ffn_w3, L0_ffn_w2, L0_ffn_sw1, L0_ffn_sw3, L0_ffn_sw2, L1_gnn_W_sa, L1_gnn_a_sa,
           L1_gnn_W_gcnb, L1_gnn_b_gcnb, L1_gnn_Wa, L1_gnn_ba, L1_gnn_Wb, L1_gnn_bb, L1_ffn_Wg, L1_ffn_W1, L1_ffn_b1, L1_ffn_W2,
           L1_ffn_b2, L1_ffn_gamma, L1_ffn_beta):
    import numpy as np
    import concourse.bacc as bacc
    from concourse.bass_utils import run_bass_kernel_spmd as run

    def chunked(w):
        w = np.asarray(w)
        return w.reshape(w.shape[0] // P, P, -1).transpose(1, 0, 2)

    def per_expert(w):
        w = np.asarray(w)
        e, k, n = w.shape
        return w.reshape(e, k // P, P, n).transpose(0, 2, 1, 3).reshape(e, P, k // P * n)

    wa, wb = np.asarray(L1_gnn_Wa), np.asarray(L1_gnn_Wb)
    columns = np.concatenate([wa[:, :D], wb[:, :D], wa[:, D:], wb[:, D:]], axis=0).T
    arrays = {
        "x": x,
        "adjb": np.asarray(adj).reshape(NT, P, NT, P).transpose(0, 3, 2, 1).reshape(NT, P, N),
        "gate": chunked(np.asarray(L0_ffn_gate_w).T),
        "sw13": np.concatenate([chunked(L0_ffn_sw1), chunked(L0_ffn_sw3)], axis=2),
        "sw2": chunked(L0_ffn_sw2),
        "moe0": np.concatenate([per_expert(L0_ffn_w1), per_expert(L0_ffn_w3), per_expert(L0_ffn_w2)], axis=2),
        "wgnn": np.concatenate([chunked(L1_gnn_W_sa), chunked(L1_gnn_W_gcnb)], axis=2),
        "wsaT": chunked(np.asarray(L1_gnn_W_sa).T),
        "acol": chunked(np.asarray(L1_gnn_a_sa).reshape(2, D).T),
        "wab": chunked(columns),
        "bab": np.concatenate([np.asarray(L1_gnn_ba), np.asarray(L1_gnn_bb)]),
        "bgcn": L1_gnn_b_gcnb,
        "wg1": chunked(L1_ffn_Wg),
        "w1": per_expert(L1_ffn_W1),
        "w2": per_expert(L1_ffn_W2),
        "b1": np.asarray(L1_ffn_b1).reshape(E1, DC, P).transpose(2, 0, 1),
        "b2": L1_ffn_b2,
        "gamma": L1_ffn_gamma,
        "beta": L1_ffn_beta,
    }
    arrays = {name: np.ascontiguousarray(a) for name, a in arrays.items()}
    nc = bacc.Bacc("TRN2", target_bir_lowering=False, num_devices=1)
    args = [nc.dram_tensor("in_" + name, a.shape, mybir.dt.from_np(a.dtype), kind="ExternalInput").ap() for name, a in arrays.items()]
    out = nc.dram_tensor("out_x", (N, D), F32, kind="ExternalOutput").ap()
    build(nc, *args, out)
    result = run(nc, [{"in_" + name: a for name, a in arrays.items()}], core_ids=[0])
    return result.results[0]["out_x"]
```
